# Optimizing a Trainium2 kernel written in Bass

```python
import numpy as np
import jax
import jax.numpy as jnp

def _softmax(x, axis=-1):
    return jax.nn.softmax(x, axis=axis)

def _gelu(x):
    return jax.nn.gelu(x, approximate=True)

def _silu(x):
    return jax.nn.silu(x)

def _sigmoid(x):
    return jax.nn.sigmoid(x)

def _layernorm(x, axis=-1, eps=1e-05):
    m = jnp.mean(x, axis=axis, keepdims=True)
    v = jnp.var(x, axis=axis, keepdims=True)
    return (x - m) / jnp.sqrt(v + eps)

def _scatter_add(tgt, idx, src, axis=0):
    return tgt.at[idx].add(src)

def _segment_sum(src, seg, n):
    return jax.ops.segment_sum(src, seg, n)
kernel_name = 'mk_gnn_ffn_d2_gnn_r8_a986a4'

def setup_inputs(seed: int=0):
    np.random.seed(seed)
    _w = jnp.asarray

    def _rec_inputs():
        import jax
        import jax.numpy as jnp
        _gk = jax.random.key(seed)
        x = -0.0002117 + 1 * jax.random.normal(jax.random.fold_in(_gk, 1), (6250, 256), jnp.float32)
        src = jax.random.randint(jax.random.fold_in(_gk, 2), (200000,), 0, 6250, jnp.int32)
        dst = jnp.minimum((6250 * jax.random.uniform(jax.random.fold_in(_gk, 3), (200000,)) ** 2.0).astype(jnp.int32), 49999)
        _o = jnp.argsort(dst, stable=True)
        src = src[_o]
        dst = dst[_o]
        edge_attr_16 = -0.000153872 + 1.00011 * jax.random.normal(jax.random.fold_in(_gk, 12), (200000, 16), jnp.float32)
        edge_attr_4 = 0.0007022 + 0.999661 * jax.random.normal(jax.random.fold_in(_gk, 13), (200000, 4), jnp.float32)
        edge_weight = jax.random.uniform(jax.random.fold_in(_gk, 15), (200000,), jnp.float32, 0.0, 0.999998)
        edge_weight_n2 = jax.random.uniform(jax.random.fold_in(_gk, 16), (200000,), jnp.float32, 0.0, 0.999998)
        return (x, src, dst, edge_attr_16, edge_attr_4, edge_weight, edge_weight_n2)
    x, src, dst, edge_attr_16, edge_attr_4, edge_weight, edge_weight_n2 = _rec_inputs()

    def _L0_gnn_setup():
        import jax, jax.numpy as jnp
        import numpy as np
        N_NODES = 12500
        N_EDGES = 100000
        DIM = 256
        EPS = 1e-05
        key = jax.random.key(seed)
        ks = jax.random.split(key, 12)
        H = DIM
        s = 1.0 / np.sqrt(H)
        s2 = 1.0 / np.sqrt(2 * H)
        return {'feat': jax.random.normal(ks[0], (N_NODES, DIM), dtype=jnp.float32), 'src': jax.random.randint(ks[1], (N_EDGES,), 0, N_NODES, dtype=jnp.int32), 'dst': jax.random.randint(ks[2], (N_EDGES,), 0, N_NODES, dtype=jnp.int32), 'iw': jax.random.uniform(ks[3], (N_EDGES,), dtype=jnp.float32), 'ow': jax.random.uniform(ks[4], (N_EDGES,), dtype=jnp.float32), 'gamma': jnp.ones((DIM,), jnp.float32), 'beta': jnp.zeros((DIM,), jnp.float32), 'W_in': jax.random.uniform(ks[5], (H, H), jnp.float32, -s, s), 'b_in': jax.random.uniform(ks[6], (H,), jnp.float32, -s, s), 'W_out': jax.random.uniform(ks[7], (H, H), jnp.float32, -s, s), 'b_out': jax.random.uniform(ks[8], (H,), jnp.float32, -s, s), 'W_x2i': jax.random.uniform(ks[9], (2 * H, 2 * H), jnp.float32, -s2, s2), 'b_x2i': jax.random.uniform(ks[10], (2 * H,), jnp.float32, -s2, s2), 'W_h2h': jax.random.uniform(ks[11], (H, 2 * H), jnp.float32, -s, s)}
    _L0_gnn_all = _L0_gnn_setup()
    _L0_gnn_in = {k: v for k, v in _L0_gnn_all.items() if k in ('gamma', 'beta', 'W_in', 'b_in', 'W_out', 'b_out', 'W_x2i', 'b_x2i', 'W_h2h')}
    del _L0_gnn_all

    def _L0_ffn_setup():
        import jax, jax.numpy as jnp
        import numpy as np
        NUM_EXPERTS = 8
        TOP_K = 2
        B, S, D = (8, 1024, 256)

        def _moe(tokens, router_w, w1, b1, w2, b2):
            N = tokens.shape[0]
            E = router_w.shape[0]
            logits = tokens.astype(jnp.float32) @ router_w.astype(jnp.float32).T
            probs = jax.nn.softmax(logits, axis=-1)
            rw, re = jax.lax.top_k(probs, TOP_K)
            if TOP_K > 1:
                rw = rw / jnp.maximum(rw.sum(-1, keepdims=True), 1e-12)
            rw = rw.astype(tokens.dtype)
            combine = jnp.zeros((N, E), tokens.dtype).at[jnp.arange(N)[:, None], re].set(rw)
            out = tokens
            for e in range(E):
                h = jax.nn.gelu(tokens @ w1[e] + b1[e], approximate=False)
                y = h @ w2[e] + b2[e]
                out = out + combine[:, e:e + 1] * y
            return out
        key = jax.random.key(seed)
        ks = jax.random.split(key, 4)
        scale = 1.0 / np.sqrt(D).astype(np.float32)
        return {'input_embeddings': jax.random.normal(ks[0], (B, S, D), jnp.float32), 'router_w': jax.random.normal(ks[1], (NUM_EXPERTS, D), jnp.float32) * scale, 'w1': jax.random.normal(ks[2], (NUM_EXPERTS, D, D), jnp.float32) * scale, 'b1': jnp.zeros((NUM_EXPERTS, D), jnp.float32), 'w2': jax.random.normal(ks[3], (NUM_EXPERTS, D, D), jnp.float32) * scale, 'b2': jnp.zeros((NUM_EXPERTS, D), jnp.float32)}
    _L0_ffn_all = _L0_ffn_setup()
    _L0_ffn_in = {k: v for k, v in _L0_ffn_all.items() if k in ('router_w', 'w1', 'b1', 'w2', 'b2')}
    del _L0_ffn_all

    def _L1_gnn_setup():
        import jax, jax.numpy as jnp
        import numpy as np
        N, E, C, R, HID = (6250, 62500, 64, 16, 64)
        key = jax.random.key(seed)
        ks = jax.random.split(key, 24)
        g = lambda k, shape, s=1.0: jax.random.normal(k, shape, dtype=jnp.float32) * s
        cs = C ** (-0.5)
        inp = {'h': g(ks[0], (N, 4 * C)), 'edge_index': jax.random.randint(ks[1], (2, E), 0, N), 'edge_sh': g(ks[2], (E, 4)), 'edge_rbf': g(ks[3], (E, R)), 'W_up0': g(ks[4], (C, C), cs), 'W_up1': g(ks[5], (C, C), cs), 'M1': g(ks[6], (R, HID), R ** (-0.5)), 'M2': g(ks[7], (HID, HID), HID ** (-0.5)), 'M3': g(ks[8], (HID, HID), HID ** (-0.5)), 'M4': g(ks[9], (HID, 4 * C), HID ** (-0.5)), 'W_lin0': g(ks[10], (C, C), cs), 'W_lin1': g(ks[11], (C, C), cs), 'Wsc0': g(ks[12], (C, C), cs), 'Wsc1': g(ks[13], (C, C), cs), 'Wc0': g(ks[14], (C, 5)), 'Wc1': g(ks[15], (C, 4)), 'WB0': g(ks[16], (C, C), cs), 'WB1': g(ks[17], (C, C), cs), 'gamma0': jnp.ones((C,), jnp.float32), 'beta0': jnp.zeros((C,), jnp.float32), 'gamma1': jnp.ones((C,), jnp.float32)}
        return inp
    _L1_gnn_all = _L1_gnn_setup()
    _L1_gnn_in = {k: v for k, v in _L1_gnn_all.items() if k in ('W_up0', 'W_up1', 'M1', 'M2', 'M3', 'M4', 'W_lin0', 'W_lin1', 'Wsc0', 'Wsc1', 'Wc0', 'Wc1', 'WB0', 'WB1', 'gamma0', 'beta0', 'gamma1')}
    del _L1_gnn_all

    def _L1_ffn_setup():
        import jax, jax.numpy as jnp
        import numpy as np
        B, S, D = (8, 512, 256)
        H = 4 * D
        CAPACITY = 0.5
        key = jax.random.key(seed)
        ks = jax.random.split(key, 6)
        x = jax.random.normal(ks[0], (B, S, D), dtype=jnp.float32)
        attention_mask = jnp.zeros((B, 1, 1, S), dtype=jnp.float32)
        wr = jax.random.normal(ks[1], (D, 1), dtype=jnp.float32) * 0.02
        br = jnp.zeros((1,), dtype=jnp.float32)
        w1 = jax.random.normal(ks[2], (D, H), dtype=jnp.float32) * 0.02
        b1 = jnp.zeros((H,), dtype=jnp.float32)
        w2 = jax.random.normal(ks[3], (H, D), dtype=jnp.float32) * 0.02
        b2 = jnp.zeros((D,), dtype=jnp.float32)
        return {'x': x, 'attention_mask': attention_mask, 'wr': wr, 'br': br, 'w1': w1, 'b1': b1, 'w2': w2, 'b2': b2}
    _L1_ffn_all = _L1_ffn_setup()
    _L1_ffn_in = {k: v for k, v in _L1_ffn_all.items() if k in ('attention_mask', 'wr', 'br', 'w1', 'b1', 'w2', 'b2')}
    del _L1_ffn_all
    return {'x': x, 'src': src, 'dst': dst, 'edge_attr_16': edge_attr_16, 'edge_attr_4': edge_attr_4, 'edge_weight': edge_weight, 'edge_weight_n2': edge_weight_n2, 'L0_gnn_gamma': _L0_gnn_in['gamma'], 'L0_gnn_beta': _L0_gnn_in['beta'], 'L0_gnn_W_in': _L0_gnn_in['W_in'], 'L0_gnn_b_in': _L0_gnn_in['b_in'], 'L0_gnn_W_out': _L0_gnn_in['W_out'], 'L0_gnn_b_out': _L0_gnn_in['b_out'], 'L0_gnn_W_x2i': _L0_gnn_in['W_x2i'], 'L0_gnn_b_x2i': _L0_gnn_in['b_x2i'], 'L0_gnn_W_h2h': _L0_gnn_in['W_h2h'], 'L0_ffn_router_w': _L0_ffn_in['router_w'], 'L0_ffn_w1': _L0_ffn_in['w1'], 'L0_ffn_b1': _L0_ffn_in['b1'], 'L0_ffn_w2': _L0_ffn_in['w2'], 'L0_ffn_b2': _L0_ffn_in['b2'], 'L1_gnn_W_up0': _L1_gnn_in['W_up0'], 'L1_gnn_W_up1': _L1_gnn_in['W_up1'], 'L1_gnn_M1': _L1_gnn_in['M1'], 'L1_gnn_M2': _L1_gnn_in['M2'], 'L1_gnn_M3': _L1_gnn_in['M3'], 'L1_gnn_M4': _L1_gnn_in['M4'], 'L1_gnn_W_lin0': _L1_gnn_in['W_lin0'], 'L1_gnn_W_lin1': _L1_gnn_in['W_lin1'], 'L1_gnn_Wsc0': _L1_gnn_in['Wsc0'], 'L1_gnn_Wsc1': _L1_gnn_in['Wsc1'], 'L1_gnn_Wc0': _L1_gnn_in['Wc0'], 'L1_gnn_Wc1': _L1_gnn_in['Wc1'], 'L1_gnn_WB0': _L1_gnn_in['WB0'], 'L1_gnn_WB1': _L1_gnn_in['WB1'], 'L1_gnn_gamma0': _L1_gnn_in['gamma0'], 'L1_gnn_beta0': _L1_gnn_in['beta0'], 'L1_gnn_gamma1': _L1_gnn_in['gamma1'], 'L1_ffn_attention_mask': _L1_ffn_in['attention_mask'], 'L1_ffn_wr': _L1_ffn_in['wr'], 'L1_ffn_br': _L1_ffn_in['br'], 'L1_ffn_w1': _L1_ffn_in['w1'], 'L1_ffn_b1': _L1_ffn_in['b1'], 'L1_ffn_w2': _L1_ffn_in['w2'], 'L1_ffn_b2': _L1_ffn_in['b2']}

def reference(x, src, dst, edge_attr_16, edge_attr_4, edge_weight, edge_weight_n2, L0_gnn_gamma, L0_gnn_beta, L0_gnn_W_in, L0_gnn_b_in, L0_gnn_W_out, L0_gnn_b_out, L0_gnn_W_x2i, L0_gnn_b_x2i, L0_gnn_W_h2h, L0_ffn_router_w, L0_ffn_w1, L0_ffn_b1, L0_ffn_w2, L0_ffn_b2, L1_gnn_W_up0, L1_gnn_W_up1, L1_gnn_M1, L1_gnn_M2, L1_gnn_M3, L1_gnn_M4, L1_gnn_W_lin0, L1_gnn_W_lin1, L1_gnn_Wsc0, L1_gnn_Wsc1, L1_gnn_Wc0, L1_gnn_Wc1, L1_gnn_WB0, L1_gnn_WB1, L1_gnn_gamma0, L1_gnn_beta0, L1_gnn_gamma1, L1_ffn_attention_mask, L1_ffn_wr, L1_ffn_br, L1_ffn_w1, L1_ffn_b1, L1_ffn_w2, L1_ffn_b2):
    import jax
    import jax.numpy as jnp

    def _L0_gnn_ref(feat, src, dst, iw, ow, gamma, beta, W_in, b_in, W_out, b_out, W_x2i, b_x2i, W_h2h):
        import jax, jax.numpy as jnp
        import numpy as np
        N_NODES = 12500
        N_EDGES = 100000
        DIM = 256
        EPS = 1e-05
        N = feat.shape[0]
        num_steps = 1
        mean = jnp.mean(feat, axis=0)
        var = jnp.var(feat, axis=0)
        h = (feat - mean) * jax.lax.rsqrt(var + EPS) * gamma + beta
        for _ in range(num_steps):
            feat_in = h @ W_in + b_in
            feat_out = h @ W_out + b_out
            a_in = jax.ops.segment_sum(feat_in[src] * iw[:, None], dst, num_segments=N)
            a_out = jax.ops.segment_sum(feat_out[dst] * ow[:, None], src, num_segments=N)
            a = jnp.concatenate((a_in, a_out), axis=1)
            xi = a @ W_x2i + b_x2i
            hh = h @ W_h2h
            i_i, i_n = jnp.split(xi, 2, axis=1)
            h_i, h_n = jnp.split(hh, 2, axis=1)
            input_gate = jax.nn.sigmoid(i_i + h_i)
            new_gate = jnp.tanh(i_n + h_n)
            h = new_gate + input_gate * (h - new_gate)
        return h

    def _L0_ffn_ref(input_embeddings, router_w, w1, b1, w2, b2):
        import jax, jax.numpy as jnp
        import numpy as np
        NUM_EXPERTS = 8
        TOP_K = 2
        B, S, D = (8, 1024, 256)

        def _moe(tokens, router_w, w1, b1, w2, b2):
            N = tokens.shape[0]
            E = router_w.shape[0]
            logits = tokens.astype(jnp.float32) @ router_w.astype(jnp.float32).T
            probs = jax.nn.softmax(logits, axis=-1)
            rw, re = jax.lax.top_k(probs, TOP_K)
            if TOP_K > 1:
                rw = rw / jnp.maximum(rw.sum(-1, keepdims=True), 1e-12)
            rw = rw.astype(tokens.dtype)
            combine = jnp.zeros((N, E), tokens.dtype).at[jnp.arange(N)[:, None], re].set(rw)
            out = tokens
            for e in range(E):
                h = jax.nn.gelu(tokens @ w1[e] + b1[e], approximate=False)
                y = h @ w2[e] + b2[e]
                out = out + combine[:, e:e + 1] * y
            return out
        b, s, d = input_embeddings.shape
        tokens = input_embeddings.reshape(b * s, d)
        return _moe(tokens, router_w, w1, b1, w2, b2).reshape(b, s, d)

    def _L1_gnn_ref(h, edge_index, edge_sh, edge_rbf, W_up0, W_up1, M1, M2, M3, M4, W_lin0, W_lin1, Wsc0, Wsc1, Wc0, Wc1, WB0, WB1, gamma0, beta0, gamma1):
        import jax, jax.numpy as jnp
        import numpy as np
        N, E, C, R, HID = (6250, 62500, 64, 16, 64)
        n = h.shape[0]
        h0 = h[:, :C]
        h1 = h[:, C:].reshape(n, C, 3)
        up0 = h0 @ W_up0
        up1 = jnp.einsum('ncx,cd->ndx', h1, W_up1)
        r = jax.nn.silu(edge_rbf @ M1)
        r = jax.nn.silu(r @ M2)
        r = jax.nn.silu(r @ M3)
        tpw = (r @ M4).reshape(-1, 4, C)
        snd, rcv = (edge_index[0], edge_index[1])
        x0 = up0[snd]
        x1 = up1[snd]
        sh0 = edge_sh[:, 0]
        sh1 = edge_sh[:, 1:]
        inv3 = 1.0 / jnp.sqrt(jnp.float32(3.0))
        m0e = tpw[:, 0] * x0 * sh0[:, None] + tpw[:, 3] * jnp.einsum('ecx,ex->ec', x1, sh1) * inv3
        m1e = tpw[:, 1][:, :, None] * x0[:, :, None] * sh1[:, None, :] + tpw[:, 2][:, :, None] * x1 * sh0[:, None, None]
        msg0 = jax.ops.segment_sum(m0e, rcv, num_segments=n)
        msg1 = jax.ops.segment_sum(m1e, rcv, num_segments=n)
        A0 = msg0 @ W_lin0
        A1 = jnp.einsum('ncx,cd->ndx', msg1, W_lin1)
        sc0 = h0 @ Wsc0
        sc1 = jnp.einsum('ncx,cd->ndx', h1, Wsc1)
        vv = jnp.sum(A1 * A1, -1)
        B0 = Wc0[:, 0] * A0 + Wc0[:, 1] * A0 * A0 + Wc0[:, 2] * vv + Wc0[:, 3] * A0 ** 3 + Wc0[:, 4] * A0 * vv
        B1 = (Wc1[:, 0] + Wc1[:, 1] * A0 + Wc1[:, 2] * A0 * A0 + Wc1[:, 3] * vv)[..., None] * A1
        o0 = B0 @ WB0 + sc0
        o1 = jnp.einsum('ncx,cd->ndx', B1, WB1) + sc1
        eps = jnp.float32(1e-05)
        mu = jnp.mean(o0, 0)
        xc = o0 - mu
        var = jnp.mean(xc * xc, 0)
        n0 = xc * jax.lax.rsqrt(var + eps) * gamma0 + beta0
        nrm1 = jnp.mean(jnp.sum(o1 * o1, -1) / 3.0, 0)
        n1 = o1 * (jax.lax.rsqrt(nrm1 + eps) * gamma1)[None, :, None]
        return jnp.concatenate([n0, n1.reshape(n, 3 * C)], -1)

    def _L1_ffn_ref(x, attention_mask, wr, br, w1, b1, w2, b2):
        import jax, jax.numpy as jnp
        import numpy as np
        B, S, D = (8, 512, 256)
        H = 4 * D
        CAPACITY = 0.5
        b, s, d = x.shape
        weights = (jnp.einsum('bsd,do->bso', x, wr) + br)[..., 0]
        k = max(1, int(CAPACITY * s))
        kk = k - 1 if k > 1 else 1
        _, idx = jax.lax.top_k(weights, k)
        sel_idx = idx[:, :kk]
        sel = jnp.take_along_axis(x, sel_idx[:, :, None], axis=1)
        h = jax.nn.gelu(jnp.einsum('bkd,dh->bkh', sel, w1) + b1)
        y = jnp.einsum('bkh,hd->bkd', h, w2) + b2
        w_sel = jnp.take_along_axis(weights, sel_idx, axis=1)
        y = y * w_sel[..., None]
        batch_idx = jnp.arange(b)[:, None]
        processed = jnp.zeros_like(x).at[batch_idx, sel_idx].set(y)
        return processed + x
    edge_index = jnp.stack([src, dst])
    x = x + _L0_gnn_ref(_layernorm(x, axis=-1), src, dst, edge_weight, edge_weight_n2, L0_gnn_gamma, L0_gnn_beta, L0_gnn_W_in, L0_gnn_b_in, L0_gnn_W_out, L0_gnn_b_out, L0_gnn_W_x2i, L0_gnn_b_x2i, L0_gnn_W_h2h)
    x = x + _L0_ffn_ref(_layernorm(x, axis=-1)[None], L0_ffn_router_w, L0_ffn_w1, L0_ffn_b1, L0_ffn_w2, L0_ffn_b2)[0]
    x = x + _L1_gnn_ref(_layernorm(x, axis=-1), edge_index, edge_attr_4, edge_attr_16, L1_gnn_W_up0, L1_gnn_W_up1, L1_gnn_M1, L1_gnn_M2, L1_gnn_M3, L1_gnn_M4, L1_gnn_W_lin0, L1_gnn_W_lin1, L1_gnn_Wsc0, L1_gnn_Wsc1, L1_gnn_Wc0, L1_gnn_Wc1, L1_gnn_WB0, L1_gnn_WB1, L1_gnn_gamma0, L1_gnn_beta0, L1_gnn_gamma1)
    x = x + _L1_ffn_ref(_layernorm(x, axis=-1)[None], L1_ffn_attention_mask, L1_ffn_wr, L1_ffn_br, L1_ffn_w1, L1_ffn_b1, L1_ffn_w2, L1_ffn_b2)[0]
    return x

_drawn_inputs = setup_inputs


def setup_inputs(seed=0):
    import zlib

    import numpy as np

    out = dict(_drawn_inputs(seed))
    spreads = {'L0_gnn_gamma': (1.0, 0.2),
     'L0_gnn_beta': (0.0, 0.1),
     'L0_ffn_b1': (0.0, 0.404),
     'L0_ffn_b2': (0.0, 0.271),
     'L1_gnn_gamma0': (1.0, 0.6),
     'L1_gnn_beta0': (0.0, 0.395),
     'L1_gnn_gamma1': (1.0, 0.554),
     'L1_ffn_b1': (0.0, 0.8),
     'L1_ffn_b2': (0.0, 0.8)}
    factors = {'L0_gnn_b_x2i': 4.235,
     'L1_gnn_Wsc0': 24.277,
     'L1_gnn_Wsc1': 8.0,
     'L1_ffn_wr': 6.625,
     'L1_ffn_w1': 7.383,
     'L1_ffn_w2': 6.893}
    for name, (base, spread) in spreads.items():
        noise = np.random.default_rng([zlib.crc32(name.encode()), seed]).standard_normal(out[name].shape)
        drawn = base * np.exp(spread * noise) if base else spread * noise
        out[name] = jnp.asarray(drawn.astype(out[name].dtype))
    for name, factor in factors.items():
        out[name] = (out[name] * factor).astype(out[name].dtype)
    return out
```

```python
import concourse.bass as bass
from concourse import mybir
from contextlib import ExitStack, contextmanager

F32 = mybir.dt.float32
I32 = mybir.dt.int32
ALU = mybir.AluOpType
ACT = mybir.ActivationFunctionType
AXX = mybir.AxisListType.X

NODES, DIM, EDGES = 6250, 256, 200000
P = 128
TILES = -(-NODES // P)
ROWS = TILES * P
TAIL = NODES - (TILES - 1) * P
BT = 7
BLOCKS = TILES // BT
TOK = BT * P
EP = 125
EC = EDGES // EP
HALF = 8
TURN = 2 * HALF
CHUNKS = -(-((EDGES - TILES) // P + TILES) // TURN) * TURN
TURNS = CHUNKS // TURN
META = 32
META2 = 4
C = 64
EPS = 1e-5
HID = 4 * DIM
MLP_IN = 16
EXPERTS = 8


class Chain:

    def __init__(self, eng, sem, start=0):
        self.eng, self.sem, self.start, self.n = eng, sem, start, 0

    def __call__(self, ins):
        ins.then_inc(self.sem, 1)
        self.n += 1
        self.eng.wait_ge(self.sem, self.start + self.n)
        return ins


def hold(eng):
    eng.nop(nofuse=True)


class Stage:

    def __init__(self, nc, ctx, tag):
        self.nc, self.ctx, self.tag = nc, ctx, tag

    def sb(self, name, shape, dt=F32):
        return self.ctx.enter_context(self.nc.sbuf_tensor(f"{self.tag}_{name}", shape, dt))

    def sem(self, name):
        return self.nc.alloc_semaphore(f"{self.tag}_{name}")

    def sems(self, name, n):
        return [self.sem(f"{name}{i}") for i in range(n)]

    def block(self):
        return self.ctx.enter_context(self.nc.Block())


@contextmanager
def stage(nc, tag):
    with nc.cleanup_on_exit():
        with ExitStack() as ctx:
            yield Stage(nc, ctx, tag)


def bc(ap, shape):
    return ap.to_broadcast(shape)


def tiles_of(dram):
    return dram.rearrange("(t p) d -> p t d", p=P)


def setup_stage(nc, K, x, xs, rows_dst, rows_src):
    with stage(nc, "set") as s:
        zero = s.sb("zero", [P, 3232])
        zeroed = s.sem("zeroed")
        written = s.sem("written")
        consts = s.sem("consts")
        block = s.block()

        @block.vector
        def _(dve):
            nc.vector.memset(zero[:, :], 0.0).then_inc(zeroed, 1)
            nc.vector.memset(K.eps[:, :], EPS)

        @block.sync
        def _(sp):
            sp.dma_start(xs[0:NODES, :], x[:, :]).then_inc(written, 16)
            sp.wait_ge(zeroed, 1)
            sp.dma_start(xs[NODES:ROWS, :], zero[0:ROWS - NODES, 0:DIM]).then_inc(written, 16)
            wide = CHUNKS * META // 16
            fills = 2
            dst_view = rows_dst.rearrange("(p r) w -> p (r w)", p=P)
            for n in range(16):
                sp.dma_start(dst_view[:, n * wide:(n + 1) * wide], zero[:, 0:wide]).then_inc(written, 16)
                fills += 1
            wide = CHUNKS * META2 // 2
            src_view = rows_src.rearrange("(p r) w -> p (r w)", p=P)
            for n in range(2):
                sp.dma_start(src_view[:, n * wide:(n + 1) * wide], zero[:, 0:wide]).then_inc(written, 16)
                fills += 1
            sp.wait_ge(written, 16 * fills)

        @block.gpsimd
        def _(pool):
            link = Chain(pool, consts)
            nc.gpsimd.memset(K.ones[:, :], 1.0)
            nc.gpsimd.memset(K.ident[:, :], 0.0)
            link(nc.gpsimd.memset(K.before[:, :], 1.0))
            nc.gpsimd.affine_select(out=K.ident[:, :], in_=K.ident[:, :], compare_op=ALU.not_equal, fill=1.0,
                                    base=0, pattern=[[-1, P]], channel_multiplier=1)
            nc.gpsimd.affine_select(out=K.upto[:, :], in_=K.before[:, :], compare_op=ALU.is_ge, fill=0.0,
                                    base=0, pattern=[[1, P]], channel_multiplier=-1)
            link(nc.gpsimd.iota(K.count_i[:, :], pattern=[[1, CHUNKS]], base=0, channel_multiplier=0))
            nc.gpsimd.affine_select(out=K.before[:, :], in_=K.before[:, :], compare_op=ALU.is_gt, fill=0.0,
                                    base=0, pattern=[[1, P]], channel_multiplier=-1)
            link(nc.gpsimd.tensor_copy(K.count[:, :], K.count_i[:, :]))


def norm_stage(nc, K, xs, gamma, beta, h_out):
    with stage(nc, "norm") as s:
        y = s.sb("y", [P, TILES, DIM])
        norm = RowNorm(nc, s, K)
        sq = s.sb("sq", [P, 2, DIM])
        mean = s.sb("mean", [P, DIM])
        gain = s.sb("gain", [P, DIM])
        gam = s.sb("gam", [P, DIM])
        bet = s.sb("bet", [P, DIM])
        loaded, sums, centred, squared, squares, used, h_ready, h_written, col_sd, dvec = (
            s.sem(n) for n in ("loaded", "sums", "centred", "squared", "squares", "used", "h_ready", "h_written",
                               "col_sd", "dvec"))
        block = s.block()

        @block.sync
        def _(sp):
            sp.dma_start(y[:, :, :], tiles_of(xs)).then_inc(loaded, 16)
            sp.dma_start(gam[:, :], gamma.rearrange("(a d) -> a d", a=1).broadcast_to([P, DIM])).then_inc(loaded, 16)
            sp.dma_start(bet[:, :], beta.rearrange("(a d) -> a d", a=1).broadcast_to([P, DIM])).then_inc(loaded, 16)
            sp.wait_ge(h_ready, 1)
            sp.dma_start(tiles_of(h_out), y[:, :, :]).then_inc(h_written, 16)
            sp.wait_ge(h_written, 16)

        @block.vector
        def _(dve):
            dve.wait_ge(loaded, 48)
            with dve.Fori(0, BLOCKS) as i:
                norm.on_vector(dve, i, lambda j: y[:, i * BT + j, :])
            link = Chain(dve, dvec)
            dve.wait_ge(sums, 1)
            link(nc.vector.tensor_scalar(mean[:, :], K.ps[0][:, 0:DIM], 1.0 / NODES, None, ALU.mult))
            nc.vector.tensor_tensor(y[:, :, :], y[:, :, :], bc(mean[:, :].unsqueeze(1), [P, TILES, DIM]),
                                    ALU.subtract).then_inc(centred, 1)
            dve.wait_ge(col_sd, 1)
            link(nc.vector.reciprocal(gain[:, :], gain[:, :]))
            link(nc.vector.tensor_tensor(gain[:, :], gain[:, :], gam[:, :], ALU.mult))
            link(nc.vector.tensor_tensor(y[:, :, :], y[:, :, :], bc(gain[:, :].unsqueeze(1), [P, TILES, DIM]), ALU.mult))
            nc.vector.tensor_tensor(y[:, :, :], y[:, :, :], bc(bet[:, :].unsqueeze(1), [P, TILES, DIM]),
                                    ALU.add).then_inc(h_ready, 1)

        @block.scalar
        def _(act):
            with act.Fori(0, BLOCKS) as i:
                norm.on_scalar(act, i)
            act.wait_ge(centred, 1)
            with act.Fori(0, (TILES - 1) // 2) as i:
                for k in range(2):
                    act.wait_ge(used, 2 * i + k + 1)
                    nc.scalar.activation(sq[:, k, :], y[:, 2 * i + k, :], ACT.Square).then_inc(squared, 1)
            act.wait_ge(used, TILES)
            nc.scalar.activation(sq[:, 0, :], y[:, TILES - 1, :], ACT.Square).then_inc(squared, 1)
            act.wait_ge(squares, 1)
            nc.scalar.activation(gain[:, :], K.ps[1][:, 0:DIM], ACT.Sqrt, bias=K.eps[:, :],
                                 scale=1.0 / NODES).then_inc(col_sd, 1)

        @block.tensor
        def _(pe):
            pe.wait_ge(norm.done, BLOCKS)
            nc.tensor.matmul(K.ps[0][:, 0:DIM], K.ones[:, :], y[:, 0, :], start=True, stop=False)
            with pe.Fori(1, TILES - 1) as t:
                nc.tensor.matmul(K.ps[0][:, 0:DIM], K.ones[:, :], y[:, t, :], start=False, stop=False)
            nc.tensor.matmul(K.ps[0][:, 0:DIM], K.ones[0:TAIL, :], y[0:TAIL, TILES - 1, :], start=False,
                             stop=True).then_inc(sums, 1)
            pe.sem_inc(used, 2)
            for t in range(2):
                pe.wait_ge(squared, t + 1)
                nc.tensor.matmul(K.ps[1][:, 0:DIM], K.ones[:, :], sq[:, t, :], start=(t == 0), stop=False).then_inc(used, 1)
            with pe.Fori(1, (TILES - 1) // 2) as i:
                for k in range(2):
                    pe.wait_ge(squared, 2 * i + k + 1)
                    nc.tensor.matmul(K.ps[1][:, 0:DIM], K.ones[:, :], sq[:, k, :], start=False, stop=False).then_inc(used, 1)
            pe.wait_ge(squared, TILES)
            nc.tensor.matmul(K.ps[1][:, 0:DIM], K.ones[0:TAIL, :], sq[0:TAIL, 0, :], start=False,
                             stop=True).then_inc(squares, 1)


class RowNorm:

    def __init__(self, nc, s, K):
        self.nc, self.K = nc, K
        self.stats = s.sb("ln_stats", [P, BT, 6])
        self.mv = s.sb("ln_mv", [P, BT, 2])
        self.sd = s.sb("ln_sd", [P, BT, 1])
        self.rstd = s.sb("ln_rstd", [P, BT, 1])
        self.stats_done = s.sem("ln_stats_done")
        self.mv_done = s.sem("ln_mv_done")
        self.sd_done = s.sem("ln_sd_done")
        self.rstd_done = s.sem("ln_rstd_done")
        self.done = s.sem("ln_done")

    def on_vector(self, dve, i, tile):
        nc = self.nc
        for j in range(BT):
            ins = nc.vector.bn_stats(self.stats[:, j, :], tile(j))
        ins.then_inc(self.stats_done, 1)
        dve.wait_ge(self.stats_done, i + 1)
        hold(dve)
        for j in range(BT):
            ins = nc.vector.bn_aggr(self.mv[:, j, :], self.stats[:, j, :])
        ins.then_inc(self.mv_done, 1)
        dve.wait_ge(self.sd_done, i + 1)
        nc.vector.reciprocal(self.rstd[:, :, :], self.sd[:, :, :]).then_inc(self.rstd_done, 1)
        dve.wait_ge(self.rstd_done, i + 1)
        hold(dve)
        for j in range(BT):
            ins = nc.vector.tensor_scalar(tile(j), tile(j), self.mv[:, j, 0:1], self.rstd[:, j, :],
                                          ALU.subtract, ALU.mult)
        ins.then_inc(self.done, 1)

    def on_scalar(self, act, i):
        act.wait_ge(self.mv_done, i + 1)
        self.nc.scalar.activation(self.sd[:, :, :], self.mv[:, :, 1:2], ACT.Sqrt,
                                  bias=self.K.eps[:, :]).then_inc(self.sd_done, 1)


def project_stage(nc, K, tag, h, weights, bias, outs):
    with stage(nc, tag) as s:
        w = s.sb("w", [P, 2, 2 * DIM])
        b = s.sb("b", [P, 2 * DIM])
        hb = s.sb("hb", [P, BT, DIM])
        hT = s.sb("hT", [P, 2 * BT, P])
        f = s.sb("f", [P, BT, 2 * DIM])
        w_loaded, h_loaded, transposed, hT_ready, product, f_ready, f_written = (
            s.sem(n) for n in ("w_loaded", "h_loaded", "transposed", "hT_ready", "product", "f_ready", "f_written"))
        block = s.block()
        n_w = 2 + (bias is not None)
        NT = 4

        @block.sync
        def _(sp):
            sp.dma_start(w[:, :, 0:DIM], weights[0].rearrange("(k p) n -> p k n", p=P)).then_inc(w_loaded, 16)
            sp.dma_start(w[:, :, DIM:], weights[1].rearrange("(k p) n -> p k n", p=P)).then_inc(w_loaded, 16)
            if bias is not None:
                for n, row in enumerate(bias):
                    sp.dma_start(b[:, n * DIM:(n + 1) * DIM],
                                 row.rearrange("(a d) -> a d", a=1).broadcast_to([P, DIM])).then_inc(w_loaded, 16)
            with sp.Fori(0, BLOCKS) as i:
                sp.wait_ge(transposed, i * NT + 1)
                sp.dma_start(hb[:, :, :], tiles_of(h)[:, bass.ds(i * BT, BT), :]).then_inc(h_loaded, 16)

        @block.tensor
        def _(pe):
            pe.wait_ge(w_loaded, 16 * (2 + (2 if bias is not None else 0)))
            pe.sem_inc(transposed, 1)
            with pe.Fori(0, BLOCKS) as i:
                pe.wait_ge(h_loaded, 16 * i + 16)
                for n in range(NT):
                    pe.wait_ge(hT_ready, i * NT + 1)
                    for m in range(4 * n, min(4 * n + 4, 2 * BT)):
                        ins = nc.tensor.transpose(K.ps[n][:, (m % 4) * P:(m % 4 + 1) * P],
                                                  hb[:, m // 2, (m % 2) * P:(m % 2 + 1) * P], K.ident[:, :])
                    ins.then_inc(transposed, 1)
                pe.wait_ge(hT_ready, i * NT + NT + 1)
                for j in range(BT):
                    pe.wait_ge(f_ready, i * BT + j + 1)
                    for k in range(2):
                        ins = nc.tensor.matmul(K.ps[4 + j % 2][:, :], hT[:, 2 * j + k, :], w[:, k, :],
                                               start=(k == 0), stop=(k == 1))
                    ins.then_inc(product, 1)

        @block.scalar
        def _(act):
            act.sem_inc(hT_ready, 1)
            with act.Fori(0, BLOCKS) as i:
                act.wait_ge(f_ready, i * BT + 2)
                hold(act)
                for n in range(NT):
                    act.wait_ge(transposed, i * NT + n + 2)
                    width = min(4, 2 * BT - 4 * n)
                    nc.scalar.activation(hT[:, 4 * n:4 * n + width, :],
                                         K.ps[n][:, 0:width * P].rearrange("p (m q) -> p m q", q=P),
                                         ACT.Copy).then_inc(hT_ready, 1)

        @block.vector
        def _(dve):
            if bias is not None:
                dve.wait_ge(w_loaded, 64)
            dve.sem_inc(f_ready, 2)

            def copy_out(i, first=False):
                if not first:
                    dve.wait_ge(f_written, 32 * i)
                    hold(dve)
                for j in range(BT):
                    dve.wait_ge(product, i * BT + j + 1)
                    if bias is None:
                        nc.vector.tensor_copy(f[:, j, :], K.ps[4 + j % 2][:, :]).then_inc(f_ready, 1)
                    else:
                        nc.vector.tensor_tensor(f[:, j, :], K.ps[4 + j % 2][:, :], b[:, :], ALU.add).then_inc(f_ready, 1)

            copy_out(0, first=True)
            with dve.Fori(1, BLOCKS) as i:
                copy_out(i)

        @block.gpsimd
        def _(pool):
            with pool.Fori(0, BLOCKS) as i:
                pool.wait_ge(f_ready, i * BT + BT + 2)
                hold(pool)
                for n in range(2):
                    pool.dma_start(tiles_of(outs[n])[:, bass.ds(i * BT, BT), :],
                                   f[:, :, n * DIM:(n + 1) * DIM]).then_inc(f_written, 16)
            pool.wait_ge(f_written, 32 * BLOCKS)


def sort_stage(nc, K, side, index, place_out, local_out):
    with stage(nc, f"sort_{side}") as s:
        key_i = s.sb("key_i", [EP, EC], I32)
        key = s.sb("key", [EP, EC])
        mask = s.sb("mask", [EP, EC])
        running = s.sb("running", [EP, EC])
        rank = s.sb("rank", [EP, EC])
        counts = s.sb("counts", [EP, TILES])
        first = s.sb("first", [EP, TILES])
        total = s.sb("total", [TILES, 1])
        padded = s.sb("padded", [TILES, 1])
        total_i = s.sb("total_i", [TILES, 1], I32)
        padded_wide = s.sb("padded_wide", [TILES, EP])
        ended = s.sb("ended", [TILES, CHUNKS])
        end_chunk = s.sb("end_chunk", [TILES, 1])
        bucket_f = s.sb("bucket_f", [1, CHUNKS])
        step, counted, totalled, padded_ready, placed, ends_ready, ended_ready, buckets_ready = (
            s.sem(n) for n in ("step", "counted", "totalled", "padded_ready", "placed", "ends_ready", "ended_ready",
                               "buckets_ready"))
        block = s.block()
        PART = CHUNKS // 4

        @block.vector
        def _(dve):
            link = Chain(dve, step)
            link(nc.vector.tensor_scalar(key_i[:, :], index[:, :], 7, None, ALU.arith_shift_right))
            link(nc.vector.tensor_copy(key[:, :], key_i[:, :]))
            link(nc.vector.tensor_scalar(key_i[:, :], index[:, :], P - 1, None, ALU.bitwise_and))
            link(nc.vector.tensor_copy(local_out[:, :], key_i[:, :]))
            link(nc.vector.memset(rank[:, :], 0.0))
            with dve.Fori(0, TILES) as b:
                dve.wait_ge(counted, b + 1)
                nc.vector.tensor_scalar(mask[:, :], key[:, :], K.count[0:EP, bass.ds(b, 1)], None, ALU.is_equal,
                                        ALU.add, accum_out=counts[:, bass.ds(b, 1)]).then_inc(counted, 1)
            dve.wait_ge(totalled, 1)
            link(nc.vector.tensor_scalar(total_i[:, :], K.ps[0][0:TILES, 0:1], float(P - 1), None, ALU.add))
            link(nc.vector.tensor_scalar(total_i[:, :], total_i[:, :], -P, None, ALU.bitwise_and))
            link(nc.vector.tensor_copy(padded[:, :], total_i[:, :]))
            nc.vector.tensor_scalar(padded_wide[:, :], K.ones[0:TILES, 0:EP], padded[:, :], None,
                                    ALU.mult).then_inc(padded_ready, 1)
            dve.wait_ge(placed, 2)
            link(nc.vector.tensor_copy(first[:, :], K.ps[1][0:EP, 0:TILES]))
            link(nc.vector.tensor_scalar(end_chunk[:, :], K.ps[2][0:TILES, 0:1], 1.0 / P, None, ALU.mult))
            nc.vector.tensor_scalar(ended[:, :], K.count[0:TILES, :], end_chunk[:, :], None,
                                    ALU.is_ge).then_inc(ended_ready, 1)
            base = link.n
            with dve.Fori(0, TILES) as b:
                turn = Chain(dve, step, base + b * 4)
                turn(nc.vector.tensor_scalar(mask[:, :], key[:, :], K.count[0:EP, bass.ds(b, 1)], None, ALU.is_equal))
                turn(nc.vector.tensor_tensor_scan(running[:, :], mask[:, :], mask[:, :], first[:, bass.ds(b, 1)],
                                                  ALU.add, ALU.max))
                turn(nc.vector.tensor_tensor(running[:, :], running[:, :], mask[:, :], ALU.mult))
                turn(nc.vector.tensor_tensor(rank[:, :], rank[:, :], running[:, :], ALU.add))
            link = Chain(dve, step, base + 4 * TILES)
            link(nc.vector.tensor_scalar(place_out[:, :], rank[:, :], -1.0, None, ALU.add))
            link(nc.vector.tensor_scalar(key_i[:, :], place_out[:, :], P - 1, 3, ALU.bitwise_and, ALU.logical_shift_left))
            r7 = mask[:, :].bitcast(I32)
            link(nc.vector.tensor_scalar(r7, place_out[:, :], 7, HALF - 1, ALU.arith_shift_right, ALU.bitwise_and))
            link(nc.vector.tensor_tensor(key_i[:, :], key_i[:, :], r7, ALU.bitwise_or))
            link(nc.vector.tensor_scalar(place_out[:, :], place_out[:, :], -P * HALF, None, ALU.bitwise_and))
            link(nc.vector.tensor_tensor(place_out[:, :], place_out[:, :], key_i[:, :], ALU.bitwise_or))
            dve.wait_ge(buckets_ready, 1)
            for n in range(4):
                ins = nc.vector.tensor_scalar(bucket_f[:, n * PART:(n + 1) * PART], K.ps[3 + n][0:1, 0:PART],
                                              float(TILES - 1), None, ALU.min)
            link(ins)
            link(nc.vector.tensor_copy(K.bucket[side][:, :], bucket_f[:, :]))

        @block.tensor
        def _(pe):
            pe.sem_inc(counted, 1)
            pe.wait_ge(counted, TILES + 1)
            nc.tensor.matmul(K.ps[0][0:TILES, 0:1], counts[:, :], K.ones[0:EP, 0:1], start=True,
                             stop=True).then_inc(totalled, 1)
            pe.wait_ge(padded_ready, 1)
            nc.tensor.matmul(K.ps[1][0:EP, 0:TILES], K.before[0:EP, 0:EP], counts[:, :], start=True, stop=False)
            nc.tensor.matmul(K.ps[1][0:EP, 0:TILES], padded_wide[:, :], K.before[0:TILES, 0:TILES], start=False,
                             stop=True).then_inc(placed, 1)
            nc.tensor.matmul(K.ps[2][0:TILES, 0:1], K.upto[0:TILES, 0:TILES], padded[:, :], start=True,
                             stop=True).then_inc(placed, 1)
            pe.wait_ge(ended_ready, 1)
            for n in range(4):
                ins = nc.tensor.matmul(K.ps[3 + n][0:1, 0:PART], K.ones[0:TILES, 0:1],
                                       ended[:, n * PART:(n + 1) * PART], start=True, stop=True)
            ins.then_inc(buckets_ready, 1)


def permute_stage(nc, K, edges, E, rows_dst, rows_src):
    TURNS_E = EC // TURN
    with stage(nc, "perm") as s:
        row = s.sb("row", [EP, 2, HALF, META])
        row2 = s.sb("row2", [EP, 2, HALF, META2])
        place = s.sb("place", [EP, 2, HALF], I32)
        place2 = s.sb("place2", [EP, 2, HALF], I32)
        loaded = s.sems("loaded", 2)
        filled = s.sem("filled")
        sent = s.sems("sent", 2)
        cleared = s.sem("cleared")
        block = s.block()
        edge_view = edges.rearrange("(p c) w -> p c w", p=EP)
        SENT = 16 * 2 * HALF

        @block.sync
        def _(sp):
            def load(i, first=False):
                for h in range(2):
                    if not first:
                        sp.wait_ge(sent[h], i * SENT)
                    sp.dma_start(row[:, h, :, :], edge_view[:, bass.ds(i * TURN + HALF * h, HALF), :]).then_inc(loaded[h], 16)

            load(0, first=True)
            with sp.Fori(1, TURNS_E) as i:
                load(i)

        @block.vector
        def _(dve):
            nc.vector.memset(row2[:, :, :, :], 0.0).then_inc(cleared, 1)
            dve.wait_ge(cleared, 1)

            def fill(i, first=False):
                for h in range(2):
                    if not first:
                        dve.wait_ge(sent[h], i * SENT)
                    dve.wait_ge(loaded[h], 16 * i + 16)
                    here = bass.ds(i * TURN + HALF * h, HALF)
                    nc.vector.tensor_copy(row[:, h, :, 0].bitcast(I32), E.src[:, here])
                    nc.vector.tensor_copy(row[:, h, :, 1], E.local_dst[:, here])
                    nc.vector.tensor_copy(place[:, h, :], E.place_dst[:, here])
                    nc.vector.tensor_copy(row2[:, h, :, 0].bitcast(I32), E.dst[:, here])
                    nc.vector.tensor_copy(row2[:, h, :, 1], E.local_src[:, here])
                    nc.vector.tensor_copy(row2[:, h, :, 2], E.weight_out[:, here])
                    nc.vector.tensor_copy(place2[:, h, :], E.place_src[:, here]).then_inc(filled, 1)

            fill(0, first=True)
            with dve.Fori(1, TURNS_E) as i:
                fill(i)

        @block.gpsimd
        def _(pool):
            with pool.Fori(0, TURNS_E) as i:
                for h in range(2):
                    pool.wait_ge(filled, 2 * i + h + 1)
                    hold(pool)
                    for c in range(HALF):
                        nc.gpsimd.indirect_dma_start(
                            out=rows_dst[:, :], out_offset=bass.IndirectOffsetOnAxis(ap=place[:, h, c:c + 1], axis=0),
                            in_=row[:, h, c, :], in_offset=None).then_inc(sent[h], 16)
                        nc.gpsimd.indirect_dma_start(
                            out=rows_src[:, :], out_offset=bass.IndirectOffsetOnAxis(ap=place2[:, h, c:c + 1], axis=0),
                            in_=row2[:, h, c, :], in_offset=None).then_inc(sent[h], 16)
            for h in range(2):
                pool.wait_ge(sent[h], TURNS_E * SENT)


class Edges:

    def __init__(self, nc, ctx):
        s = Stage(nc, ctx, "edges")
        self.src, self.dst, self.place_dst, self.place_src = (
            s.sb(n, [EP, EC], I32) for n in ("src", "dst", "place_dst", "place_src"))
        self.local_dst, self.local_src, self.weight_out = (
            s.sb(n, [EP, EC]) for n in ("local_dst", "local_src", "weight_out"))


def load_edges_stage(nc, E, src, dst, weight_out):
    with stage(nc, "edges") as s:
        loaded = s.sem("loaded")
        block = s.block()

        @block.sync
        def _(sp):
            for tile, array in ((E.src, src), (E.dst, dst), (E.weight_out, weight_out)):
                sp.dma_start(tile[:, :], array.rearrange("(p c) -> p c", p=EP)).then_inc(loaded, 16)
            sp.wait_ge(loaded, 48)


def gather_stage(nc, K, side, rows, words, table, out):
    with stage(nc, f"gather_{side}") as s:
        acc = s.sb("acc", [P, TILES, DIM])
        row = s.sb("row", [P, 2, HALF, words])
        got = s.sb("got", [P, TURN, DIM])
        pick = s.sb("pick", [P, TURN, P])
        loaded = s.sems("loaded", 2)
        gathered = s.sems("gathered", TURN)
        used = s.sems("used", 2)
        picked, added, cleared, written = (s.sem(n) for n in ("picked", "added", "cleared", "written"))
        block = s.block()
        view = rows.rearrange("(g p c) w -> g p c w", p=P, c=HALF)

        @block.sync
        def _(sp):
            with sp.Fori(0, TURNS) as i:
                for h in range(2):
                    sp.wait_ge(used[h], HALF * i + 1)
                    sp.dma_start(row[:, h, :, :], view[i * 2 + h, :, :, :]).then_inc(loaded[h], 16)
            sp.wait_ge(added, CHUNKS + 8)
            sp.dma_start(tiles_of(out), acc[:, :, :]).then_inc(written, 16)
            sp.wait_ge(written, 16)

        @block.gpsimd
        def _(pool):
            with pool.Fori(0, TURNS) as i:
                for h in range(2):
                    pool.wait_ge(used[h], HALF * i + 1)
                    hold(pool)
                    pool.wait_ge(loaded[h], 16 * i + 16)
                    hold(pool)
                    for c in range(HALF):
                        nc.gpsimd.indirect_dma_start(
                            out=got[:, HALF * h + c, :], out_offset=None, in_=table[:, :],
                            in_offset=bass.IndirectOffsetOnAxis(ap=row[:, h, c, 0:1].bitcast(I32), axis=0)
                        ).then_inc(gathered[HALF * h + c], 16)

        @block.vector
        def _(dve):
            nc.vector.memset(acc[:, :, :], 0.0).then_inc(cleared, 1)
            dve.wait_ge(cleared, 1)
            dve.sem_inc(added, 8)
            dve.sem_inc(used[0], 1)
            dve.sem_inc(used[1], 1)
            with dve.Fori(0, TURNS) as i:
                for h in range(2):
                    dve.wait_ge(used[h], HALF * i + 1)
                    dve.wait_ge(loaded[h], 16 * i + 16)
                    for c in range(HALF):
                        nc.vector.tensor_scalar(pick[:, HALF * h + c, :], K.count[:, 0:P], row[:, h, c, 1:2],
                                                row[:, h, c, 2:3], ALU.is_equal, ALU.mult).then_inc(picked, 1)
                    for c in range(HALF):
                        n = HALF * h + c
                        b = nc.vector.value_load(K.bucket[side][0:1, bass.ds(i * TURN + n, 1)], min_val=0,
                                                 max_val=TILES - 1)
                        dve.wait_ge(used[h], HALF * i + c + 2)
                        dve.wait_ge(added, i * TURN + n + 8)
                        nc.vector.tensor_tensor(acc[:, b, :], acc[:, b, :], K.ps[c][:, 0:DIM], ALU.add).then_inc(added, 1)

        @block.tensor
        def _(pe):
            with pe.Fori(0, TURNS) as i:
                for h in range(2):
                    for c in range(HALF):
                        n = HALF * h + c
                        pe.wait_ge(gathered[n], 16 * i + 16)
                        pe.wait_ge(picked, i * TURN + n + 1)
                        pe.wait_ge(added, i * TURN + n + 1)
                        nc.tensor.matmul(K.ps[c][:, 0:DIM], pick[:, n, :], got[:, n, :], start=True,
                                         stop=True).then_inc(used[h], 1)


def load_block(sp, views, tiles, i, loaded):
    for view, tile in zip(views, tiles):
        sp.dma_start(tile[:, :, :], tiles_of(view)[:, bass.ds(i * BT, BT), :]).then_inc(loaded, 16)


def row_bc(vec):
    return vec.rearrange("(a d) -> a d", a=1).broadcast_to([P, vec.shape[0]])


def update_stage(nc, K, x, h, a_in, a_out, w_x2i, b_x2i, w_h2h, x1_out, y1_out):
    with stage(nc, "upd") as s:
        KT = 6
        w = s.sb("w", [P, KT, 2 * DIM])
        b = s.sb("b", [P, 2 * DIM])
        srcs = [s.sb(n, [P, BT, DIM]) for n in ("a_in", "a_out", "h")]
        xb = s.sb("x", [P, BT, DIM])
        aT = s.sb("aT", [P, KT * BT, P])
        gate = s.sb("gate", [P, BT, 2 * DIM])
        y = s.sb("y", [P, BT, DIM])
        norm = RowNorm(nc, s, K)
        w_loaded, loaded, transposed, aT_ready, product, biased, gates, step, x1_ready, written = (
            s.sem(n) for n in ("w_loaded", "loaded", "transposed", "aT_ready", "product", "biased", "gates", "step",
                               "x1_ready", "written"))
        block = s.block()
        n_banks = -(-KT * BT // 4)

        @block.sync
        def _(sp):
            sp.dma_start(w[:, 0:4, :], w_x2i.rearrange("(k p) n -> p k n", p=P)).then_inc(w_loaded, 16)
            sp.dma_start(w[:, 4:6, :], w_h2h.rearrange("(k p) n -> p k n", p=P)).then_inc(w_loaded, 16)
            sp.dma_start(b[:, :], row_bc(b_x2i)).then_inc(w_loaded, 16)

            def turn(i, first=False):
                if not first:
                    sp.wait_ge(written, 32 * i)
                load_block(sp, (a_in, a_out, h, x), (*srcs, xb), i, loaded)
                sp.wait_ge(norm.done, i + 1)
                sp.dma_start(tiles_of(x1_out)[:, bass.ds(i * BT, BT), :], xb[:, :, :]).then_inc(written, 16)
                sp.dma_start(tiles_of(y1_out)[:, bass.ds(i * BT, BT), :], y[:, :, :]).then_inc(written, 16)

            turn(0, first=True)
            with sp.Fori(1, BLOCKS) as i:
                turn(i)
            sp.wait_ge(written, 32 * BLOCKS)

        @block.tensor
        def _(pe):
            pe.wait_ge(w_loaded, 48)
            with pe.Fori(0, BLOCKS) as i:
                pe.wait_ge(loaded, 64 * i + 64)
                for n in range(n_banks):
                    pe.wait_ge(aT_ready, i * n_banks + n + 1)
                    for m in range(4 * n, min(4 * n + 4, KT * BT)):
                        j, k = divmod(m, KT)
                        ins = nc.tensor.transpose(K.ps[n % 4][:, (m % 4) * P:(m % 4 + 1) * P],
                                                  srcs[k // 2][:, j, (k % 2) * P:(k % 2 + 1) * P], K.ident[:, :])
                    ins.then_inc(transposed, 1)
                pe.wait_ge(aT_ready, (i + 1) * n_banks + 4)
                for j in range(BT):
                    pe.wait_ge(biased, i * BT + j + 1)
                    for k in range(KT):
                        ins = nc.tensor.matmul(K.ps[4 + j % 2][:, :], aT[:, KT * j + k, :], w[:, k, :],
                                               start=(k == 0), stop=(k == KT - 1))
                    ins.then_inc(product, 1)

        @block.scalar
        def _(act):
            act.sem_inc(aT_ready, 4)
            with act.Fori(0, BLOCKS) as i:
                act.wait_ge(biased, i * BT + 2)
                hold(act)
                for n in range(n_banks):
                    act.wait_ge(transposed, i * n_banks + n + 1)
                    width = min(4, KT * BT - 4 * n)
                    nc.scalar.activation(aT[:, 4 * n:4 * n + width, :],
                                         K.ps[n % 4][:, 0:width * P].rearrange("p (m q) -> p m q", q=P),
                                         ACT.Copy).then_inc(aT_ready, 1)
                act.wait_ge(biased, (i + 1) * BT + 2)
                nc.scalar.activation(gate[:, :, 0:DIM], gate[:, :, 0:DIM], ACT.Sigmoid).then_inc(gates, 1)
                nc.scalar.activation(gate[:, :, DIM:], gate[:, :, DIM:], ACT.Tanh).then_inc(gates, 1)
                norm.on_scalar(act, i)

        @block.vector
        def _(dve):
            dve.wait_ge(w_loaded, 48)
            dve.sem_inc(biased, 2)

            def turn(i, first=False):
                for j in range(BT):
                    dve.wait_ge(product, i * BT + j + 1)
                    nc.vector.tensor_tensor(gate[:, j, :], K.ps[4 + j % 2][:, :], b[:, :], ALU.add).then_inc(biased, 1)
                link = Chain(dve, step, i * 5)
                if not first:
                    dve.wait_ge(written, 32 * i)
                dve.wait_ge(loaded, 64 * i + 64)
                dve.wait_ge(gates, 2 * i + 2)
                link(nc.vector.tensor_tensor(y[:, :, :], srcs[2][:, :, :], gate[:, :, DIM:], ALU.subtract))
                link(nc.vector.tensor_tensor(y[:, :, :], y[:, :, :], gate[:, :, 0:DIM], ALU.mult))
                link(nc.vector.tensor_tensor(y[:, :, :], y[:, :, :], gate[:, :, DIM:], ALU.add))
                link(nc.vector.tensor_tensor(xb[:, :, :], xb[:, :, :], y[:, :, :], ALU.add))
                link(nc.vector.tensor_copy(y[:, :, :], xb[:, :, :]))
                norm.on_vector(dve, i, lambda j: y[:, j, :])

            turn(0, first=True)
            with dve.Fori(1, BLOCKS) as i:
                turn(i)


def moe_stage(nc, K, y1, x1, router_T, w1, b1, w2, b2, x2_out, y2_out):
    E8 = EXPERTS
    NB = 4
    WIDE = TOK // 2
    with stage(nc, "moe") as s:
        w1s = s.sb("w1", [P, E8, 2, DIM])
        w2s = s.sb("w2", [P, E8, 2, DIM])
        b1s = s.sb("b1", [P, E8, 2])
        b2s = s.sb("b2", [E8, DIM])
        rT = s.sb("rT", [P, 2, E8])
        yb = s.sb("yb", [P, BT, DIM])
        xb = s.sb("xb", [P, BT, DIM])
        yT = s.sb("yT", [P, 2, TOK])
        hT = s.sb("hT", [P, 2, 2, TOK])
        acc = s.sb("acc", [P, BT, DIM])
        lg, pr, left, pick, comb = (s.sb(n, [P, BT, E8]) for n in ("lg", "pr", "left", "pick", "comb"))
        rev = s.sb("rev", [P, BT, E8])
        m1, m2, tot, idx = (s.sb(n, [P, BT, 1]) for n in ("m1", "m2", "tot", "idx"))
        combT = s.sb("combT", [E8, BT, P])
        norm = RowNorm(nc, s, K)
        (w_loaded, loaded, transposed, yT_ready, logits, shifted, expd, step, comb_ready, combT_done, combT_ready,
         hidden, hT_ready, expert, added, written) = (
            s.sem(n) for n in ("w_loaded", "loaded", "transposed", "yT_ready", "logits", "shifted", "expd", "step",
                               "comb_ready", "combT_done", "combT_ready", "hidden", "hT_ready", "expert", "added",
                               "written"))
        block = s.block()
        HPE = 4
        ADDS = BT * E8 + BT

        @block.sync
        def _(sp):
            sp.dma_start(w1s[:, :, :, :], w1.rearrange("e (k p) n -> p e k n", p=P)).then_inc(w_loaded, 16)
            sp.dma_start(w2s[:, :, :, :], w2.rearrange("e (k p) n -> p e k n", p=P)).then_inc(w_loaded, 16)
            with nc.allow_non_contiguous_dma("the first biases, once"):
                sp.dma_start(b1s[:, :, :], b1.rearrange("e (k p) -> p e k", p=P)).then_inc(w_loaded, 16)
            sp.dma_start(b2s[:, :], b2[:, :]).then_inc(w_loaded, 16)
            sp.dma_start(rT[:, :, :], router_T.rearrange("(k p) e -> p k e", p=P)).then_inc(w_loaded, 16)

            def turn(i, first=False):
                if not first:
                    sp.wait_ge(written, 32 * i)
                load_block(sp, (y1, x1), (yb, xb), i, loaded)
                sp.wait_ge(norm.done, i + 1)
                sp.dma_start(tiles_of(x2_out)[:, bass.ds(i * BT, BT), :], xb[:, :, :]).then_inc(written, 16)
                sp.dma_start(tiles_of(y2_out)[:, bass.ds(i * BT, BT), :], acc[:, :, :]).then_inc(written, 16)

            turn(0, first=True)
            with sp.Fori(1, BLOCKS) as i:
                turn(i)
            sp.wait_ge(written, 32 * BLOCKS)

        @block.tensor
        def _(pe):
            pe.wait_ge(w_loaded, 80)
            with pe.Fori(0, BLOCKS) as i:
                pe.wait_ge(loaded, 32 * i + 32)
                for n in range(NB):
                    pe.wait_ge(yT_ready, i * NB + n + 1)
                    for m in range(4 * n, min(4 * n + 4, 2 * BT)):
                        k, j = divmod(m, BT)
                        ins = nc.tensor.transpose(K.ps[n][:, (m % 4) * P:(m % 4 + 1) * P],
                                                  yb[:, j, k * P:(k + 1) * P], K.ident[:, :])
                    ins.then_inc(transposed, 1)
                pe.wait_ge(yT_ready, (i + 1) * NB + 4)
                pe.wait_ge(shifted, i + 1)
                for j in range(BT):
                    for k in range(2):
                        ins = nc.tensor.matmul(K.ps[4][:, j * E8:(j + 1) * E8], yT[:, k, j * P:(j + 1) * P],
                                               rT[:, k, :], start=(k == 0), stop=(k == 1))
                ins.then_inc(logits, 1)

                def hidden_of(e):
                    for m in range(2):
                        for q in range(2):
                            n = (2 * m + q)
                            pe.wait_ge(hT_ready, (i * E8 + e) * HPE + n + 1)
                            for k in range(2):
                                ins = nc.tensor.matmul(K.ps[n][:, 0:WIDE], w1s[:, e, k, m * P:(m + 1) * P],
                                                       yT[:, k, q * WIDE:(q + 1) * WIDE], start=(k == 0), stop=(k == 1))
                            ins.then_inc(hidden, 1)

                def output_of(e):
                    pe.wait_ge(hT_ready, (i * E8 + e + 1) * HPE + 4)
                    for j in range(BT):
                        n = e * BT + j
                        pe.wait_ge(added, i * ADDS + n + 1)
                        for k in range(2):
                            ins = nc.tensor.matmul(K.ps[5 + n % 3][:, 0:DIM], hT[:, e % 2, k, j * P:(j + 1) * P],
                                                   w2s[:, e, k, :], start=(k == 0), stop=(k == 1))
                        ins.then_inc(expert, 1)

                hidden_of(0)
                for e in range(E8):
                    if e + 1 < E8:
                        hidden_of(e + 1)
                    output_of(e)
                pe.wait_ge(comb_ready, i + 1)
                for j in range(BT):
                    ins = nc.tensor.transpose(K.ps[j // 4][0:E8, (j % 4) * P:(j % 4 + 1) * P],
                                              comb[:, j, :], K.ident[:, :])
                ins.then_inc(combT_done, 1)
                pe.wait_ge(combT_ready, i + 1)
                for j in range(BT):
                    n = E8 * BT + j
                    pe.wait_ge(added, i * ADDS + n + 1)
                    nc.tensor.matmul(K.ps[5 + n % 3][:, 0:DIM], combT[:, j, :], b2s[:, :], start=True,
                                     stop=True).then_inc(expert, 1)

        @block.scalar
        def _(act):
            act.sem_inc(yT_ready, 4)
            act.sem_inc(hT_ready, 4)
            with act.Fori(0, BLOCKS) as i:
                act.wait_ge(added, i * ADDS + 3)
                hold(act)
                for n in range(NB):
                    act.wait_ge(transposed, i * NB + n + 1)
                    width = min(4, 2 * BT - 4 * n)
                    nc.scalar.activation(yT[:, :, :].rearrange("p k t -> p (k t)")[:, 4 * n * P:(4 * n + width) * P],
                                         K.ps[n][:, 0:width * P], ACT.Copy).then_inc(yT_ready, 1)
                act.wait_ge(shifted, i + 2)
                nc.scalar.activation(pr[:, :, :], lg[:, :, :], ACT.Exp).then_inc(expd, 1)
                for e in range(E8):
                    if e >= 2:
                        act.wait_ge(expert, i * ADDS + (e - 1) * BT)
                        hold(act)
                    for m in range(2):
                        for q in range(2):
                            n = 2 * m + q
                            act.wait_ge(hidden, (i * E8 + e) * HPE + n + 1)
                            nc.scalar.activation(hT[:, e % 2, m, q * WIDE:(q + 1) * WIDE], K.ps[n][:, 0:WIDE], ACT.Gelu,
                                                 bias=b1s[:, e, m:m + 1]).then_inc(hT_ready, 1)
                act.wait_ge(combT_done, i + 1)
                nc.scalar.activation(combT[:, 0:4, :], K.ps[0][0:E8, :].rearrange("p (j t) -> p j t", t=P), ACT.Copy)
                nc.scalar.activation(combT[:, 4:BT, :], K.ps[1][0:E8, 0:(BT - 4) * P].rearrange("p (j t) -> p j t", t=P),
                                     ACT.Copy).then_inc(combT_ready, 1)
                norm.on_scalar(act, i)

        @block.vector
        def _(dve):
            dve.wait_ge(w_loaded, 80)
            dve.sem_inc(shifted, 1)
            dve.sem_inc(added, 3)
            nc.vector.tensor_scalar(rev[:, :, :], bc(K.count[:, 0:E8].unsqueeze(1), [P, BT, E8]), -1.0, float(E8),
                                    ALU.mult, ALU.add).then_inc(step, 1)
            dve.wait_ge(step, 1)

            def turn(i, first=False):
                link = Chain(dve, step, i * STEPS + 1)
                wide = lambda t: bc(t[:, :, :], [P, BT, E8])
                TT, TR = nc.vector.tensor_tensor, nc.vector.tensor_reduce
                dve.wait_ge(logits, i + 1)
                link(nc.vector.tensor_copy(lg[:, :, :], K.ps[4][:, 0:BT * E8].rearrange("p (j e) -> p j e", e=E8)))
                link(TR(m1[:, :, :], lg[:, :, :], AXX, ALU.max))
                TT(lg[:, :, :], lg[:, :, :], wide(m1), ALU.subtract).then_inc(shifted, 1)
                dve.wait_ge(expd, i + 1)
                link(TR(tot[:, :, :], pr[:, :, :], AXX, ALU.add))
                link(nc.vector.reciprocal(tot[:, :, :], tot[:, :, :]))
                link(TT(pr[:, :, :], pr[:, :, :], wide(tot), ALU.mult))

                def choose(source, best, mask_out):
                    link(TR(best[:, :, :], source[:, :, :], AXX, ALU.max))
                    link(TT(mask_out[:, :, :], source[:, :, :], wide(best), ALU.is_equal))
                    link(TT(mask_out[:, :, :], mask_out[:, :, :], rev[:, :, :], ALU.mult))
                    link(TR(idx[:, :, :], mask_out[:, :, :], AXX, ALU.max))
                    link(TT(mask_out[:, :, :], rev[:, :, :], wide(idx), ALU.is_equal))

                choose(pr, m1, comb)
                link(nc.vector.scalar_tensor_tensor(left[:, :, :], comb[:, :, :], -2.0, pr[:, :, :], ALU.mult, ALU.add))
                choose(left, m2, pick)
                link(TT(comb[:, :, :], comb[:, :, :], pick[:, :, :], ALU.add))
                link(TT(comb[:, :, :], comb[:, :, :], pr[:, :, :], ALU.mult))
                link(TT(tot[:, :, :], m1[:, :, :], m2[:, :, :], ALU.add))
                link(nc.vector.tensor_scalar(tot[:, :, :], tot[:, :, :], 1e-12, None, ALU.max))
                link(nc.vector.reciprocal(tot[:, :, :], tot[:, :, :]))
                TT(comb[:, :, :], comb[:, :, :], wide(tot), ALU.mult).then_inc(comb_ready, 1)
                dve.wait_ge(comb_ready, i + 1)
                if not first:
                    dve.wait_ge(written, 32 * i)
                dve.wait_ge(loaded, 32 * i + 32)
                for e in range(E8):
                    for j in range(BT):
                        n = e * BT + j
                        dve.wait_ge(expert, i * ADDS + n + 1)
                        if e:
                            dve.wait_ge(added, i * ADDS + n - BT + 4)
                        base = yb[:, j, :] if e == 0 else acc[:, j, :]
                        nc.vector.scalar_tensor_tensor(acc[:, j, :], K.ps[5 + n % 3][:, 0:DIM], comb[:, j, e:e + 1], base,
                                                       ALU.mult, ALU.add).then_inc(added, 1)
                for j in range(BT):
                    n = E8 * BT + j
                    dve.wait_ge(expert, i * ADDS + n + 1)
                    dve.wait_ge(added, i * ADDS + n - BT + 4)
                    TT(acc[:, j, :], acc[:, j, :], K.ps[5 + n % 3][:, 0:DIM], ALU.add).then_inc(added, 1)
                dve.wait_ge(added, (i + 1) * ADDS + 3)
                link(TT(xb[:, :, :], xb[:, :, :], acc[:, :, :], ALU.add))
                link(nc.vector.tensor_copy(acc[:, :, :], xb[:, :, :]))
                steps.append(link.n)
                norm.on_vector(dve, i, lambda j: acc[:, j, :])

            steps = []
            STEPS = 23
            turn(0, first=True)
            assert steps[0] == STEPS, steps
            with dve.Fori(1, BLOCKS) as i:
                turn(i)


def message_stage(nc, K, rows, table, m1, m2, m3, m4, out):
    with stage(nc, "msg") as s:
        acc = s.sb("acc", [P, TILES, DIM])
        row = s.sb("row", [P, 2, HALF, META])
        got = s.sb("got", [P, TURN, DIM])
        m1s = s.sb("m1", [P, HALF // 2, P])
        m2s, m3s = s.sb("m2", [P, P]), s.sb("m3", [P, P])
        m4s = s.sb("m4", [P, DIM])
        attr = s.sb("attr", [P, P])
        attrT = s.sb("attrT", [P, P])
        hid = s.sb("hid", [P, 3, 512])
        same = s.sb("same", [P, 2, P])
        pick = s.sb("pick", [P, 2, 4, P])
        prod = s.sb("prod", [P, 2, 2 * DIM])
        loaded = s.sems("loaded", 2)
        gathered = s.sems("gathered", TURN)
        used = s.sems("used", 2)
        (w_loaded, scaled, attr_ready, attr_turned, attrT_ready, layer, act_done, weights, prods, matched, picked,
         added, cleared, written) = (
            s.sem(n) for n in ("w_loaded", "scaled", "attr_ready", "attr_turned", "attrT_ready", "layer", "act_done",
                               "weights", "prods", "matched", "picked", "added", "cleared", "written"))
        block = s.block()
        view = rows.rearrange("(g p c) w -> g p c w", p=P, c=HALF)
        TURN_BANK, MLP_BANK, W_BANK, SUM_BANK = 0, 1, 3, 6

        @block.sync
        def _(sp):
            sp.dma_start(m1s[:, :, :], m1[:, :, :]).then_inc(w_loaded, 16)
            for tile, array in ((m2s, m2), (m3s, m3), (m4s, m4)):
                sp.dma_start(tile[:, :], array[:, :]).then_inc(w_loaded, 16)
            with sp.Fori(0, TURNS) as i:
                for h in range(2):
                    sp.wait_ge(used[h], HALF * i + 1)
                    sp.dma_start(row[:, h, :, :], view[i * 2 + h, :, :, :]).then_inc(loaded[h], 16)
            sp.wait_ge(added, CHUNKS + 2)
            sp.dma_start(tiles_of(out), acc[:, :, :]).then_inc(written, 16)
            sp.wait_ge(written, 16)

        @block.gpsimd
        def _(pool):
            with pool.Fori(0, TURNS) as i:
                for h in range(2):
                    pool.wait_ge(used[h], HALF * i + 1)
                    hold(pool)
                    pool.wait_ge(loaded[h], 16 * i + 16)
                    hold(pool)
                    for c in range(HALF):
                        nc.gpsimd.indirect_dma_start(
                            out=got[:, HALF * h + c, :], out_offset=None, in_=table[:, :],
                            in_offset=bass.IndirectOffsetOnAxis(ap=row[:, h, c, 0:1].bitcast(I32), axis=0)
                        ).then_inc(gathered[HALF * h + c], 16)

        @block.vector
        def _(dve):
            nc.vector.memset(acc[:, :, :], 0.0).then_inc(cleared, 1)
            dve.wait_ge(w_loaded, 64)
            nc.vector.tensor_scalar(m4s[:, 3 * C:], m4s[:, 3 * C:], float(3.0 ** -0.5), None, ALU.mult).then_inc(scaled, 1)
            dve.wait_ge(cleared, 1)
            dve.sem_inc(added, 2)
            dve.sem_inc(used[0], 1)
            dve.sem_inc(used[1], 1)
            dve.sem_inc(attr_turned, 1)
            dve.sem_inc(picked, 2)
            with dve.Fori(0, TURNS) as i:
                for h in range(2):
                    half = i * 2 + h
                    dve.wait_ge(attr_turned, half + 1)
                    dve.wait_ge(loaded[h], 16 * i + 16)
                    nc.vector.tensor_copy(attr[:, :].rearrange("p (c f) -> p c f", f=MLP_IN),
                                          row[:, h, :, 8:8 + MLP_IN]).then_inc(attr_ready, 1)

                    def multiply(c):
                        n = HALF * h + c
                        dve.wait_ge(picked, half * HALF + c + 1)
                        nc.vector.tensor_scalar(same[:, c % 2, :], K.count[:, 0:P], row[:, h, c, 1:2], None,
                                                ALU.is_equal).then_inc(matched, 1)
                        w = K.ps[W_BANK + c % 2][:, 0:DIM].rearrange("p (k d) -> p k d", d=C)
                        dve.wait_ge(weights, half * HALF + c + 1)
                        dve.wait_ge(gathered[n], 16 * i + 16)
                        if c >= 2:
                            dve.wait_ge(used[h], HALF * i + c)
                        else:
                            dve.wait_ge(used[1 - h], HALF * (i + h) + 1)
                        nc.vector.tensor_tensor(
                            prod[:, c % 2, :].rearrange("p (k d) -> p k d", d=C)[:, 0:8:7, :], w[:, 0:2, :],
                            bc(got[:, n, 0:C].unsqueeze(1), [P, 2, C]), ALU.mult)
                        nc.vector.tensor_tensor(
                            prod[:, c % 2, C:7 * C].rearrange("p (k a d) -> p k a d", k=2, d=C),
                            bc(w[:, 2:4, :].unsqueeze(2), [P, 2, 3, C]),
                            bc(got[:, n, C:].rearrange("p (a d) -> p a d", d=C).unsqueeze(1), [P, 2, 3, C]),
                            ALU.mult).then_inc(prods, 1)

                    def add(c):
                        n = HALF * h + c
                        b = nc.vector.value_load(K.bucket["dst"][0:1, bass.ds(i * TURN + n, 1)], min_val=0,
                                                 max_val=TILES - 1)
                        dve.wait_ge(used[h], HALF * i + c + 2)
                        dve.wait_ge(added, i * TURN + n + 2)
                        nc.vector.tensor_tensor(acc[:, b, :], acc[:, b, :], K.ps[SUM_BANK + c % 2][:, 0:DIM],
                                                ALU.add).then_inc(added, 1)

                    multiply(0)
                    for c in range(1, HALF):
                        multiply(c)
                        add(c - 1)
                    add(HALF - 1)

        @block.scalar
        def _(act):
            with act.Fori(0, TURNS) as i:
                for h in range(2):
                    half = i * 2 + h
                    act.wait_ge(attr_turned, half + 2)
                    nc.scalar.activation(attrT[:, :], K.ps[TURN_BANK][:, 0:P], ACT.Copy).then_inc(attrT_ready, 1)
                    for n in range(3):
                        act.wait_ge(layer, half * 3 + n + 1)
                        nc.scalar.activation(hid[:, n, :], K.ps[MLP_BANK + n % 2][:, :], ACT.Silu).then_inc(act_done, 1)
                    for c in range(HALF):
                        act.wait_ge(matched, half * HALF + c + 1)
                        if c >= 2:
                            act.wait_ge(used[h], HALF * i + c)
                        else:
                            act.wait_ge(used[1 - h], HALF * (i + h) + 1)
                        for k in range(4):
                            ins = nc.scalar.activation(pick[:, c % 2, k, :], same[:, c % 2, :], ACT.Copy,
                                                       scale=row[:, h, c, 3 + k:4 + k])
                        ins.then_inc(picked, 1)

        @block.tensor
        def _(pe):
            pe.wait_ge(w_loaded, 64)
            pe.wait_ge(scaled, 1)
            with pe.Fori(0, TURNS) as i:
                for h in range(2):
                    half = i * 2 + h
                    pe.wait_ge(attr_ready, half + 1)
                    nc.tensor.transpose(K.ps[TURN_BANK][:, 0:P], attr[:, :], K.ident[:, :]).then_inc(attr_turned, 1)
                    pe.wait_ge(attrT_ready, half + 1)
                    for j in range(HALF // 2):
                        ins = nc.tensor.matmul(K.ps[MLP_BANK][:, j * P:(j + 1) * P], m1s[:, j, :], attrT[:, :],
                                               start=True, stop=True)
                    ins.then_inc(layer, 1)
                    for n, w in ((1, m2s), (2, m3s)):
                        pe.wait_ge(act_done, half * 3 + n)
                        nc.tensor.matmul(K.ps[MLP_BANK + n % 2][:, :], w[:, :], hid[:, n - 1, :], start=True,
                                         stop=True).then_inc(layer, 1)
                    pe.wait_ge(act_done, half * 3 + 3)

                    def weigh(c):
                        lo = C * (c % 2)
                        if c >= 2:
                            pe.wait_ge(prods, half * HALF + c - 1)
                        nc.tensor.matmul(K.ps[W_BANK + c % 2][:, 0:DIM], hid[lo:lo + C, 2, (c // 2) * P:(c // 2 + 1) * P],
                                         m4s[lo:lo + C, :], start=True, stop=True).then_inc(weights, 1)

                    weigh(0)
                    weigh(1)
                    for c in range(HALF):
                        n = HALF * h + c
                        pe.wait_ge(prods, half * HALF + c + 1)
                        pe.wait_ge(picked, half * HALF + c + 3)
                        pe.wait_ge(added, i * TURN + n + 1)
                        bank = K.ps[SUM_BANK + c % 2]
                        nc.tensor.matmul(bank[:, 0:DIM], pick[:, c % 2, 0, :], prod[:, c % 2, 0:DIM], start=True, stop=False)
                        for a in range(3):
                            both = prod[:, c % 2, :].rearrange("p (k d) -> p k d", d=C)[:, 4 + a:8:3 - a, :]
                            into = bank[:, 0:DIM].rearrange("p (k d) -> p k d", d=C)[:, 0:2 + a:1 + a, :]
                            ins = nc.tensor.matmul(into, pick[:, c % 2, 1 + a, :], both, start=False, stop=(a == 2))
                        ins.then_inc(used[h], 1)
                        if c + 2 < HALF:
                            weigh(c + 2)


def mix_stage(nc, K, msg, sc, w_lin, w_b, poly0, poly1, o_out):
    with stage(nc, "mix") as s:
        wl, wb = s.sb("wl", [P, 2, P]), s.sb("wb", [P, 2, P])
        c0, c1 = s.sb("c0", [P, 5, C]), s.sb("c1", [P, 4, C])
        mb, scb = s.sb("mb", [P, BT, DIM]), s.sb("scb", [P, BT, DIM])
        T = s.sb("T", [P, 2 * BT, P])
        a = s.sb("a", [P, BT, DIM])
        bb = s.sb("bb", [P, BT, DIM])
        a2, vv, t0, t1 = (s.sb(n, [P, BT, C]) for n in ("a2", "vv", "t0", "t1"))
        w_loaded, loaded, turned, T_ready, product, copied, poly, step, written, o_ready, b_ready = (
            s.sem(n) for n in ("w_loaded", "loaded", "turned", "T_ready", "product", "copied", "poly", "step",
                               "written", "o_ready", "b_ready"))
        block = s.block()
        NB = 4

        @block.sync
        def _(sp):
            sp.dma_start(wl[:, :, :], w_lin[:, :, :]).then_inc(w_loaded, 16)
            sp.dma_start(wb[:, :, :], w_b[:, :, :]).then_inc(w_loaded, 16)
            for tile, array, n in ((c0, poly0, 5), (c1, poly1, 4)):
                sp.dma_start(tile[:, :, :], array.rearrange("(a n) d -> a n d", a=1).broadcast_to([P, n, C])).then_inc(w_loaded, 16)

            def turn(i, first=False):
                if not first:
                    sp.wait_ge(written, 16 * i)
                load_block(sp, (msg, sc), (mb, scb), i, loaded)
                sp.wait_ge(o_ready, i + 1)
                sp.dma_start(tiles_of(o_out)[:, bass.ds(i * BT, BT), :], scb[:, :, :]).then_inc(written, 16)

            turn(0, first=True)
            with sp.Fori(1, BLOCKS) as i:
                turn(i)
            sp.wait_ge(written, 16 * BLOCKS)

        @block.tensor
        def _(pe):
            pe.wait_ge(w_loaded, 64)
            with pe.Fori(0, BLOCKS) as i:
                for r, (src, w) in enumerate(((mb, wl), (bb, wb))):
                    if r == 0:
                        pe.wait_ge(loaded, 32 * i + 32)
                    else:
                        pe.wait_ge(b_ready, i + 1)
                    for n in range(NB):
                        pe.wait_ge(T_ready, (2 * i + r) * NB + n + 1)
                        for m in range(4 * n, min(4 * n + 4, 2 * BT)):
                            ins = nc.tensor.transpose(K.ps[n][:, (m % 4) * P:(m % 4 + 1) * P],
                                                      src[:, m // 2, (m % 2) * P:(m % 2 + 1) * P], K.ident[:, :])
                        ins.then_inc(turned, 1)
                    pe.wait_ge(T_ready, (2 * i + r + 1) * NB + 4)
                    for j in range(BT):
                        pe.wait_ge(copied, (2 * i + r) * BT + j + 1)
                        for k in range(2):
                            ins = nc.tensor.matmul(K.ps[4 + j % 4][:, k * P:(k + 1) * P], T[:, 2 * j + k, :], w[:, k, :],
                                                   start=True, stop=True)
                        ins.then_inc(product, 1)

        @block.scalar
        def _(act):
            act.sem_inc(T_ready, 4)
            with act.Fori(0, BLOCKS) as i:
                for r in range(2):
                    act.wait_ge(copied, (2 * i + r) * BT + 4)
                    hold(act)
                    for n in range(NB):
                        act.wait_ge(turned, (2 * i + r) * NB + n + 1)
                        width = min(4, 2 * BT - 4 * n)
                        nc.scalar.activation(T[:, 4 * n:4 * n + width, :],
                                             K.ps[n][:, 0:width * P].rearrange("p (m q) -> p m q", q=P),
                                             ACT.Copy).then_inc(T_ready, 1)

        @block.vector
        def _(dve):
            dve.wait_ge(w_loaded, 64)
            dve.sem_inc(copied, 4)
            STEPS = 21
            with dve.Fori(0, BLOCKS) as i:
                link = Chain(dve, step, i * STEPS)
                TT = nc.vector.tensor_tensor
                wide = lambda t: bc(t.unsqueeze(1), [P, BT, C])
                for j in range(BT):
                    dve.wait_ge(product, 2 * i * BT + j + 1)
                    nc.vector.tensor_copy(a[:, j, :], K.ps[4 + j % 4][:, 0:DIM]).then_inc(copied, 1)
                dve.wait_ge(copied, 2 * i * BT + BT + 4)
                A0 = a[:, :, 0:C]
                A1 = a[:, :, C:].rearrange("p j (x d) -> p j x d", d=C)
                B0, tt = bb[:, :, 0:C], t1[:, :, :]
                link(TT(bb[:, :, C:], a[:, :, C:], a[:, :, C:], ALU.mult))
                link(TT(vv[:, :, :], bb[:, :, C:2 * C], bb[:, :, 2 * C:3 * C], ALU.add))
                link(TT(vv[:, :, :], vv[:, :, :], bb[:, :, 3 * C:], ALU.add))
                link(TT(a2[:, :, :], A0, A0, ALU.mult))
                link(TT(t0[:, :, :], A0, wide(c1[:, 1, :]), ALU.mult))
                link(TT(t0[:, :, :], t0[:, :, :], wide(c1[:, 0, :]), ALU.add))
                link(TT(tt, a2[:, :, :], wide(c1[:, 2, :]), ALU.mult))
                link(TT(t0[:, :, :], t0[:, :, :], tt, ALU.add))
                link(TT(tt, vv[:, :, :], wide(c1[:, 3, :]), ALU.mult))
                link(TT(t0[:, :, :], t0[:, :, :], tt, ALU.add))
                for x in range(3):
                    ins = TT(bb[:, :, C + C * x:2 * C + C * x], a[:, :, C + C * x:2 * C + C * x], t0[:, :, :], ALU.mult)
                link(ins)
                link(TT(B0, A0, wide(c0[:, 0, :]), ALU.mult))
                link(TT(tt, a2[:, :, :], wide(c0[:, 1, :]), ALU.mult))
                link(TT(B0, B0, tt, ALU.add))
                link(TT(tt, vv[:, :, :], wide(c0[:, 2, :]), ALU.mult))
                link(TT(B0, B0, tt, ALU.add))
                link(TT(a2[:, :, :], a2[:, :, :], A0, ALU.mult))
                link(TT(tt, a2[:, :, :], wide(c0[:, 3, :]), ALU.mult))
                link(TT(B0, B0, tt, ALU.add))
                link(TT(vv[:, :, :], vv[:, :, :], A0, ALU.mult))
                link(TT(tt, vv[:, :, :], wide(c0[:, 4, :]), ALU.mult))
                TT(B0, B0, tt, ALU.add).then_inc(b_ready, 1)
                for j in range(BT):
                    dve.wait_ge(product, (2 * i + 1) * BT + j + 1)
                    TT(scb[:, j, :], scb[:, j, :], K.ps[4 + j % 4][:, 0:DIM], ALU.add).then_inc(copied, 1)
                dve.wait_ge(copied, (2 * i + 2) * BT + 4)
                nc.vector.tensor_copy(t0[:, 0:1, 0:1], t0[:, 0:1, 0:1]).then_inc(o_ready, 1)
                assert link.n == STEPS, link.n


def finish_stage(nc, K, o, x2, gamma0, beta0, gamma1, r3_out, y3_out):
    with stage(nc, "fin") as s:
        ob = s.sb("ob", [P, TILES, DIM])
        xb = s.sb("xb", [P, BT, DIM])
        yb = s.sb("yb", [P, BT, DIM])
        sq = s.sb("sq", [P, 2, DIM])
        gain = s.sb("gain", [P, DIM])
        shift = s.sb("shift", [P, C])
        g0 = s.sb("g0", [P, 2 * C])
        b0 = s.sb("b0", [P, C])
        norm = RowNorm(nc, s, K)
        loaded, x_loaded, sums, centred, squared, squares, used, col_sd, step, r_ready, written = (
            s.sem(n) for n in ("loaded", "x_loaded", "sums", "centred", "squared", "squares", "used", "col_sd", "step",
                               "r_ready", "written"))
        block = s.block()

        @block.sync
        def _(sp):
            sp.dma_start(ob[:, :, :], tiles_of(o)).then_inc(loaded, 16)
            sp.dma_start(g0[:, 0:C], row_bc(gamma0)).then_inc(loaded, 16)
            sp.dma_start(g0[:, C:], row_bc(gamma1)).then_inc(loaded, 16)
            sp.dma_start(b0[:, :], row_bc(beta0)).then_inc(loaded, 16)

            def turn(i, first=False):
                if not first:
                    sp.wait_ge(written, 32 * i)
                load_block(sp, (x2,), (xb,), i, x_loaded)
                sp.wait_ge(r_ready, i + 1)
                sp.dma_start(tiles_of(r3_out)[:, bass.ds(i * BT, BT), :], xb[:, :, :]).then_inc(written, 16)
                sp.dma_start(tiles_of(y3_out)[:, bass.ds(i * BT, BT), :], yb[:, :, :]).then_inc(written, 16)

            turn(0, first=True)
            with sp.Fori(1, BLOCKS) as i:
                turn(i)
            sp.wait_ge(written, 32 * BLOCKS)

        @block.tensor
        def _(pe):
            pe.wait_ge(loaded, 64)
            nc.tensor.matmul(K.ps[0][:, 0:C], K.ones[:, :], ob[:, 0, 0:C], start=True, stop=False)
            with pe.Fori(1, TILES - 1) as t:
                nc.tensor.matmul(K.ps[0][:, 0:C], K.ones[:, :], ob[:, t, 0:C], start=False, stop=False)
            nc.tensor.matmul(K.ps[0][:, 0:C], K.ones[0:TAIL, :], ob[0:TAIL, TILES - 1, 0:C], start=False,
                             stop=True).then_inc(sums, 1)
            pe.sem_inc(used, 2)
            for t in range(2):
                pe.wait_ge(squared, t + 1)
                nc.tensor.matmul(K.ps[1][:, 0:DIM], K.ones[:, :], sq[:, t, :], start=(t == 0), stop=False).then_inc(used, 1)
            with pe.Fori(1, (TILES - 1) // 2) as i:
                for k in range(2):
                    pe.wait_ge(squared, 2 * i + k + 1)
                    nc.tensor.matmul(K.ps[1][:, 0:DIM], K.ones[:, :], sq[:, k, :], start=False, stop=False).then_inc(used, 1)
            pe.wait_ge(squared, TILES)
            nc.tensor.matmul(K.ps[1][:, 0:DIM], K.ones[0:TAIL, :], sq[0:TAIL, 0, :], start=False,
                             stop=True).then_inc(squares, 1)

        @block.scalar
        def _(act):
            act.wait_ge(centred, 1)
            with act.Fori(0, (TILES - 1) // 2) as i:
                for k in range(2):
                    act.wait_ge(used, 2 * i + k + 1)
                    nc.scalar.activation(sq[:, k, :], ob[:, 2 * i + k, :], ACT.Square).then_inc(squared, 1)
            act.wait_ge(used, TILES)
            nc.scalar.activation(sq[:, 0, :], ob[:, TILES - 1, :], ACT.Square).then_inc(squared, 1)
            act.wait_ge(step, 4)
            nc.scalar.activation(gain[:, 0:C], gain[:, 0:C], ACT.Sqrt, bias=K.eps[:, :], scale=1.0 / NODES)
            nc.scalar.activation(gain[:, C:2 * C], gain[:, C:2 * C], ACT.Sqrt, bias=K.eps[:, :],
                                 scale=1.0 / (3 * NODES)).then_inc(col_sd, 1)
            with act.Fori(0, BLOCKS) as i:
                norm.on_scalar(act, i)

        @block.vector
        def _(dve):
            link = Chain(dve, step)
            TT = nc.vector.tensor_tensor
            dve.wait_ge(sums, 1)
            link(nc.vector.tensor_scalar(shift[:, :], K.ps[0][:, 0:C], 1.0 / NODES, None, ALU.mult))
            TT(ob[:, :, 0:C], ob[:, :, 0:C], bc(shift[:, :].unsqueeze(1), [P, TILES, C]), ALU.subtract).then_inc(centred, 1)
            dve.wait_ge(squares, 1)
            link(nc.vector.tensor_copy(gain[:, :], K.ps[1][:, 0:DIM]))
            link(TT(gain[:, C:2 * C], gain[:, C:2 * C], gain[:, 2 * C:3 * C], ALU.add))
            link(TT(gain[:, C:2 * C], gain[:, C:2 * C], gain[:, 3 * C:], ALU.add))
            dve.wait_ge(col_sd, 1)
            link(nc.vector.reciprocal(gain[:, 0:2 * C], gain[:, 0:2 * C]))
            link(TT(gain[:, 0:2 * C], gain[:, 0:2 * C], g0[:, :], ALU.mult))
            dve.wait_ge(centred, 1)
            for x in range(4):
                ins = TT(ob[:, :, x * C:(x + 1) * C], ob[:, :, x * C:(x + 1) * C],
                         bc(gain[:, min(x, 1) * C:(min(x, 1) + 1) * C].unsqueeze(1), [P, TILES, C]), ALU.mult)
            link(ins)
            link(TT(ob[:, :, 0:C], ob[:, :, 0:C], bc(b0[:, :].unsqueeze(1), [P, TILES, C]), ALU.add))
            base = link.n

            def turn(i, first=False):
                here = Chain(dve, step, i * 2 + base)
                dve.wait_ge(x_loaded, 16 * i + 16)
                TT(xb[:, :, 0:C], xb[:, :, 0:C], ob[:, bass.ds(i * BT, BT), 0:C], ALU.add)
                for x in range(3):
                    into = xb[:, :, C:].rearrange("p j (d x) -> p j d x", x=3)[:, :, :, x]
                    ins = TT(into, into, ob[:, bass.ds(i * BT, BT), (x + 1) * C:(x + 2) * C], ALU.add)
                here(ins)
                here(nc.vector.tensor_copy(yb[:, :, :], xb[:, :, :]))
                norm.on_vector(dve, i, lambda j: yb[:, j, :])
                dve.wait_ge(norm.done, i + 1)
                TT(xb[:, :, :], xb[:, :, :], yb[:, :, :], ALU.add).then_inc(r_ready, 1)

            with dve.Fori(0, BLOCKS) as i:
                turn(i)


def ffn_stage(nc, K, y3, wr, br, w1, b1, w2, b2, z_out, score):
    M = HID // P
    WIDE = TOK // 2
    NB = 4
    with stage(nc, "ffn") as s:
        w1s = s.sb("w1", [P, 2, HID])
        w2s = s.sb("w2", [P, M, DIM])
        b1s = s.sb("b1", [P, M])
        b2s, wrs = s.sb("b2", [P, DIM]), s.sb("wr", [P, DIM])
        brs = s.sb("br", [P, 1])
        yb = s.sb("yb", [P, BT, DIM])
        scr = s.sb("scr", [P, BT, DIM])
        yT = s.sb("yT", [P, 2, TOK])
        hT = s.sb("hT", [P, M, TOK])
        z = s.sb("z", [P, BT, DIM])
        (w_loaded, loaded, turned, yT_ready, hidden, hT_ready, output, used, weighed, scored, step, written) = (
            s.sem(n) for n in ("w_loaded", "loaded", "turned", "yT_ready", "hidden", "hT_ready", "output", "used",
                               "weighed", "scored", "step", "written"))
        block = s.block()

        @block.sync
        def _(sp):
            sp.dma_start(w1s[:, :, :], w1.rearrange("(k p) n -> p k n", p=P)).then_inc(w_loaded, 16)
            sp.dma_start(w2s[:, :, :], w2.rearrange("(m p) n -> p m n", p=P)).then_inc(w_loaded, 16)
            with nc.allow_non_contiguous_dma("the first bias, once"):
                sp.dma_start(b1s[:, :], b1.rearrange("(m p) -> p m", p=P)).then_inc(w_loaded, 16)
            sp.dma_start(b2s[:, :], row_bc(b2)).then_inc(w_loaded, 16)
            sp.dma_start(wrs[:, :], row_bc(wr.rearrange("d o -> (d o)"))).then_inc(w_loaded, 16)
            sp.dma_start(brs[:, :], row_bc(br)).then_inc(w_loaded, 16)
            with sp.Fori(0, BLOCKS) as i:
                sp.wait_ge(scored, i + 1)
                sp.wait_ge(turned, i * NB + 1)
                load_block(sp, (y3,), (yb,), i, loaded)

        @block.gpsimd
        def _(pool):
            with pool.Fori(0, BLOCKS) as i:
                pool.wait_ge(weighed, i + 1)
                hold(pool)
                pool.dma_start(tiles_of(z_out)[:, bass.ds(i * BT, BT), :], z[:, :, :]).then_inc(written, 16)
            pool.wait_ge(written, 16 * BLOCKS)

        @block.tensor
        def _(pe):
            pe.wait_ge(w_loaded, 96)
            pe.sem_inc(turned, 1)
            with pe.Fori(0, BLOCKS) as i:
                pe.wait_ge(loaded, 16 * i + 16)
                for n in range(NB):
                    pe.wait_ge(yT_ready, i * NB + n + 1)
                    pe.wait_ge(hT_ready, i * 2 * M + 4)
                    for m in range(4 * n, min(4 * n + 4, 2 * BT)):
                        k, j = divmod(m, BT)
                        ins = nc.tensor.transpose(K.ps[n][:, (m % 4) * P:(m % 4 + 1) * P],
                                                  yb[:, j, k * P:(k + 1) * P], K.ident[:, :])
                    ins.then_inc(turned, 1)
                pe.wait_ge(yT_ready, (i + 1) * NB + 4)
                for m in range(M):
                    for q in range(2):
                        n = 2 * m + q
                        pe.wait_ge(hT_ready, i * 2 * M + n + 1)
                        for k in range(2):
                            ins = nc.tensor.matmul(K.ps[n % 4][:, 0:WIDE], w1s[:, k, m * P:(m + 1) * P],
                                                   yT[:, k, q * WIDE:(q + 1) * WIDE], start=(k == 0), stop=(k == 1))
                        ins.then_inc(hidden, 1)
                pe.wait_ge(hT_ready, (i + 1) * 2 * M + 4)
                for j in range(BT):
                    pe.wait_ge(used, i * BT + j + 1)
                    for m in range(M):
                        ins = nc.tensor.matmul(K.ps[4 + j % 4][:, 0:DIM], hT[:, m, j * P:(j + 1) * P], w2s[:, m, :],
                                               start=(m == 0), stop=(m == M - 1))
                    ins.then_inc(output, 1)

        @block.scalar
        def _(act):
            act.sem_inc(yT_ready, 4)
            act.sem_inc(hT_ready, 4)
            with act.Fori(0, BLOCKS) as i:
                act.wait_ge(used, i * BT + 4)
                hold(act)
                for n in range(NB):
                    act.wait_ge(turned, i * NB + n + 2)
                    width = min(4, 2 * BT - 4 * n)
                    nc.scalar.activation(yT[:, :, :].rearrange("p k t -> p (k t)")[:, 4 * n * P:(4 * n + width) * P],
                                         K.ps[n][:, 0:width * P], ACT.Copy).then_inc(yT_ready, 1)
                for m in range(M):
                    for q in range(2):
                        n = 2 * m + q
                        act.wait_ge(hidden, i * 2 * M + n + 1)
                        nc.scalar.activation(hT[:, m, q * WIDE:(q + 1) * WIDE], K.ps[n % 4][:, 0:WIDE],
                                             ACT.Gelu_apprx_tanh, bias=b1s[:, m:m + 1]).then_inc(hT_ready, 1)

        @block.vector
        def _(dve):
            dve.wait_ge(w_loaded, 96)
            dve.sem_inc(used, 4)
            dve.sem_inc(scored, 1)
            TT = nc.vector.tensor_tensor

            def turn(i, first=False):
                link = Chain(dve, step, i * 2)
                dve.wait_ge(loaded, 16 * i + 16)
                link(TT(scr[:, :, :], yb[:, :, :], bc(wrs[:, :].unsqueeze(1), [P, BT, DIM]), ALU.mult))
                at = score[:, bass.ds(i * BT, BT)]
                link(nc.vector.tensor_reduce(at, scr[:, :, :], AXX, ALU.add))
                nc.vector.tensor_scalar(at, at, brs[:, :], None, ALU.add).then_inc(scored, 1)
                dve.wait_ge(scored, i + 2)
                if not first:
                    dve.wait_ge(written, 16 * i)
                for j in range(BT):
                    dve.wait_ge(output, i * BT + j + 1)
                    TT(z[:, j, :], K.ps[4 + j % 4][:, 0:DIM], b2s[:, :], ALU.add).then_inc(used, 1)
                dve.wait_ge(used, (i + 1) * BT + 4)
                TT(z[:, :, :], z[:, :, :], bc(at.unsqueeze(2), [P, BT, DIM]), ALU.mult).then_inc(weighed, 1)

            turn(0, first=True)
            with dve.Fori(1, BLOCKS) as i:
                turn(i)


def select_stage(nc, K, score, z, r3, out):
    KEPT = max(1, int(0.5 * NODES)) - 1
    SIGN = -2 ** 31
    with stage(nc, "sel") as s:
        zb = s.sb("zb", [P, TILES, DIM])
        rb = s.sb("rb", [P, TILES, DIM])
        w = s.sb("w", [P, TILES])
        hit = s.sb("hit", [P, TILES])
        above = s.sb("above", [P, TILES])
        prior = s.sb("prior", [P, TILES])
        order = s.sb("order", [P, 1], I32)
        trial, neg, word = (s.sb(n, [P, 1], I32) for n in ("trial", "neg", "word"))
        bits = s.sb("bits", [P, 32], I32)
        keep = s.sb("keep", [P, 1])
        keep_i = s.sb("keep_i", [P, 1], I32)
        cnt = s.sb("cnt", [P, 1])
        loaded, masked, bits_ready, counted, summed, step, turned_on, ready, written = (
            s.sem(n) for n in ("loaded", "masked", "bits_ready", "counted", "summed", "step", "turned_on", "ready",
                               "written"))
        block = s.block()

        @block.sync
        def _(sp):
            sp.dma_start(zb[:, :, :], tiles_of(z)).then_inc(loaded, 16)
            sp.dma_start(rb[:, :, :], tiles_of(r3)).then_inc(loaded, 16)
            sp.wait_ge(ready, 1)
            full = (TILES - 1) * P
            sp.dma_start(tiles_of(out[0:full, :]), rb[:, 0:TILES - 1, :]).then_inc(written, 16)
            sp.dma_start(out[full:NODES, :], rb[0:TAIL, TILES - 1, :]).then_inc(written, 16)
            sp.wait_ge(written, 32)

        @block.gpsimd
        def _(pool):
            nc.gpsimd.affine_select(out=w[:, :], in_=score[:, :], compare_op=ALU.is_ge, fill=-3.4028234663852886e38,
                                    base=NODES - 1, pattern=[[-P, TILES]], channel_multiplier=-1).then_inc(masked, 1)

        @block.tensor
        def _(pe):
            with pe.Fori(0, 33) as n:
                pe.wait_ge(counted, n + 1)
                nc.tensor.matmul(K.ps[0][:, 0:1], K.ones[:, :], cnt[:, :], start=True, stop=True).then_inc(summed, 1)
            pe.wait_ge(counted, 34)
            nc.tensor.matmul(K.ps[1][:, 0:TILES], K.before[:, :], hit[:, :], start=True, stop=True)
            nc.tensor.matmul(K.ps[2][:, 0:TILES], K.ones[:, :], hit[:, :], start=True, stop=True).then_inc(summed, 1)

        @block.vector
        def _(dve):
            link = Chain(dve, step)
            TS, TT = nc.vector.tensor_scalar, nc.vector.tensor_tensor
            link(nc.vector.memset(order[:, :], 0))
            for n in range(32):
                link(nc.vector.memset(bits[:, n:n + 1], SIGN if n == 0 else 1 << (31 - n)))
            dve.wait_ge(masked, 1)

            def to_float(into, code):
                yield TS(neg[:, :], code[:, :], 31, None, ALU.arith_shift_right)
                yield TS(word[:, :], neg[:, :], -1, SIGN, ALU.bitwise_xor, ALU.bitwise_or)
                yield TT(into[:, :], code[:, :], word[:, :], ALU.bitwise_xor)

            base = link.n
            STEPS = 7
            with dve.Fori(0, 32) as n:
                here = Chain(dve, step, base + n * STEPS)
                here(TT(trial[:, :], order[:, :], bits[:, bass.ds(n, 1)], ALU.bitwise_or))
                for ins in to_float(keep_i, trial):
                    here(ins)
                TS(hit[:, :], w[:, :], keep_i[:, :].bitcast(F32), None, ALU.is_ge, ALU.add,
                   accum_out=cnt[:, :]).then_inc(counted, 1)
                dve.wait_ge(summed, n + 1)
                here(TS(keep[:, :], K.ps[0][:, 0:1], float(KEPT), -1.0, ALU.is_ge, ALU.mult))
                here(nc.vector.tensor_copy(neg[:, :], keep[:, :]))
                TT(neg[:, :], neg[:, :], bits[:, bass.ds(n, 1)], ALU.bitwise_and).then_inc(turned_on, 1)
                dve.wait_ge(turned_on, n + 1)
                here(TT(order[:, :], order[:, :], neg[:, :], ALU.bitwise_or))
            link = Chain(dve, step, base + 32 * STEPS)
            for ins in to_float(trial, order):
                link(ins)
            lowest = trial[:, :].bitcast(F32)
            TS(above[:, :], w[:, :], lowest, None, ALU.is_gt, ALU.add, accum_out=cnt[:, :]).then_inc(counted, 1)
            dve.wait_ge(summed, 33)
            link(TS(cnt[:, :], K.ps[0][:, 0:1], -1.0, float(KEPT), ALU.mult, ALU.add))
            TS(hit[:, :], w[:, :], lowest, None, ALU.is_equal).then_inc(counted, 1)
            dve.wait_ge(summed, 34)
            link(nc.vector.memset(prior[:, 0:1], 0.0))
            link(nc.vector.tensor_copy(w[:, :], K.ps[2][:, 0:TILES]))
            link(nc.vector.tensor_tensor_scan(prior[:, 1:TILES], w[:, 0:TILES - 1], w[:, 0:TILES - 1], 0.0, ALU.add, ALU.max))
            link(TT(prior[:, :], prior[:, :], K.ps[1][:, 0:TILES], ALU.add))
            link(TS(prior[:, :], prior[:, :], cnt[:, :], None, ALU.is_lt))
            link(TT(prior[:, :], prior[:, :], hit[:, :], ALU.mult))
            link(TT(above[:, :], above[:, :], prior[:, :], ALU.add))
            dve.wait_ge(loaded, 32)
            link(TT(zb[:, :, :], zb[:, :, :], bc(above[:, :].unsqueeze(2), [P, TILES, DIM]), ALU.mult))
            TT(rb[:, :, :], rb[:, :, :], zb[:, :, :], ALU.add).then_inc(ready, 1)


class Consts:
    def __init__(self, nc, ctx):
        def sb(name, shape, dt=F32):
            return ctx.enter_context(nc.sbuf_tensor(name, shape, dt))
        self.ones, self.ident, self.before, self.upto = (sb(n, [P, P]) for n in ("ones", "ident", "before", "upto"))
        self.count = sb("count", [P, CHUNKS])
        self.count_i = sb("count_i", [P, CHUNKS], I32)
        self.eps = sb("eps", [P, 1])
        self.bucket = {side: sb(f"bucket_{side}", [1, CHUNKS], I32) for side in ("dst", "src")}
        self.ps = [ctx.enter_context(nc.psum_tensor(f"ps{n}", [P, 512], F32)) for n in range(8)]


def program(nc, A, out):
    def nodes(name):
        return nc.dram_tensor(name, [ROWS, DIM], F32).ap()

    rows_dst = nc.dram_tensor("rows_dst", [CHUNKS * P, META], F32).ap()
    rows_src = nc.dram_tensor("rows_src", [CHUNKS * P, META2], F32).ap()
    x0, h, feat_in, feat_out, a_in, a_out = (nodes(n) for n in ("x0", "h", "feat_in", "feat_out", "a_in", "a_out"))
    x1, y1, x2, y2, up, skip, msg, o = (nodes(n) for n in ("x1", "y1", "x2", "y2", "up", "skip", "msg", "o"))
    r3, y3, z = (nodes(n) for n in ("r3", "y3", "z"))
    with ExitStack() as ctx:
        K = Consts(nc, ctx)
        setup_stage(nc, K, A["x"], x0, rows_dst, rows_src)
        norm_stage(nc, K, x0, A["L0_gnn_gamma"], A["L0_gnn_beta"], h)
        project_stage(nc, K, "proj0", h, (A["L0_gnn_W_in"], A["L0_gnn_W_out"]), (A["L0_gnn_b_in"], A["L0_gnn_b_out"]),
                      (feat_in, feat_out))
        with ExitStack() as edge_ctx:
            E = Edges(nc, edge_ctx)
            load_edges_stage(nc, E, A["src"], A["dst"], A["edge_weight_n2"])
            sort_stage(nc, K, "dst", E.dst, E.place_dst, E.local_dst)
            sort_stage(nc, K, "src", E.src, E.place_src, E.local_src)
            permute_stage(nc, K, A["edge_rows"], E, rows_dst, rows_src)
        gather_stage(nc, K, "dst", rows_dst, META, feat_in, a_in)
        gather_stage(nc, K, "src", rows_src, META2, feat_out, a_out)
        update_stage(nc, K, x0, h, a_in, a_out, A["L0_gnn_W_x2i"], A["L0_gnn_b_x2i"], A["L0_gnn_W_h2h"], x1, y1)
        moe_stage(nc, K, y1, x1, A["router_T"], A["L0_ffn_w1"], A["L0_ffn_b1"], A["L0_ffn_w2"], A["L0_ffn_b2"], x2, y2)
        project_stage(nc, K, "proj1", y2, (A["W_up"], A["W_sc"]), None, (up, skip))
        message_stage(nc, K, rows_dst, up, A["M1_blocks"], A["M2_blocks"], A["M3_blocks"], A["M4_twice"], msg)
        mix_stage(nc, K, msg, skip, A["W_lin"], A["W_wb"], A["poly0"], A["poly1"], o)
        finish_stage(nc, K, o, x2, A["L1_gnn_gamma0"], A["L1_gnn_beta0"], A["L1_gnn_gamma1"], r3, y3)
        score = ctx.enter_context(nc.sbuf_tensor("score", [P, TILES], F32))
        ffn_stage(nc, K, y3, A["L1_ffn_wr"], A["L1_ffn_br"], A["L1_ffn_w1"], A["L1_ffn_b1"], A["L1_ffn_w2"],
                  A["L1_ffn_b2"], z, score)
        select_stage(nc, K, score, z, r3, out)


def kernel(**inputs):
    import numpy as np
    import concourse.bacc as bacc
    from concourse.bass_utils import run_bass_kernel_spmd

    nc = bacc.Bacc("TRN2", target_bir_lowering=False, num_devices=1)
    laid = {name: np.asarray(a) for name, a in inputs.items() if name in USED}
    rows = np.zeros((EDGES, META), np.float32)
    rows[:, 2] = np.asarray(inputs["edge_weight"])
    rows[:, 3:7] = np.asarray(inputs["edge_attr_4"])
    rows[:, 8:24] = np.asarray(inputs["edge_attr_16"])
    laid["edge_rows"] = rows
    for name, w0, w1 in (("up", "L1_gnn_W_up0", "L1_gnn_W_up1"), ("sc", "L1_gnn_Wsc0", "L1_gnn_Wsc1")):
        w = np.zeros((DIM, DIM), np.float32)
        w[:C, :C] = np.asarray(inputs[w0])
        for a in range(3):
            w[C + a::3, C + C * a:2 * C + C * a] = np.asarray(inputs[w1])
        laid["W_" + name] = w
    m1 = np.zeros((P, HALF // 2, P), np.float32)
    for c in range(HALF):
        m1[MLP_IN * c:MLP_IN * (c + 1), c // 2, C * (c % 2):C * (c % 2 + 1)] = np.asarray(inputs["L1_gnn_M1"])
    laid["M1_blocks"] = m1
    for name in ("M2", "M3"):
        w = np.zeros((P, P), np.float32)
        w[:C, :C] = w[C:, C:] = np.asarray(inputs["L1_gnn_" + name])
        laid[name + "_blocks"] = w
    laid["M4_twice"] = np.concatenate([np.asarray(inputs["L1_gnn_M4"])] * 2)
    for name, w0, w1 in (("lin", "L1_gnn_W_lin0", "L1_gnn_W_lin1"), ("wb", "L1_gnn_WB0", "L1_gnn_WB1")):
        w = np.zeros((P, 2, P), np.float32)
        w[:C, 0, :C] = np.asarray(inputs[w0])
        w[C:, 0, C:] = w[:C, 1, :C] = w[C:, 1, C:] = np.asarray(inputs[w1])
        laid["W_" + name] = w
    laid["poly0"] = np.ascontiguousarray(np.asarray(inputs["L1_gnn_Wc0"]).T)
    laid["poly1"] = np.ascontiguousarray(np.asarray(inputs["L1_gnn_Wc1"]).T)
    laid["router_T"] = np.ascontiguousarray(np.asarray(inputs["L0_ffn_router_w"]).T)
    arrays, A = {}, {}
    for name, a in laid.items():
        arrays[f"in_{name}"] = np.ascontiguousarray(a)
        A[name] = nc.dram_tensor(f"in_{name}", a.shape, mybir.dt.from_np(a.dtype), kind="ExternalInput").ap()
    out = nc.dram_tensor("out_0", (NODES, DIM), F32, kind="ExternalOutput").ap()
    program(nc, A, out)
    return run_bass_kernel_spmd(nc, [arrays], core_ids=[0]).results[0]["out_0"]


USED = ["x", "src", "dst", "edge_weight_n2", "L0_gnn_gamma", "L0_gnn_beta", "L0_gnn_W_in", "L0_gnn_b_in", "L0_gnn_W_out",
        "L0_gnn_b_out", "L0_gnn_W_x2i", "L0_gnn_b_x2i", "L0_gnn_W_h2h", "L0_ffn_w1", "L0_ffn_b1", "L0_ffn_w2",
        "L0_ffn_b2", "L1_gnn_gamma0", "L1_gnn_beta0", "L1_gnn_gamma1", "L1_ffn_wr", "L1_ffn_br", "L1_ffn_w1",
        "L1_ffn_b1", "L1_ffn_w2", "L1_ffn_b2"]
```

```python
import concourse.bass as bass
from concourse import mybir
from contextlib import ExitStack, contextmanager

F32 = mybir.dt.float32
I32 = mybir.dt.int32
ALU = mybir.AluOpType
ACT = mybir.ActivationFunctionType
AXX = mybir.AxisListType.X

NODES, DIM, EDGES = 6250, 256, 200000
P = 128
TILES = -(-NODES // P)
ROWS = TILES * P
TAIL = NODES - (TILES - 1) * P
BT = 7
BLOCKS = TILES // BT
TOK = BT * P
EP = 125
EC = EDGES // EP
HALF = 8
TURN = 2 * HALF
CHUNKS = -(-((EDGES - TILES) // P + TILES) // TURN) * TURN
TURNS = CHUNKS // TURN
META = 32
META2 = 4
C = 64
EPS = 1e-5
HID = 4 * DIM
MLP_IN = 16
EXPERTS = 8


class Chain:

    def __init__(self, eng, sem, start=0):
        self.eng, self.sem, self.start, self.n = eng, sem, start, 0

    def __call__(self, ins):
        ins.then_inc(self.sem, 1)
        self.n += 1
        self.eng.wait_ge(self.sem, self.start + self.n)
        return ins


def hold(eng):
    eng.nop(nofuse=True)


class Stage:

    def __init__(self, nc, ctx, tag):
        self.nc, self.ctx, self.tag = nc, ctx, tag

    def sb(self, name, shape, dt=F32):
        return self.ctx.enter_context(self.nc.sbuf_tensor(f"{self.tag}_{name}", shape, dt))

    def sem(self, name):
        return self.nc.alloc_semaphore(f"{self.tag}_{name}")

    def sems(self, name, n):
        return [self.sem(f"{name}{i}") for i in range(n)]

    def block(self):
        return self.ctx.enter_context(self.nc.Block())


@contextmanager
def stage(nc, tag):
    with nc.cleanup_on_exit():
        with ExitStack() as ctx:
            yield Stage(nc, ctx, tag)


def bc(ap, shape):
    return ap.to_broadcast(shape)


def tiles_of(dram):
    return dram.rearrange("(t p) d -> p t d", p=P)


class RowNorm:

    def __init__(self, nc, s, K):
        self.nc, self.K = nc, K
        self.stats = s.sb("ln_stats", [P, BT, 6])
        self.mv = s.sb("ln_mv", [P, BT, 2])
        self.sd = s.sb("ln_sd", [P, BT, 1])
        self.rstd = s.sb("ln_rstd", [P, BT, 1])
        self.stats_done = s.sem("ln_stats_done")
        self.mv_done = s.sem("ln_mv_done")
        self.sd_done = s.sem("ln_sd_done")
        self.rstd_done = s.sem("ln_rstd_done")
        self.done = s.sem("ln_done")

    def on_vector(self, dve, i, tile):
        nc = self.nc
        for j in range(BT):
            ins = nc.vector.bn_stats(self.stats[:, j, :], tile(j))
        ins.then_inc(self.stats_done, 1)
        dve.wait_ge(self.stats_done, i + 1)
        hold(dve)
        for j in range(BT):
            ins = nc.vector.bn_aggr(self.mv[:, j, :], self.stats[:, j, :])
        ins.then_inc(self.mv_done, 1)
        dve.wait_ge(self.sd_done, i + 1)
        nc.vector.reciprocal(self.rstd[:, :, :], self.sd[:, :, :]).then_inc(self.rstd_done, 1)
        dve.wait_ge(self.rstd_done, i + 1)
        hold(dve)
        for j in range(BT):
            ins = nc.vector.tensor_scalar(tile(j), tile(j), self.mv[:, j, 0:1], self.rstd[:, j, :],
                                          ALU.subtract, ALU.mult)
        ins.then_inc(self.done, 1)

    def on_scalar(self, act, i):
        act.wait_ge(self.mv_done, i + 1)
        self.nc.scalar.activation(self.sd[:, :, :], self.mv[:, :, 1:2], ACT.Sqrt,
                                  bias=self.K.eps[:, :]).then_inc(self.sd_done, 1)




class Sorter:

    def __init__(self, nc, s, K, side, work):
        self.nc, self.K, self.side, self.work = nc, K, side, work
        self.counts = s.sb(f"{side}_counts", [EP, TILES])
        self.first = s.sb(f"{side}_first", [EP, TILES])
        self.total_i = s.sb(f"{side}_total_i", [TILES, 1], I32)
        self.padded = s.sb(f"{side}_padded", [TILES, 1])
        self.slack = s.sb(f"{side}_slack", [TILES, 1])
        self.slack_wide = s.sb(f"{side}_slack_wide", [TILES, P])
        self.padded_wide = s.sb(f"{side}_padded_wide", [TILES, EP])
        self.end_chunk = s.sb(f"{side}_end_chunk", [TILES, 1])
        self.step, self.counted, self.totalled, self.padded_ready, self.placed, self.ended_ready, self.tables = (
            s.sem(f"{side}_{n}") for n in ("step", "counted", "totalled", "padded_ready", "placed", "ended_ready",
                                           "tables"))
        self.link = None

    def count_on_vector(self, dve, index, local_out=None):
        nc, K, W, side = self.nc, self.K, self.work, self.side
        link = self.link = Chain(dve, self.step)
        link(nc.vector.tensor_scalar(W.key_i[:, :], index[:, :], 7, None, ALU.arith_shift_right))
        link(nc.vector.tensor_copy(W.key[:, :], W.key_i[:, :]))
        if local_out is not None:
            link(nc.vector.tensor_scalar(W.key_i[:, :], index[:, :], P - 1, None, ALU.bitwise_and))
            link(nc.vector.tensor_copy(local_out, W.key_i[:, :]))
        with dve.Fori(0, TILES) as b:
            dve.wait_ge(self.counted, b + 1)
            nc.vector.tensor_scalar(W.mask[:, :], W.key[:, :], K.count[0:EP, bass.ds(b, 1)], None, ALU.is_equal,
                                    ALU.add, accum_out=self.counts[:, bass.ds(b, 1)]).then_inc(self.counted, 1)
        dve.wait_ge(self.totalled, 1)
        link(nc.vector.tensor_scalar(self.total_i[:, :], K.ps[0][0:TILES, 0:1], float(P - 1), None, ALU.add))
        link(nc.vector.tensor_scalar(self.total_i[:, :], self.total_i[:, :], -P, None, ALU.bitwise_and))
        link(nc.vector.tensor_copy(self.padded[:, :], self.total_i[:, :]))
        link(nc.vector.tensor_tensor(self.slack[:, :], self.padded[:, :], K.ps[0][0:TILES, 0:1], ALU.subtract))
        nc.vector.tensor_scalar(self.slack_wide[:, :], K.ones[0:TILES, :], self.slack[:, :], None, ALU.mult)
        nc.vector.tensor_scalar(self.padded_wide[:, :], K.ones[0:TILES, 0:EP], self.padded[:, :], None,
                                ALU.mult).then_inc(self.padded_ready, 1)
        dve.wait_ge(self.placed, 2)
        link(nc.vector.tensor_copy(self.first[:, :], K.ps[1][0:EP, 0:TILES]))
        link(nc.vector.tensor_scalar(self.end_chunk[:, :], K.ps[2][0:TILES, 0:1], 1.0 / P, None, ALU.mult))
        nc.vector.tensor_scalar(W.ended[:, :], K.count[0:TILES, :], self.end_chunk[:, :], None,
                                ALU.is_ge).then_inc(self.ended_ready, 1)
        PART = CHUNKS // 4
        for n in range(4):
            here = slice(n * PART, (n + 1) * PART)
            dve.wait_ge(self.tables, n + 1)
            bucket = nc.vector.tensor_scalar(K.bucket[side][:, here], K.ps[3][0:1, 0:PART], float(TILES - 1), None, ALU.min)
            if side == "dst":
                link(nc.vector.tensor_scalar(K.base[:, here], K.ps[3][:, 0:PART], float(TILES - 1), float(P),
                                             ALU.min, ALU.mult))
                link(nc.vector.scalar_tensor_tensor(W.off[:, here], K.count[0:1, here], float(P), K.ps[4][0:1, 0:PART],
                                                    ALU.mult, ALU.subtract))
                ins = nc.vector.tensor_scalar(K.off[:, here], W.off[:, here], float(EDGES), None, ALU.min)
            else:
                ins = bucket
            link(ins)

    def count_on_tensor(self, pe):
        nc, K, W = self.nc, self.K, self.work
        pe.sem_inc(self.counted, 1)
        pe.wait_ge(self.counted, TILES + 1)
        nc.tensor.matmul(K.ps[0][0:TILES, 0:1], self.counts[:, :], K.ones[0:EP, 0:1], start=True,
                         stop=True).then_inc(self.totalled, 1)
        pe.wait_ge(self.padded_ready, 1)
        nc.tensor.matmul(K.ps[1][0:EP, 0:TILES], K.before[0:EP, 0:EP], self.counts[:, :], start=True, stop=False)
        nc.tensor.matmul(K.ps[1][0:EP, 0:TILES], self.padded_wide[:, :], K.before[0:TILES, 0:TILES], start=False,
                         stop=True).then_inc(self.placed, 1)
        nc.tensor.matmul(K.ps[2][0:TILES, 0:1], K.upto[0:TILES, 0:TILES], self.padded[:, :], start=True,
                         stop=True).then_inc(self.placed, 1)
        pe.wait_ge(self.ended_ready, 1)
        PART = CHUNKS // 4
        per = 3 if self.side == "dst" else 1
        for n in range(4):
            if n:
                pe.wait_ge(self.step, self.steps_before_tables() + n * per)
            here = slice(n * PART, (n + 1) * PART)
            nc.tensor.matmul(K.ps[3][:, 0:PART], K.ones[0:TILES, :], W.ended[:, here], start=True, stop=True)
            nc.tensor.matmul(K.ps[4][:, 0:PART], self.slack_wide[:, :], W.ended[:, here], start=True,
                             stop=True).then_inc(self.tables, 1)

    def steps_before_tables(self):
        return 8 if self.side == "dst" else 10

    def rank_on_vector(self, dve, place_out):
        nc, K, W = self.nc, self.K, self.work
        link = self.link
        link(nc.vector.memset(W.rank[:, :], 0.0))
        base = link.n
        with dve.Fori(0, TILES) as b:
            turn = Chain(dve, self.step, base + b * 4)
            turn(nc.vector.tensor_scalar(W.mask[:, :], W.key[:, :], K.count[0:EP, bass.ds(b, 1)], None, ALU.is_equal))
            turn(nc.vector.tensor_tensor_scan(W.running[:, :], W.mask[:, :], W.mask[:, :], self.first[:, bass.ds(b, 1)],
                                              ALU.add, ALU.max))
            turn(nc.vector.tensor_tensor(W.running[:, :], W.running[:, :], W.mask[:, :], ALU.mult))
            turn(nc.vector.tensor_tensor(W.rank[:, :], W.rank[:, :], W.running[:, :], ALU.add))
        link = self.link = Chain(dve, self.step, base + 4 * TILES)
        link(nc.vector.tensor_scalar(place_out, W.rank[:, :], -1.0, None, ALU.add))

    def interleave_on_vector(self, place):
        nc, W, link = self.nc, self.work, self.link
        r7 = W.mask[:, :].bitcast(I32)
        link(nc.vector.tensor_scalar(W.key_i[:, :], place, P - 1, 3, ALU.bitwise_and, ALU.logical_shift_left))
        link(nc.vector.tensor_scalar(r7, place, 7, HALF - 1, ALU.arith_shift_right, ALU.bitwise_and))
        link(nc.vector.tensor_tensor(W.key_i[:, :], W.key_i[:, :], r7, ALU.bitwise_or))
        link(nc.vector.tensor_scalar(place, place, -P * HALF, None, ALU.bitwise_and))
        link(nc.vector.tensor_tensor(place, place, W.key_i[:, :], ALU.bitwise_or))


class SortWork:

    def __init__(self, s):
        self.key_i = s.sb("key_i", [EP, EC], I32)
        self.key, self.mask = (s.sb(n, [EP, EC]) for n in ("key", "mask"))
        running, rank = (s.sb(n, [EP, CHUNKS]) for n in ("running", "rank"))
        self.running, self.rank = running[:, 0:EC], rank[:, 0:EC]
        self.ended, self.off = rank[0:TILES, :], running[0:1, :]


class Project:
    NT = 4

    def __init__(self, nc, s, K, h, weights, bias, outs):
        self.nc, self.K, self.h, self.weights, self.bias, self.outs = nc, K, h, weights, bias, outs
        self.w = s.sb("pr_w", [P, 2, 2 * DIM])
        self.b = s.sb("pr_b", [P, 2 * DIM]) if bias is not None else None
        self.hb = s.sb("pr_hb", [P, BT, DIM])
        self.hT = s.sb("pr_hT", [P, 2 * BT, P])
        self.f = s.sb("pr_f", [P, BT, 2 * DIM])
        (self.w_loaded, self.h_loaded, self.transposed, self.hT_ready, self.product, self.f_ready, self.f_written) = (
            s.sem(n) for n in ("w_loaded", "h_loaded", "transposed", "hT_ready", "product", "f_ready", "f_written"))
        self.n_w = 2 + (2 if bias is not None else 0)

    def on_tensor(self, pe):
        nc, K, NT = self.nc, self.K, self.NT
        pe.wait_ge(self.w_loaded, 16 * self.n_w)
        with pe.Fori(0, BLOCKS) as i:
            pe.wait_ge(self.h_loaded, 16 * i + 16)
            for n in range(NT):
                pe.wait_ge(self.hT_ready, i * NT + 1)
                for m in range(4 * n, min(4 * n + 4, 2 * BT)):
                    ins = nc.tensor.transpose(K.ps[n][:, (m % 4) * P:(m % 4 + 1) * P],
                                              self.hb[:, m // 2, (m % 2) * P:(m % 2 + 1) * P], K.ident[:, :])
                ins.then_inc(self.transposed, 1)
            pe.wait_ge(self.hT_ready, i * NT + NT + 1)
            for j in range(BT):
                pe.wait_ge(self.f_ready, i * BT + j + 1)
                for k in range(2):
                    ins = nc.tensor.matmul(K.ps[4 + j % 4][:, :], self.hT[:, 2 * j + k, :], self.w[:, k, :],
                                           start=(k == 0), stop=(k == 1))
                ins.then_inc(self.product, 1)

    def on_scalar(self, act, h_written=None):
        nc, K, NT = self.nc, self.K, self.NT
        for n in range(2):
            act.dma_start(self.w[:, :, n * DIM:(n + 1) * DIM],
                          self.weights[n].rearrange("(k p) n -> p k n", p=P)).then_inc(self.w_loaded, 16)
        if self.bias is not None:
            for n, row in enumerate(self.bias):
                act.dma_start(self.b[:, n * DIM:(n + 1) * DIM], row_bc(row)).then_inc(self.w_loaded, 16)
        if h_written is not None:
            act.wait_ge(h_written, 16)

        def load(i):
            act.dma_start(self.hb[:, :, :], tiles_of(self.h)[:, bass.ds(i * BT, BT), :]).then_inc(self.h_loaded, 16)

        act.sem_inc(self.hT_ready, 1)
        load(0)

        def turn(i, last=False):
            act.wait_ge(self.f_ready, i * BT + 4)
            hold(act)
            for n in range(NT):
                act.wait_ge(self.transposed, i * NT + n + 1)
                width = min(4, 2 * BT - 4 * n)
                nc.scalar.activation(self.hT[:, 4 * n:4 * n + width, :],
                                     K.ps[n][:, 0:width * P].rearrange("p (m q) -> p m q", q=P),
                                     ACT.Copy).then_inc(self.hT_ready, 1)
            if not last:
                load(i + 1)
            act.wait_ge(self.f_ready, (i + 1) * BT + 4)
            for n in range(2):
                act.dma_start(tiles_of(self.outs[n])[:, bass.ds(i * BT, BT), :],
                              self.f[:, :, n * DIM:(n + 1) * DIM]).then_inc(self.f_written, 16)

        with act.Fori(0, BLOCKS - 1) as i:
            turn(i)
        turn(BLOCKS - 1, last=True)
        act.wait_ge(self.f_written, 32 * BLOCKS)

    def on_vector(self, dve):
        nc, K = self.nc, self.K
        dve.wait_ge(self.w_loaded, 16 * self.n_w)
        dve.sem_inc(self.f_ready, 4)

        def copy_out(i, first=False):
            if not first:
                dve.wait_ge(self.f_written, 32 * i)
                hold(dve)
            for j in range(BT):
                dve.wait_ge(self.product, i * BT + j + 1)
                if self.bias is None:
                    ins = nc.vector.tensor_copy(self.f[:, j, :], K.ps[4 + j % 4][:, :])
                else:
                    ins = nc.vector.tensor_tensor(self.f[:, j, :], K.ps[4 + j % 4][:, :], self.b[:, :], ALU.add)
                ins.then_inc(self.f_ready, 1)

        copy_out(0, first=True)
        with dve.Fori(1, BLOCKS) as i:
            copy_out(i)


def project_stage(nc, K, tag, h, weights, bias, outs):
    with stage(nc, tag) as s:
        project = Project(nc, s, K, h, weights, bias, outs)
        block = s.block()

        @block.tensor
        def _(pe):
            project.on_tensor(pe)

        @block.scalar
        def _(act):
            project.on_scalar(act)

        @block.vector
        def _(dve):
            project.on_vector(dve)


COPY_COLS = 32


def front_stage(nc, K, A, x0, h, feats, rows_dst, rows_src):
    with stage(nc, "front") as s:
        W = SortWork(s)
        src_i = s.sb("src_i", [EP, EC], I32)
        dst_i = s.sb("dst_i", [EP, EC], I32)
        record = s.sb("record", [EP, EC, META2])
        slot = s.sb("slot", [EP, 2, HALF, META2])
        broken = s.sb("broken", [EP, 1])
        zero = s.sb("zero", [P, CHUNKS * META2 // 16])
        y = s.sb("y", [P, TILES, DIM])
        sq = s.sb("sq", [P, 2, DIM])
        mean, gain, gam, bet = (s.sb(n, [P, DIM]) for n in ("mean", "gain", "gam", "bet"))
        rows = s.sb("rows", [EP, 2, COPY_COLS, META])
        to_src = Sorter(nc, s, K, "src", W)
        to_dst = Sorter(nc, s, K, "dst", W)
        norm = RowNorm(nc, s, K)
        project = Project(nc, s, K, h, (A["L0_gnn_W_in"], A["L0_gnn_W_out"]), (A["L0_gnn_b_in"], A["L0_gnn_b_out"]), feats)
        (consts, edges_loaded, next_loaded, zeroed, zeros_written, recorded, x_cleared, x_loaded, sums, centred, squared,
         squares, used, h_ready, h_written, col_sd, step, checked, broken_ready, flag_done, x0_written, rows_filled) = (
            s.sem(n) for n in ("consts", "edges_loaded", "next_loaded", "zeroed", "zeros_written", "recorded", "x_cleared",
                               "x_loaded", "sums", "centred", "squared", "squares", "used", "h_ready", "h_written",
                               "col_sd", "step", "checked", "broken_ready", "flag_done", "x0_written", "rows_filled"))
        slot_loaded, sent = s.sems("slot_loaded", 2), s.sems("sent", 2)
        rows_loaded, rows_written = s.sems("rows_loaded", 2), s.sems("rows_written", 2)
        block = s.block()
        TURNS_E = EC // TURN
        SENT = 16 * HALF
        COPIES = EC // (2 * COPY_COLS)
        following = W.running[:, :].bitcast(I32)

        @block.sync
        def _(sp):
            sp.dma_start(src_i[:, :], A["src"].rearrange("(p c) -> p c", p=EP)).then_inc(edges_loaded, 16)
            sp.dma_start(W.rank, A["edge_weight_n2"].rearrange("(p c) -> p c", p=EP)).then_inc(edges_loaded, 16)
            sp.dma_start(dst_i[:, :], A["dst"].rearrange("(p c) -> p c", p=EP)).then_inc(edges_loaded, 16)
            cut = (EP - 1) * EC
            sp.dma_start(following[0:EP - 1, :], A["dst"][1:cut + 1].rearrange("(p c) -> p c", p=EP - 1)).then_inc(next_loaded, 16)
            sp.dma_start(following[EP - 1:EP, 0:EC - 1], A["dst"][cut + 1:EDGES].rearrange("(p c) -> p c", p=1)).then_inc(next_loaded, 16)
            sp.dma_start(following[EP - 1:EP, EC - 1:EC], A["dst"][EDGES - 1:EDGES].rearrange("(p c) -> p c", p=1)).then_inc(next_loaded, 16)
            sp.dma_start(x0[0:NODES, :], A["x"][:, :]).then_inc(x0_written, 16)
            sp.wait_ge(zeroed, 1)
            src_view = rows_src.rearrange("(p r) w -> p (r w)", p=P)
            wide = CHUNKS * META2 // 16
            for n in range(16):
                sp.dma_start(src_view[:, n * wide:(n + 1) * wide], zero[:, :]).then_inc(zeros_written, 16)
            sp.dma_start(rows_dst[EDGES:EDGES + P, :], zero[:, 0:META]).then_inc(zeros_written, 16)
            sp.dma_start(x0[NODES:ROWS, :], zero[0:ROWS - NODES, 0:DIM]).then_inc(x0_written, 16)

            def load(i, first=False):
                for k in range(2):
                    if not first:
                        sp.wait_ge(sent[k], i * SENT)
                    sp.dma_start(slot[:, k, :, :], record[:, bass.ds(i * TURN + HALF * k, HALF), :]).then_inc(slot_loaded[k], 16)

            sp.wait_ge(recorded, 1)
            load(0, first=True)
            with sp.Fori(1, TURNS_E) as i:
                load(i)
            sp.wait_ge(x0_written, 32)

        @block.gpsimd
        def _(pool):
            link = Chain(pool, consts)
            nc.gpsimd.memset(K.ones[:, :], 1.0)
            nc.gpsimd.memset(K.ident[:, :], 0.0)
            nc.gpsimd.iota(K.count[:, :], pattern=[[1, CHUNKS]], base=0, channel_multiplier=0,
                           allow_small_or_imprecise_dtypes=True)
            link(nc.gpsimd.memset(K.before[:, :], 1.0))
            nc.gpsimd.affine_select(out=K.ident[:, :], in_=K.ident[:, :], compare_op=ALU.not_equal, fill=1.0,
                                    base=0, pattern=[[-1, P]], channel_multiplier=1)
            link(nc.gpsimd.affine_select(out=K.upto[:, :], in_=K.before[:, :], compare_op=ALU.is_ge, fill=0.0,
                                         base=0, pattern=[[1, P]], channel_multiplier=-1))
            link(nc.gpsimd.affine_select(out=K.before[:, :], in_=K.before[:, :], compare_op=ALU.is_gt, fill=0.0,
                                         base=0, pattern=[[1, P]], channel_multiplier=-1))
            pool.wait_ge(zeros_written, 16 * 17)
            with pool.Fori(0, TURNS_E) as i:
                for k in range(2):
                    pool.wait_ge(slot_loaded[k], 16 * i + 16)
                    hold(pool)
                    for c in range(HALF):
                        nc.gpsimd.indirect_dma_start(
                            out=rows_src[:, :],
                            out_offset=bass.IndirectOffsetOnAxis(ap=slot[:, k, c, 3:4].bitcast(I32), axis=0),
                            in_=slot[:, k, c, :], in_offset=None).then_inc(sent[k], 16)
            for k in range(2):
                pool.wait_ge(sent[k], TURNS_E * SENT)

        @block.vector
        def _(dve):
            nc.vector.memset(zero[:, :], 0.0).then_inc(zeroed, 1)
            nc.vector.memset(K.eps[:, :], EPS)
            nc.vector.memset(y[:, TILES - 1, :], 0.0).then_inc(x_cleared, 1)
            TT = nc.vector.tensor_tensor
            link = Chain(dve, step)
            dve.wait_ge(edges_loaded, 48)
            dve.wait_ge(next_loaded, 48)
            link(nc.vector.tensor_copy(record[:, :, 2], W.rank))
            link(TT(W.mask[:, :], dst_i[:, :], following, ALU.is_gt))
            nc.vector.tensor_reduce(broken[:, :], W.mask[:, :], AXX, ALU.add).then_inc(broken_ready, 1)
            dve.wait_ge(broken_ready, 1)
            dve.wait_ge(consts, 3)
            to_src.count_on_vector(dve, src_i, record[:, :, 1])
            assert to_src.link.n == 10 + 4, to_src.link.n
            place = record[:, :, 3].bitcast(I32)
            to_src.rank_on_vector(dve, place)
            to_src.interleave_on_vector(place)
            nc.vector.tensor_copy(record[:, :, 0].bitcast(I32), dst_i[:, :]).then_inc(recorded, 1)
            dve.wait_ge(recorded, 1)
            to_dst.count_on_vector(dve, dst_i)
            assert to_dst.link.n == 8 + 12, to_dst.link.n
            dve.wait_ge(flag_done, 1)
            link(nc.vector.tensor_copy(K.unsorted[:, :], K.ps[5][0:1, 0:1]))

            dve.wait_ge(x_loaded, 64)
            with dve.Fori(0, BLOCKS) as i:
                norm.on_vector(dve, i, lambda j: y[:, i * BT + j, :])
            dve.wait_ge(sums, 1)
            link(nc.vector.tensor_scalar(mean[:, :], K.ps[0][:, 0:DIM], 1.0 / NODES, None, ALU.mult))
            TT(y[:, :, :], y[:, :, :], bc(mean[:, :].unsqueeze(1), [P, TILES, DIM]), ALU.subtract).then_inc(centred, 1)
            dve.wait_ge(col_sd, 1)
            link(nc.vector.reciprocal(gain[:, :], gain[:, :]))
            link(TT(gain[:, :], gain[:, :], gam[:, :], ALU.mult))
            link(TT(y[:, :, :], y[:, :, :], bc(gain[:, :].unsqueeze(1), [P, TILES, DIM]), ALU.mult))
            TT(y[:, :, :], y[:, :, :], bc(bet[:, :].unsqueeze(1), [P, TILES, DIM]), ALU.add).then_inc(h_ready, 1)
            project.on_vector(dve)

            with dve.Fori(0, COPIES) as i:
                for k in range(2):
                    here = bass.ds((2 * i + k) * COPY_COLS, COPY_COLS)
                    dve.wait_ge(rows_loaded[k], 16 * i + 16)
                    nc.vector.tensor_copy(rows[:, k, :, 0].bitcast(I32), src_i[:, here])
                    nc.vector.tensor_copy(rows[:, k, :, 1], dst_i[:, here]).then_inc(rows_filled, 1)

        @block.scalar
        def _(act):
            full = (TILES - 1) * P
            act.wait_ge(x_cleared, 1)
            act.dma_start(y[:, 0:TILES - 1, :], tiles_of(A["x"][0:full, :])).then_inc(x_loaded, 16)
            act.dma_start(y[0:TAIL, TILES - 1, :], A["x"][full:NODES, :]).then_inc(x_loaded, 16)
            act.dma_start(gam[:, :], row_bc(A["L0_gnn_gamma"])).then_inc(x_loaded, 16)
            act.dma_start(bet[:, :], row_bc(A["L0_gnn_beta"])).then_inc(x_loaded, 16)
            with act.Fori(0, BLOCKS) as i:
                norm.on_scalar(act, i)
            act.wait_ge(centred, 1)
            with act.Fori(0, (TILES - 1) // 2) as i:
                for k in range(2):
                    act.wait_ge(used, 2 * i + k + 1)
                    nc.scalar.activation(sq[:, k, :], y[:, 2 * i + k, :], ACT.Square).then_inc(squared, 1)
            act.wait_ge(used, TILES)
            nc.scalar.activation(sq[:, 0, :], y[:, TILES - 1, :], ACT.Square).then_inc(squared, 1)
            act.wait_ge(squares, 1)
            nc.scalar.activation(gain[:, :], K.ps[1][:, 0:DIM], ACT.Sqrt, bias=K.eps[:, :],
                                 scale=1.0 / NODES).then_inc(col_sd, 1)
            act.wait_ge(h_ready, 1)
            act.dma_start(tiles_of(h), y[:, :, :]).then_inc(h_written, 16)
            project.on_scalar(act, h_written)

            edge_view = A["edge_rows"].rearrange("(p c) w -> p c w", p=EP)
            table_view = rows_dst[0:EDGES, :].rearrange("(p c) w -> p c w", p=EP)

            def load(i):
                for k in range(2):
                    if not isinstance(i, int):
                        act.wait_ge(rows_written[k], 16 * i)
                    act.dma_start(rows[:, k, :, :],
                                  edge_view[:, bass.ds((2 * i + k) * COPY_COLS, COPY_COLS), :]).then_inc(rows_loaded[k], 16)

            def store(i):
                for k in range(2):
                    act.wait_ge(rows_filled, 2 * i + k + 1)
                    act.dma_start(table_view[:, bass.ds((2 * i + k) * COPY_COLS, COPY_COLS), :],
                                  rows[:, k, :, :]).then_inc(rows_written[k], 16)

            load(0)
            store(0)
            with act.Fori(1, COPIES) as i:
                load(i)
                store(i)
            for k in range(2):
                act.wait_ge(rows_written[k], 16 * COPIES)

        @block.tensor
        def _(pe):
            to_src.count_on_tensor(pe)
            to_dst.count_on_tensor(pe)
            nc.tensor.matmul(K.ps[5][:, 0:1], K.ones[0:EP, :], broken[:, :], start=True, stop=True).then_inc(flag_done, 1)
            pe.wait_ge(norm.done, BLOCKS)
            nc.tensor.matmul(K.ps[0][:, 0:DIM], K.ones[:, :], y[:, 0, :], start=True, stop=False)
            with pe.Fori(1, TILES - 1) as t:
                nc.tensor.matmul(K.ps[0][:, 0:DIM], K.ones[:, :], y[:, t, :], start=False, stop=False)
            nc.tensor.matmul(K.ps[0][:, 0:DIM], K.ones[0:TAIL, :], y[0:TAIL, TILES - 1, :], start=False,
                             stop=True).then_inc(sums, 1)
            pe.sem_inc(used, 2)
            for t in range(2):
                pe.wait_ge(squared, t + 1)
                nc.tensor.matmul(K.ps[1][:, 0:DIM], K.ones[:, :], sq[:, t, :], start=(t == 0), stop=False).then_inc(used, 1)
            with pe.Fori(1, (TILES - 1) // 2) as i:
                for k in range(2):
                    pe.wait_ge(squared, 2 * i + k + 1)
                    nc.tensor.matmul(K.ps[1][:, 0:DIM], K.ones[:, :], sq[:, k, :], start=False, stop=False).then_inc(used, 1)
            pe.wait_ge(squared, TILES)
            nc.tensor.matmul(K.ps[1][:, 0:DIM], K.ones[0:TAIL, :], sq[0:TAIL, 0, :], start=False,
                             stop=True).then_inc(squares, 1)
            project.on_tensor(pe)


def unsorted_stages(nc, K, A, rows_dst):
    with stage(nc, "order") as s:
        W = SortWork(s)
        dst_i = s.sb("dst_i", [EP, EC], I32)
        place = s.sb("place_all", [EP, EC], I32)
        src_i = s.sb("src_i", [EP, EC], I32)
        zero = s.sb("zero", [P, CHUNKS * META // 16])
        row = s.sb("row", [EP, 2, HALF, META])
        at = s.sb("at", [EP, 2, HALF], I32)
        sorter = Sorter(nc, s, K, "dst", W)
        edges_loaded, zeroed, zeros_written, filled, ranked = (
            s.sem(n) for n in ("edges_loaded", "zeroed", "zeros_written", "filled", "ranked"))
        loaded, sent = s.sems("loaded", 2), s.sems("sent", 2)
        TURNS_E = EC // TURN
        SENT = 16 * HALF
        any_broken = nc.values_load(K.unsorted[0:1, 0:1], min_val=0, max_val=EDGES)
        with nc.If(any_broken > 0):
            nc.all_engine_barrier()
            blocks = ExitStack()
            block = blocks.enter_context(nc.Block())

            @block.sync
            def _(sp):
                sp.dma_start(dst_i[:, :], A["dst"].rearrange("(p c) -> p c", p=EP)).then_inc(edges_loaded, 16)
                sp.dma_start(src_i[:, :], A["src"].rearrange("(p c) -> p c", p=EP)).then_inc(edges_loaded, 16)
                sp.wait_ge(zeroed, 1)
                view = rows_dst.rearrange("(p r) w -> p (r w)", p=P)
                wide = CHUNKS * META // 16
                for n in range(16):
                    sp.dma_start(view[:, n * wide:(n + 1) * wide], zero[:, :]).then_inc(zeros_written, 16)
                edge_view = A["edge_rows"].rearrange("(p c) w -> p c w", p=EP)

                def load(i, first=False):
                    for k in range(2):
                        if not first:
                            sp.wait_ge(sent[k], i * SENT)
                        sp.dma_start(row[:, k, :, :], edge_view[:, bass.ds(i * TURN + HALF * k, HALF), :]).then_inc(loaded[k], 16)

                load(0, first=True)
                with sp.Fori(1, TURNS_E) as i:
                    load(i)

            @block.vector
            def _(dve):
                nc.vector.memset(zero[:, :], 0.0).then_inc(zeroed, 1)
                dve.wait_ge(edges_loaded, 32)
                sorter.count_on_vector(dve, dst_i)
                sorter.rank_on_vector(dve, place[:, :])
                sorter.link(nc.vector.tensor_scalar(K.off[:, :], K.count[0:1, :], float(P), None, ALU.mult))

                def fill(i, first=False):
                    for k in range(2):
                        if not first:
                            dve.wait_ge(sent[k], i * SENT)
                        dve.wait_ge(loaded[k], 16 * i + 16)
                        here = bass.ds(i * TURN + HALF * k, HALF)
                        nc.vector.tensor_copy(row[:, k, :, 0].bitcast(I32), src_i[:, here])
                        nc.vector.tensor_copy(row[:, k, :, 1], dst_i[:, here])
                        nc.vector.tensor_copy(at[:, k, :], place[:, here]).then_inc(filled, 1)

                fill(0, first=True)
                with dve.Fori(1, TURNS_E) as i:
                    fill(i)

            @block.tensor
            def _(pe):
                sorter.count_on_tensor(pe)

            @block.gpsimd
            def _(pool):
                pool.wait_ge(zeros_written, 16 * 16)
                with pool.Fori(0, TURNS_E) as i:
                    for k in range(2):
                        pool.wait_ge(filled, 2 * i + k + 1)
                        hold(pool)
                        for c in range(HALF):
                            nc.gpsimd.indirect_dma_start(
                                out=rows_dst[:, :], out_offset=bass.IndirectOffsetOnAxis(ap=at[:, k, c:c + 1], axis=0),
                                in_=row[:, k, c, :], in_offset=None).then_inc(sent[k], 16)
                for k in range(2):
                    pool.wait_ge(sent[k], TURNS_E * SENT)
            blocks.close()


def load_rows(nc, sp, K, rows_dst, row, h, i, loaded):
    for c in range(HALF):
        at = sp.value_load(K.off[0:1, bass.ds(i * TURN + HALF * h + c, 1)], min_val=0, max_val=(CHUNKS - 1) * P)
        sp.dma_start(row[:, h, c, :], rows_dst[bass.ds(at, P), :]).then_inc(loaded, 16)


def gather_stage(nc, K, side, rows, words, table, out):
    dst = side == "dst"
    with stage(nc, f"gather_{side}") as s:
        acc = s.sb("acc", [P, TILES, DIM])
        row = s.sb("row", [P, 2, HALF, words])
        local = s.sb("local", [P, 2, HALF])
        got = s.sb("got", [P, TURN, DIM])
        pick = s.sb("pick", [P, TURN, P])
        loaded = s.sems("loaded", 2)
        gathered = s.sems("gathered", TURN)
        used = s.sems("used", 2)
        localised, picked, added, cleared, written = (
            s.sem(n) for n in ("localised", "picked", "added", "cleared", "written"))
        block = s.block()
        LOAD = 16 * (HALF if dst else 1)

        @block.sync
        def _(sp):
            with sp.Fori(0, TURNS) as i:
                for h in range(2):
                    sp.wait_ge(used[h], HALF * i + 1)
                    if dst:
                        load_rows(nc, sp, K, rows, row, h, i, loaded[h])
                    else:
                        view = rows.rearrange("(g p c) w -> g p c w", p=P, c=HALF)
                        sp.dma_start(row[:, h, :, :], view[i * 2 + h, :, :, :]).then_inc(loaded[h], 16)
            sp.wait_ge(added, CHUNKS + 8)
            sp.dma_start(tiles_of(out), acc[:, :, :]).then_inc(written, 16)
            sp.wait_ge(written, 16)

        @block.gpsimd
        def _(pool):
            with pool.Fori(0, TURNS) as i:
                for h in range(2):
                    pool.wait_ge(used[h], HALF * i + 1)
                    hold(pool)
                    pool.wait_ge(loaded[h], LOAD * i + LOAD)
                    hold(pool)
                    for c in range(HALF):
                        nc.gpsimd.indirect_dma_start(
                            out=got[:, HALF * h + c, :], out_offset=None, in_=table[:, :],
                            in_offset=bass.IndirectOffsetOnAxis(ap=row[:, h, c, 0:1].bitcast(I32), axis=0)
                        ).then_inc(gathered[HALF * h + c], 16)

        @block.vector
        def _(dve):
            nc.vector.memset(acc[:, :, :], 0.0).then_inc(cleared, 1)
            dve.wait_ge(cleared, 1)
            dve.sem_inc(added, 8)
            dve.sem_inc(used[0], 1)
            dve.sem_inc(used[1], 1)
            with dve.Fori(0, TURNS) as i:
                for h in range(2):
                    dve.wait_ge(used[h], HALF * i + 1)
                    dve.wait_ge(loaded[h], LOAD * i + LOAD)
                    if dst:
                        nc.vector.tensor_tensor(local[:, h, :], row[:, h, :, 1], K.base[:, bass.ds(i * TURN + HALF * h, HALF)],
                                                ALU.subtract).then_inc(localised, 1)
                        dve.wait_ge(localised, 2 * i + h + 1)
                    for c in range(HALF):
                        node = local[:, h, c:c + 1] if dst else row[:, h, c, 1:2]
                        nc.vector.tensor_scalar(pick[:, HALF * h + c, :], K.count[:, 0:P], node,
                                                row[:, h, c, 2:3], ALU.is_equal, ALU.mult).then_inc(picked, 1)
                    for c in range(HALF):
                        n = HALF * h + c
                        b = nc.vector.value_load(K.bucket[side][0:1, bass.ds(i * TURN + n, 1)], min_val=0,
                                                 max_val=TILES - 1)
                        dve.wait_ge(used[h], HALF * i + c + 2)
                        dve.wait_ge(added, i * TURN + n + 8)
                        nc.vector.tensor_tensor(acc[:, b, :], acc[:, b, :], K.ps[c][:, 0:DIM], ALU.add).then_inc(added, 1)

        @block.tensor
        def _(pe):
            with pe.Fori(0, TURNS) as i:
                for h in range(2):
                    for c in range(HALF):
                        n = HALF * h + c
                        pe.wait_ge(gathered[n], 16 * i + 16)
                        pe.wait_ge(picked, i * TURN + n + 1)
                        pe.wait_ge(added, i * TURN + n + 1)
                        nc.tensor.matmul(K.ps[c][:, 0:DIM], pick[:, n, :], got[:, n, :], start=True,
                                         stop=True).then_inc(used[h], 1)


def load_block(sp, views, tiles, i, loaded):
    for view, tile in zip(views, tiles):
        sp.dma_start(tile[:, :, :], tiles_of(view)[:, bass.ds(i * BT, BT), :]).then_inc(loaded, 16)


def row_bc(vec):
    return vec.rearrange("(a d) -> a d", a=1).broadcast_to([P, vec.shape[0]])


def update_stage(nc, K, x, h, a_in, a_out, w_x2i, b_x2i, w_h2h, x1_out, y1_out):
    with stage(nc, "upd") as s:
        KT = 6
        w = s.sb("w", [P, KT, 2 * DIM])
        b = s.sb("b", [P, 2 * DIM])
        srcs = [s.sb(n, [P, BT, DIM]) for n in ("a_in", "a_out", "h")]
        xb = s.sb("x", [P, BT, DIM])
        aT = s.sb("aT", [P, KT * BT, P])
        gate = s.sb("gate", [P, BT, 2 * DIM])
        y = s.sb("y", [P, BT, DIM])
        norm = RowNorm(nc, s, K)
        w_loaded, loaded, transposed, aT_ready, product, biased, gates, step, x1_ready, written = (
            s.sem(n) for n in ("w_loaded", "loaded", "transposed", "aT_ready", "product", "biased", "gates", "step",
                               "x1_ready", "written"))
        block = s.block()
        n_banks = -(-KT * BT // 4)

        @block.sync
        def _(sp):
            sp.dma_start(w[:, 0:4, :], w_x2i.rearrange("(k p) n -> p k n", p=P)).then_inc(w_loaded, 16)
            sp.dma_start(w[:, 4:6, :], w_h2h.rearrange("(k p) n -> p k n", p=P)).then_inc(w_loaded, 16)
            sp.dma_start(b[:, :], row_bc(b_x2i)).then_inc(w_loaded, 16)

            def turn(i, first=False):
                if not first:
                    sp.wait_ge(written, 32 * i)
                load_block(sp, (a_in, a_out, h, x), (*srcs, xb), i, loaded)
                sp.wait_ge(norm.done, i + 1)
                sp.dma_start(tiles_of(x1_out)[:, bass.ds(i * BT, BT), :], xb[:, :, :]).then_inc(written, 16)
                sp.dma_start(tiles_of(y1_out)[:, bass.ds(i * BT, BT), :], y[:, :, :]).then_inc(written, 16)

            turn(0, first=True)
            with sp.Fori(1, BLOCKS) as i:
                turn(i)
            sp.wait_ge(written, 32 * BLOCKS)

        @block.tensor
        def _(pe):
            pe.wait_ge(w_loaded, 48)
            with pe.Fori(0, BLOCKS) as i:
                pe.wait_ge(loaded, 64 * i + 64)
                for n in range(n_banks):
                    pe.wait_ge(aT_ready, i * n_banks + n + 1)
                    for m in range(4 * n, min(4 * n + 4, KT * BT)):
                        j, k = divmod(m, KT)
                        ins = nc.tensor.transpose(K.ps[n % 4][:, (m % 4) * P:(m % 4 + 1) * P],
                                                  srcs[k // 2][:, j, (k % 2) * P:(k % 2 + 1) * P], K.ident[:, :])
                    ins.then_inc(transposed, 1)
                pe.wait_ge(aT_ready, (i + 1) * n_banks + 4)
                for j in range(BT):
                    pe.wait_ge(biased, i * BT + j + 1)
                    for k in range(KT):
                        ins = nc.tensor.matmul(K.ps[4 + j % 2][:, :], aT[:, KT * j + k, :], w[:, k, :],
                                               start=(k == 0), stop=(k == KT - 1))
                    ins.then_inc(product, 1)

        @block.scalar
        def _(act):
            act.sem_inc(aT_ready, 4)
            with act.Fori(0, BLOCKS) as i:
                act.wait_ge(biased, i * BT + 2)
                hold(act)
                for n in range(n_banks):
                    act.wait_ge(transposed, i * n_banks + n + 1)
                    width = min(4, KT * BT - 4 * n)
                    nc.scalar.activation(aT[:, 4 * n:4 * n + width, :],
                                         K.ps[n % 4][:, 0:width * P].rearrange("p (m q) -> p m q", q=P),
                                         ACT.Copy).then_inc(aT_ready, 1)
                act.wait_ge(biased, (i + 1) * BT + 2)
                nc.scalar.activation(gate[:, :, 0:DIM], gate[:, :, 0:DIM], ACT.Sigmoid).then_inc(gates, 1)
                nc.scalar.activation(gate[:, :, DIM:], gate[:, :, DIM:], ACT.Tanh).then_inc(gates, 1)
                norm.on_scalar(act, i)

        @block.vector
        def _(dve):
            dve.wait_ge(w_loaded, 48)
            dve.sem_inc(biased, 2)

            def turn(i, first=False):
                for j in range(BT):
                    dve.wait_ge(product, i * BT + j + 1)
                    nc.vector.tensor_tensor(gate[:, j, :], K.ps[4 + j % 2][:, :], b[:, :], ALU.add).then_inc(biased, 1)
                link = Chain(dve, step, i * 5)
                if not first:
                    dve.wait_ge(written, 32 * i)
                dve.wait_ge(loaded, 64 * i + 64)
                dve.wait_ge(gates, 2 * i + 2)
                link(nc.vector.tensor_tensor(y[:, :, :], srcs[2][:, :, :], gate[:, :, DIM:], ALU.subtract))
                link(nc.vector.tensor_tensor(y[:, :, :], y[:, :, :], gate[:, :, 0:DIM], ALU.mult))
                link(nc.vector.tensor_tensor(y[:, :, :], y[:, :, :], gate[:, :, DIM:], ALU.add))
                link(nc.vector.tensor_tensor(xb[:, :, :], xb[:, :, :], y[:, :, :], ALU.add))
                link(nc.vector.tensor_copy(y[:, :, :], xb[:, :, :]))
                norm.on_vector(dve, i, lambda j: y[:, j, :])

            turn(0, first=True)
            with dve.Fori(1, BLOCKS) as i:
                turn(i)


def moe_stage(nc, K, y1, x1, router_T, w1, b1, w2, b2, x2_out, y2_out):
    E8 = EXPERTS
    NB = 4
    WIDE = TOK // 2
    with stage(nc, "moe") as s:
        w1s = s.sb("w1", [P, E8, 2, DIM])
        w2s = s.sb("w2", [P, E8, 2, DIM])
        b1s = s.sb("b1", [P, E8, 2])
        b2s = s.sb("b2", [E8, DIM])
        rT = s.sb("rT", [P, 2, E8])
        yb = s.sb("yb", [P, BT, DIM])
        xb = s.sb("xb", [P, BT, DIM])
        yT = s.sb("yT", [P, 2, TOK])
        hT = s.sb("hT", [P, 2, 2, TOK])
        acc = s.sb("acc", [P, BT, DIM])
        lg, pr, left, pick, comb = (s.sb(n, [P, BT, E8]) for n in ("lg", "pr", "left", "pick", "comb"))
        rev = s.sb("rev", [P, BT, E8])
        m1, m2, tot, idx = (s.sb(n, [P, BT, 1]) for n in ("m1", "m2", "tot", "idx"))
        combT = s.sb("combT", [E8, BT, P])
        norm = RowNorm(nc, s, K)
        (w_loaded, loaded, transposed, yT_ready, logits, shifted, expd, step, comb_ready, combT_done, combT_ready,
         hidden, hT_ready, expert, added, written) = (
            s.sem(n) for n in ("w_loaded", "loaded", "transposed", "yT_ready", "logits", "shifted", "expd", "step",
                               "comb_ready", "combT_done", "combT_ready", "hidden", "hT_ready", "expert", "added",
                               "written"))
        block = s.block()
        HPE = 4
        ADDS = BT * E8 + BT

        @block.sync
        def _(sp):
            sp.dma_start(w1s[:, :, :, :], w1.rearrange("e (k p) n -> p e k n", p=P)).then_inc(w_loaded, 16)
            sp.dma_start(w2s[:, :, :, :], w2.rearrange("e (k p) n -> p e k n", p=P)).then_inc(w_loaded, 16)
            with nc.allow_non_contiguous_dma("the first biases, once"):
                sp.dma_start(b1s[:, :, :], b1.rearrange("e (k p) -> p e k", p=P)).then_inc(w_loaded, 16)
            sp.dma_start(b2s[:, :], b2[:, :]).then_inc(w_loaded, 16)
            sp.dma_start(rT[:, :, :], router_T.rearrange("(k p) e -> p k e", p=P)).then_inc(w_loaded, 16)

            def turn(i, first=False):
                if not first:
                    sp.wait_ge(written, 32 * i)
                load_block(sp, (y1, x1), (yb, xb), i, loaded)
                sp.wait_ge(norm.done, i + 1)
                sp.dma_start(tiles_of(x2_out)[:, bass.ds(i * BT, BT), :], xb[:, :, :]).then_inc(written, 16)
                sp.dma_start(tiles_of(y2_out)[:, bass.ds(i * BT, BT), :], acc[:, :, :]).then_inc(written, 16)

            turn(0, first=True)
            with sp.Fori(1, BLOCKS) as i:
                turn(i)
            sp.wait_ge(written, 32 * BLOCKS)

        @block.tensor
        def _(pe):
            pe.wait_ge(w_loaded, 80)
            with pe.Fori(0, BLOCKS) as i:
                pe.wait_ge(loaded, 32 * i + 32)
                for n in range(NB):
                    pe.wait_ge(yT_ready, i * NB + n + 1)
                    for m in range(4 * n, min(4 * n + 4, 2 * BT)):
                        k, j = divmod(m, BT)
                        ins = nc.tensor.transpose(K.ps[n][:, (m % 4) * P:(m % 4 + 1) * P],
                                                  yb[:, j, k * P:(k + 1) * P], K.ident[:, :])
                    ins.then_inc(transposed, 1)
                pe.wait_ge(yT_ready, (i + 1) * NB + 4)
                pe.wait_ge(shifted, i + 1)
                for j in range(BT):
                    for k in range(2):
                        ins = nc.tensor.matmul(K.ps[4][:, j * E8:(j + 1) * E8], yT[:, k, j * P:(j + 1) * P],
                                               rT[:, k, :], start=(k == 0), stop=(k == 1))
                ins.then_inc(logits, 1)

                def hidden_of(e):
                    for m in range(2):
                        for q in range(2):
                            n = (2 * m + q)
                            pe.wait_ge(hT_ready, (i * E8 + e) * HPE + n + 1)
                            for k in range(2):
                                ins = nc.tensor.matmul(K.ps[n][:, 0:WIDE], w1s[:, e, k, m * P:(m + 1) * P],
                                                       yT[:, k, q * WIDE:(q + 1) * WIDE], start=(k == 0), stop=(k == 1))
                            ins.then_inc(hidden, 1)

                def output_of(e):
                    pe.wait_ge(hT_ready, (i * E8 + e + 1) * HPE + 4)
                    for j in range(BT):
                        n = e * BT + j
                        pe.wait_ge(added, i * ADDS + n + 1)
                        for k in range(2):
                            ins = nc.tensor.matmul(K.ps[5 + n % 3][:, 0:DIM], hT[:, e % 2, k, j * P:(j + 1) * P],
                                                   w2s[:, e, k, :], start=(k == 0), stop=(k == 1))
                        ins.then_inc(expert, 1)

                hidden_of(0)
                for e in range(E8):
                    if e + 1 < E8:
                        hidden_of(e + 1)
                    output_of(e)
                pe.wait_ge(comb_ready, i + 1)
                for j in range(BT):
                    ins = nc.tensor.transpose(K.ps[j // 4][0:E8, (j % 4) * P:(j % 4 + 1) * P],
                                              comb[:, j, :], K.ident[:, :])
                ins.then_inc(combT_done, 1)
                pe.wait_ge(combT_ready, i + 1)
                for j in range(BT):
                    n = E8 * BT + j
                    pe.wait_ge(added, i * ADDS + n + 1)
                    nc.tensor.matmul(K.ps[5 + n % 3][:, 0:DIM], combT[:, j, :], b2s[:, :], start=True,
                                     stop=True).then_inc(expert, 1)

        @block.scalar
        def _(act):
            act.sem_inc(yT_ready, 4)
            act.sem_inc(hT_ready, 4)
            with act.Fori(0, BLOCKS) as i:
                act.wait_ge(added, i * ADDS + 3)
                hold(act)
                for n in range(NB):
                    act.wait_ge(transposed, i * NB + n + 1)
                    width = min(4, 2 * BT - 4 * n)
                    nc.scalar.activation(yT[:, :, :].rearrange("p k t -> p (k t)")[:, 4 * n * P:(4 * n + width) * P],
                                         K.ps[n][:, 0:width * P], ACT.Copy).then_inc(yT_ready, 1)
                act.wait_ge(shifted, i + 2)
                nc.scalar.activation(pr[:, :, :], lg[:, :, :], ACT.Exp).then_inc(expd, 1)
                for e in range(E8):
                    if e >= 2:
                        act.wait_ge(expert, i * ADDS + (e - 1) * BT)
                        hold(act)
                    for m in range(2):
                        for q in range(2):
                            n = 2 * m + q
                            act.wait_ge(hidden, (i * E8 + e) * HPE + n + 1)
                            nc.scalar.activation(hT[:, e % 2, m, q * WIDE:(q + 1) * WIDE], K.ps[n][:, 0:WIDE], ACT.Gelu,
                                                 bias=b1s[:, e, m:m + 1]).then_inc(hT_ready, 1)
                act.wait_ge(combT_done, i + 1)
                nc.scalar.activation(combT[:, 0:4, :], K.ps[0][0:E8, :].rearrange("p (j t) -> p j t", t=P), ACT.Copy)
                nc.scalar.activation(combT[:, 4:BT, :], K.ps[1][0:E8, 0:(BT - 4) * P].rearrange("p (j t) -> p j t", t=P),
                                     ACT.Copy).then_inc(combT_ready, 1)
                norm.on_scalar(act, i)

        @block.vector
        def _(dve):
            dve.wait_ge(w_loaded, 80)
            dve.sem_inc(shifted, 1)
            dve.sem_inc(added, 3)
            nc.vector.tensor_scalar(rev[:, :, :], bc(K.count[:, 0:E8].unsqueeze(1), [P, BT, E8]), -1.0, float(E8),
                                    ALU.mult, ALU.add).then_inc(step, 1)
            dve.wait_ge(step, 1)

            def turn(i, first=False):
                link = Chain(dve, step, i * STEPS + 1)
                wide = lambda t: bc(t[:, :, :], [P, BT, E8])
                TT, TR = nc.vector.tensor_tensor, nc.vector.tensor_reduce
                dve.wait_ge(logits, i + 1)
                link(nc.vector.tensor_copy(lg[:, :, :], K.ps[4][:, 0:BT * E8].rearrange("p (j e) -> p j e", e=E8)))
                link(TR(m1[:, :, :], lg[:, :, :], AXX, ALU.max))
                TT(lg[:, :, :], lg[:, :, :], wide(m1), ALU.subtract).then_inc(shifted, 1)
                dve.wait_ge(expd, i + 1)
                link(TR(tot[:, :, :], pr[:, :, :], AXX, ALU.add))
                link(nc.vector.reciprocal(tot[:, :, :], tot[:, :, :]))
                link(TT(pr[:, :, :], pr[:, :, :], wide(tot), ALU.mult))

                def choose(source, best, mask_out):
                    link(TR(best[:, :, :], source[:, :, :], AXX, ALU.max))
                    link(TT(mask_out[:, :, :], source[:, :, :], wide(best), ALU.is_equal))
                    link(TT(mask_out[:, :, :], mask_out[:, :, :], rev[:, :, :], ALU.mult))
                    link(TR(idx[:, :, :], mask_out[:, :, :], AXX, ALU.max))
                    link(TT(mask_out[:, :, :], rev[:, :, :], wide(idx), ALU.is_equal))

                choose(pr, m1, comb)
                link(nc.vector.scalar_tensor_tensor(left[:, :, :], comb[:, :, :], -2.0, pr[:, :, :], ALU.mult, ALU.add))
                choose(left, m2, pick)
                link(TT(comb[:, :, :], comb[:, :, :], pick[:, :, :], ALU.add))
                link(TT(comb[:, :, :], comb[:, :, :], pr[:, :, :], ALU.mult))
                link(TT(tot[:, :, :], m1[:, :, :], m2[:, :, :], ALU.add))
                link(nc.vector.tensor_scalar(tot[:, :, :], tot[:, :, :], 1e-12, None, ALU.max))
                link(nc.vector.reciprocal(tot[:, :, :], tot[:, :, :]))
                TT(comb[:, :, :], comb[:, :, :], wide(tot), ALU.mult).then_inc(comb_ready, 1)
                dve.wait_ge(comb_ready, i + 1)
                if not first:
                    dve.wait_ge(written, 32 * i)
                dve.wait_ge(loaded, 32 * i + 32)
                for e in range(E8):
                    for j in range(BT):
                        n = e * BT + j
                        dve.wait_ge(expert, i * ADDS + n + 1)
                        if e:
                            dve.wait_ge(added, i * ADDS + n - BT + 4)
                        base = yb[:, j, :] if e == 0 else acc[:, j, :]
                        nc.vector.scalar_tensor_tensor(acc[:, j, :], K.ps[5 + n % 3][:, 0:DIM], comb[:, j, e:e + 1], base,
                                                       ALU.mult, ALU.add).then_inc(added, 1)
                for j in range(BT):
                    n = E8 * BT + j
                    dve.wait_ge(expert, i * ADDS + n + 1)
                    dve.wait_ge(added, i * ADDS + n - BT + 4)
                    TT(acc[:, j, :], acc[:, j, :], K.ps[5 + n % 3][:, 0:DIM], ALU.add).then_inc(added, 1)
                dve.wait_ge(added, (i + 1) * ADDS + 3)
                link(TT(xb[:, :, :], xb[:, :, :], acc[:, :, :], ALU.add))
                link(nc.vector.tensor_copy(acc[:, :, :], xb[:, :, :]))
                steps.append(link.n)
                norm.on_vector(dve, i, lambda j: acc[:, j, :])

            steps = []
            STEPS = 23
            turn(0, first=True)
            assert steps[0] == STEPS, steps
            with dve.Fori(1, BLOCKS) as i:
                turn(i)
def message_stage(nc, K, rows, table, m1, m2, m3, m4, out):
    with stage(nc, "msg") as s:
        PAIRS = HALF // 2
        acc = s.sb("acc", [P, TILES, DIM])
        row = s.sb("row", [P, 2, HALF, META])
        local = s.sb("local", [P, 2, HALF])
        got = s.sb("got", [P, TURN, DIM])
        m1s = s.sb("m1", [P, PAIRS, P])
        m2s, m3s = s.sb("m2", [P, P]), s.sb("m3", [P, P])
        m4s = s.sb("m4", [P, DIM])
        attr = s.sb("attr", [P, P])
        attrT = s.sb("attrT", [P, P])
        hid = s.sb("hid", [P, 2, 512])
        hid3 = s.sb("hid3", [P, 2, 512])
        same = s.sb("same", [P, 2, 2, P])
        wsh = s.sb("wsh", [P, 2, 2, 2, C])
        xsh = s.sb("xsh", [P, 2, 2, 3, C])
        mess = s.sb("mess", [P, 2, 2, 4, C])
        u = s.sb("u", [P, 2, C])
        dot = s.sb("dot", [P, 2, C])
        dotw = s.sb("dotw", [P, 2, C])
        loaded = s.sems("loaded", 2)
        gathered = s.sems("gathered", TURN)
        used = s.sems("used", 2)
        (w_loaded, scaled, attr_ready, attr_turned, attrT_ready, layer, act_done, weights, w_scaled, x_scaled, matched,
         step, joined, added, cleared, written, localised) = (
            s.sem(n) for n in ("w_loaded", "scaled", "attr_ready", "attr_turned", "attrT_ready", "layer", "act_done",
                               "weights", "w_scaled", "x_scaled", "matched", "step", "joined", "added", "cleared",
                               "written", "localised"))
        block = s.block()
        MLP_BANK = K.ps[0]
        weight_part = [K.psum[:, 1 + 2 * n:3 + 2 * n, 0:DIM] for n in range(2)]
        sum_part = [K.ps[5 + n].rearrange("p (c d) -> p c d", c=2) for n in range(2)]
        LOAD = 16 * HALF

        @block.sync
        def _(sp):
            sp.dma_start(m1s[:, :, :], m1[:, :, :]).then_inc(w_loaded, 16)
            for tile, array in ((m2s, m2), (m3s, m3), (m4s, m4)):
                sp.dma_start(tile[:, :], array[:, :]).then_inc(w_loaded, 16)
            with sp.Fori(0, TURNS) as i:
                for h in range(2):
                    sp.wait_ge(used[h], PAIRS * i + 2)
                    load_rows(nc, sp, K, rows, row, h, i, loaded[h])
            sp.wait_ge(added, CHUNKS + 4)
            sp.dma_start(tiles_of(out), acc[:, :, :]).then_inc(written, 16)
            sp.wait_ge(written, 16)

        @block.gpsimd
        def _(pool):
            with pool.Fori(0, TURNS) as i:
                for h in range(2):
                    pool.wait_ge(used[h], PAIRS * i + 2)
                    hold(pool)
                    pool.wait_ge(loaded[h], LOAD * i + LOAD)
                    hold(pool)
                    for c in range(HALF):
                        nc.gpsimd.indirect_dma_start(
                            out=got[:, HALF * h + c, :], out_offset=None, in_=table[:, :],
                            in_offset=bass.IndirectOffsetOnAxis(ap=row[:, h, c, 0:1].bitcast(I32), axis=0)
                        ).then_inc(gathered[HALF * h + c], 16)

        def following(i, h):
            return (i, 1) if h == 0 else (i + 1, 0)

        def next_pair(i, h, p):
            return (i, h, p + 1) if p + 1 < PAIRS else (*following(i, h), 0)

        def number(i, h, p):
            return (i * 2 + h) * PAIRS + p

        def turns(eng, turn):
            with eng.Fori(0, TURNS - 1) as i:
                turn(i)
            turn(TURNS - 1, last=True)

        @block.vector
        def _(dve):
            nc.vector.memset(acc[:, :, :], 0.0).then_inc(cleared, 1)
            dve.wait_ge(w_loaded, 64)
            nc.vector.tensor_scalar(m4s[:, 3 * C:], m4s[:, 3 * C:], float(3.0 ** -0.5), None, ALU.mult).then_inc(scaled, 1)
            dve.wait_ge(cleared, 1)
            for sem in (joined, *used):
                dve.sem_inc(sem, 2)
            dve.sem_inc(added, 4)
            TT, STT = nc.vector.tensor_tensor, nc.vector.scalar_tensor_tensor
            STEPS = 12

            def prepare(i, h):
                if not (isinstance(i, int) and i == 0 and h == 0):
                    dve.wait_ge(attr_turned, 2 * i + h)
                dve.wait_ge(loaded[h], LOAD * i + LOAD)
                nc.vector.tensor_copy(attr[:, :].rearrange("p (c f) -> p c f", f=MLP_IN),
                                      row[:, h, :, 8:8 + MLP_IN]).then_inc(attr_ready, 1)
                TT(local[:, h, :], row[:, h, :, 1], K.base[:, bass.ds(i * TURN + HALF * h, HALF)],
                   ALU.subtract).then_inc(localised, 1)

            def match(i, h, p):
                dve.wait_ge(localised, 2 * i + h + 1)
                if p >= 2:
                    dve.wait_ge(used[h], PAIRS * i + p + 1)
                elif h == 1:
                    dve.wait_ge(used[0], PAIRS * i + PAIRS + p + 1)
                else:
                    dve.wait_ge(used[1], PAIRS * i + p + 1)
                TT(same[:, p % 2, :, :], bc(K.count[:, 0:P].unsqueeze(1), [P, 2, P]),
                   bc(local[:, h, 2 * p:2 * p + 2].unsqueeze(2), [P, 2, P]), ALU.is_equal).then_inc(matched, 1)

            def join(i, h, p):
                g, slot, c = number(i, h, p), p % 2, 2 * p
                w, x = weight_part[slot], got[:, HALF * h + c:HALF * h + c + 2, :]
                m = mess[:, slot, :, :, :]
                base = g * STEPS
                dve.wait_ge(x_scaled, g + 1)
                if not (isinstance(i, int) and i == 0 and h == 0 and p == 0):
                    dve.wait_ge(step, base)
                TT(dot[:, :, :], xsh[:, slot, :, 0, :], xsh[:, slot, :, 1, :], ALU.add).then_inc(step, 1)
                dve.wait_ge(w_scaled, g + 1)
                TT(u[:, :, :], w[:, :, C:2 * C], x[:, :, 0:C], ALU.mult).then_inc(step, 1)
                TT(m[:, :, 1:4, :], bc(wsh[:, slot, :, 1, :].unsqueeze(2), [P, 2, 3, C]),
                   x[:, :, C:].rearrange("p c (a d) -> p c a d", d=C), ALU.mult).then_inc(step, 1)
                dve.wait_ge(step, base + 1)
                TT(dot[:, :, :], dot[:, :, :], xsh[:, slot, :, 2, :], ALU.add).then_inc(step, 1)
                TT(m[:, :, 0, :], wsh[:, slot, :, 0, :], x[:, :, 0:C], ALU.mult).then_inc(step, 1)
                dve.wait_ge(step, base + 3)
                for n in range(2):
                    for a in range(3):
                        STT(m[:, n, 1 + a, :], u[:, n, :], row[:, h, c + n, 4 + a:5 + a], m[:, n, 1 + a, :],
                            ALU.mult, ALU.add).then_inc(step, 1)
                    if n == 0:
                        dve.wait_ge(step, base + 5)
                        TT(dotw[:, :, :], w[:, :, 3 * C:], dot[:, :, :], ALU.mult).then_inc(step, 1)
                dve.wait_ge(step, base + 9)
                TT(m[:, :, 0, :], m[:, :, 0, :], dotw[:, :, :], ALU.add).then_inc(joined, 1)

            def add(i, h, p):
                for n in range(2):
                    b = nc.vector.value_load(K.bucket["dst"][0:1, bass.ds(i * TURN + HALF * h + 2 * p + n, 1)],
                                             min_val=0, max_val=TILES - 1)
                    dve.wait_ge(used[h], PAIRS * i + p + 3)
                    dve.wait_ge(added, 2 * number(i, h, p) + n + 4)
                    TT(acc[:, b, :], acc[:, b, :], sum_part[p % 2][:, n, :], ALU.add).then_inc(added, 1)

            def turn(i, last=False):
                for h in range(2):
                    for p in range(PAIRS):
                        end = last and h == 1 and p == PAIRS - 1
                        if not end:
                            match(*next_pair(i, h, p))
                        join(i, h, p)
                        if p:
                            add(i, h, p - 1)
                        if p == 0 and not (last and h == 1):
                            prepare(*following(i, h))
                    add(i, h, PAIRS - 1)

            prepare(0, 0)
            match(0, 0, 0)
            turns(dve, turn)

        @block.scalar
        def _(act):
            def mlp(i, h, part):
                half = i * 2 + h
                if part == 0:
                    act.wait_ge(attr_turned, half + 1)
                    nc.scalar.activation(attrT[:, :], MLP_BANK[:, 0:P], ACT.Copy).then_inc(attrT_ready, 1)
                else:
                    act.wait_ge(layer, half * 3 + part)
                    into = hid[:, part - 1, :] if part < 3 else hid3[:, h, :]
                    nc.scalar.activation(into, MLP_BANK[:, :], ACT.Silu).then_inc(act_done, 1)

            def scale_weights(i, h, p):
                act.wait_ge(weights, number(i, h, p) + 1)
                act.wait_ge(joined, number(i, h, p) + 1)
                for n in range(2):
                    w = weight_part[p % 2][:, n, :].rearrange("p (k d) -> p k d", d=C)
                    ins = nc.scalar.activation(wsh[:, p % 2, n, :, :], w[:, 0:3:2, :], ACT.Copy,
                                               scale=row[:, h, 2 * p + n, 3:4])
                ins.then_inc(w_scaled, 1)

            def scale_vectors(i, h, p):
                for n in range(2):
                    c = 2 * p + n
                    act.wait_ge(gathered[HALF * h + c], 16 * i + 16)
                    for a in range(3):
                        ins = nc.scalar.activation(xsh[:, p % 2, n, a, :], got[:, HALF * h + c, C * (a + 1):C * (a + 2)],
                                                   ACT.Copy, scale=row[:, h, c, 4 + a:5 + a])
                ins.then_inc(x_scaled, 1)

            def turn(i, last=False):
                for h in range(2):
                    for p in range(PAIRS):
                        more, end = not (last and h == 1), last and h == 1 and p == PAIRS - 1
                        if not end:
                            scale_weights(*next_pair(i, h, p))
                        if p == 1 and more:
                            mlp(*following(i, h), 1)
                        if not end:
                            scale_vectors(*next_pair(i, h, p))
                        if p < 3 and more:
                            mlp(*following(i, h), (0, 2, 3)[p])

            for part in range(4):
                mlp(0, 0, part)
            scale_weights(0, 0, 0)
            scale_vectors(0, 0, 0)
            turns(act, turn)

        @block.tensor
        def _(pe):
            pe.wait_ge(w_loaded, 64)
            pe.wait_ge(scaled, 1)

            def mlp(i, h, part):
                half = i * 2 + h
                if part == 0:
                    pe.wait_ge(attr_ready, half + 1)
                    nc.tensor.transpose(MLP_BANK[:, 0:P], attr[:, :], K.ident[:, :]).then_inc(attr_turned, 1)
                elif part == 1:
                    pe.wait_ge(attrT_ready, half + 1)
                    for j in range(PAIRS):
                        ins = nc.tensor.matmul(MLP_BANK[:, j * P:(j + 1) * P], m1s[:, j, :], attrT[:, :],
                                               start=True, stop=True)
                    ins.then_inc(layer, 1)
                else:
                    pe.wait_ge(act_done, half * 3 + part - 1)
                    nc.tensor.matmul(MLP_BANK[:, :], (m2s, m3s)[part - 2][:, :], hid[:, part - 2, :], start=True,
                                     stop=True).then_inc(layer, 1)

            def weigh(i, h, p):
                if p == 0:
                    pe.wait_ge(act_done, (i * 2 + h) * 3 + 3)
                pe.wait_ge(joined, number(i, h, p) + 1)
                for n in range(2):
                    ins = nc.tensor.matmul(weight_part[p % 2][:, n, :], hid3[C * n:C * n + C, h, p * P:(p + 1) * P],
                                           m4s[C * n:C * n + C, :], start=True, stop=True)
                ins.then_inc(weights, 1)

            def turn(i, last=False):
                for h in range(2):
                    for p in range(PAIRS):
                        more, end = not (last and h == 1), last and h == 1 and p == PAIRS - 1
                        if not end:
                            weigh(*next_pair(i, h, p))
                        if p == 1 and more:
                            mlp(*following(i, h), 1)
                        g = number(i, h, p)
                        pe.wait_ge(matched, g + 1)
                        pe.wait_ge(joined, g + 3)
                        pe.wait_ge(added, 2 * g + 2)
                        for n in range(2):
                            ins = nc.tensor.matmul(sum_part[p % 2][:, n, :], same[:, p % 2, n, :],
                                                   mess[:, p % 2, n, :, :].rearrange("p k d -> p (k d)"), start=True,
                                                   stop=True)
                        ins.then_inc(used[h], 1)
                        if p < 3 and more:
                            mlp(*following(i, h), (0, 2, 3)[p])

            for part in range(4):
                mlp(0, 0, part)
            weigh(0, 0, 0)
            turns(pe, turn)


def mix_stage(nc, K, msg, sc, w_lin, w_b, poly0, poly1, o_out):
    with stage(nc, "mix") as s:
        wl, wb = s.sb("wl", [P, 2, P]), s.sb("wb", [P, 2, P])
        c0, c1 = s.sb("c0", [P, 5, C]), s.sb("c1", [P, 4, C])
        mb, scb = s.sb("mb", [P, BT, DIM]), s.sb("scb", [P, BT, DIM])
        T = s.sb("T", [P, 2 * BT, P])
        a = s.sb("a", [P, BT, DIM])
        bb = s.sb("bb", [P, BT, DIM])
        a2, vv, t0, t1 = (s.sb(n, [P, BT, C]) for n in ("a2", "vv", "t0", "t1"))
        w_loaded, loaded, turned, T_ready, product, copied, poly, step, written, o_ready, b_ready = (
            s.sem(n) for n in ("w_loaded", "loaded", "turned", "T_ready", "product", "copied", "poly", "step",
                               "written", "o_ready", "b_ready"))
        block = s.block()
        NB = 4

        @block.sync
        def _(sp):
            sp.dma_start(wl[:, :, :], w_lin[:, :, :]).then_inc(w_loaded, 16)
            sp.dma_start(wb[:, :, :], w_b[:, :, :]).then_inc(w_loaded, 16)
            for tile, array, n in ((c0, poly0, 5), (c1, poly1, 4)):
                sp.dma_start(tile[:, :, :], array.rearrange("(a n) d -> a n d", a=1).broadcast_to([P, n, C])).then_inc(w_loaded, 16)

            def turn(i, first=False):
                if not first:
                    sp.wait_ge(written, 16 * i)
                load_block(sp, (msg, sc), (mb, scb), i, loaded)
                sp.wait_ge(o_ready, i + 1)
                sp.dma_start(tiles_of(o_out)[:, bass.ds(i * BT, BT), :], scb[:, :, :]).then_inc(written, 16)

            turn(0, first=True)
            with sp.Fori(1, BLOCKS) as i:
                turn(i)
            sp.wait_ge(written, 16 * BLOCKS)

        @block.tensor
        def _(pe):
            pe.wait_ge(w_loaded, 64)
            with pe.Fori(0, BLOCKS) as i:
                for r, (src, w) in enumerate(((mb, wl), (bb, wb))):
                    if r == 0:
                        pe.wait_ge(loaded, 32 * i + 32)
                    else:
                        pe.wait_ge(b_ready, i + 1)
                    for n in range(NB):
                        pe.wait_ge(T_ready, (2 * i + r) * NB + n + 1)
                        for m in range(4 * n, min(4 * n + 4, 2 * BT)):
                            ins = nc.tensor.transpose(K.ps[n][:, (m % 4) * P:(m % 4 + 1) * P],
                                                      src[:, m // 2, (m % 2) * P:(m % 2 + 1) * P], K.ident[:, :])
                        ins.then_inc(turned, 1)
                    pe.wait_ge(T_ready, (2 * i + r + 1) * NB + 4)
                    for j in range(BT):
                        pe.wait_ge(copied, (2 * i + r) * BT + j + 1)
                        for k in range(2):
                            ins = nc.tensor.matmul(K.ps[4 + j % 4][:, k * P:(k + 1) * P], T[:, 2 * j + k, :], w[:, k, :],
                                                   start=True, stop=True)
                        ins.then_inc(product, 1)

        @block.scalar
        def _(act):
            act.sem_inc(T_ready, 4)
            with act.Fori(0, BLOCKS) as i:
                for r in range(2):
                    act.wait_ge(copied, (2 * i + r) * BT + 4)
                    hold(act)
                    for n in range(NB):
                        act.wait_ge(turned, (2 * i + r) * NB + n + 1)
                        width = min(4, 2 * BT - 4 * n)
                        nc.scalar.activation(T[:, 4 * n:4 * n + width, :],
                                             K.ps[n][:, 0:width * P].rearrange("p (m q) -> p m q", q=P),
                                             ACT.Copy).then_inc(T_ready, 1)

        @block.vector
        def _(dve):
            dve.wait_ge(w_loaded, 64)
            dve.sem_inc(copied, 4)
            STEPS = 21
            with dve.Fori(0, BLOCKS) as i:
                link = Chain(dve, step, i * STEPS)
                TT = nc.vector.tensor_tensor
                wide = lambda t: bc(t.unsqueeze(1), [P, BT, C])
                for j in range(BT):
                    dve.wait_ge(product, 2 * i * BT + j + 1)
                    nc.vector.tensor_copy(a[:, j, :], K.ps[4 + j % 4][:, 0:DIM]).then_inc(copied, 1)
                dve.wait_ge(copied, 2 * i * BT + BT + 4)
                A0 = a[:, :, 0:C]
                A1 = a[:, :, C:].rearrange("p j (x d) -> p j x d", d=C)
                B0, tt = bb[:, :, 0:C], t1[:, :, :]
                link(TT(bb[:, :, C:], a[:, :, C:], a[:, :, C:], ALU.mult))
                link(TT(vv[:, :, :], bb[:, :, C:2 * C], bb[:, :, 2 * C:3 * C], ALU.add))
                link(TT(vv[:, :, :], vv[:, :, :], bb[:, :, 3 * C:], ALU.add))
                link(TT(a2[:, :, :], A0, A0, ALU.mult))
                link(TT(t0[:, :, :], A0, wide(c1[:, 1, :]), ALU.mult))
                link(TT(t0[:, :, :], t0[:, :, :], wide(c1[:, 0, :]), ALU.add))
                link(TT(tt, a2[:, :, :], wide(c1[:, 2, :]), ALU.mult))
                link(TT(t0[:, :, :], t0[:, :, :], tt, ALU.add))
                link(TT(tt, vv[:, :, :], wide(c1[:, 3, :]), ALU.mult))
                link(TT(t0[:, :, :], t0[:, :, :], tt, ALU.add))
                for x in range(3):
                    ins = TT(bb[:, :, C + C * x:2 * C + C * x], a[:, :, C + C * x:2 * C + C * x], t0[:, :, :], ALU.mult)
                link(ins)
                link(TT(B0, A0, wide(c0[:, 0, :]), ALU.mult))
                link(TT(tt, a2[:, :, :], wide(c0[:, 1, :]), ALU.mult))
                link(TT(B0, B0, tt, ALU.add))
                link(TT(tt, vv[:, :, :], wide(c0[:, 2, :]), ALU.mult))
                link(TT(B0, B0, tt, ALU.add))
                link(TT(a2[:, :, :], a2[:, :, :], A0, ALU.mult))
                link(TT(tt, a2[:, :, :], wide(c0[:, 3, :]), ALU.mult))
                link(TT(B0, B0, tt, ALU.add))
                link(TT(vv[:, :, :], vv[:, :, :], A0, ALU.mult))
                link(TT(tt, vv[:, :, :], wide(c0[:, 4, :]), ALU.mult))
                TT(B0, B0, tt, ALU.add).then_inc(b_ready, 1)
                for j in range(BT):
                    dve.wait_ge(product, (2 * i + 1) * BT + j + 1)
                    TT(scb[:, j, :], scb[:, j, :], K.ps[4 + j % 4][:, 0:DIM], ALU.add).then_inc(copied, 1)
                dve.wait_ge(copied, (2 * i + 2) * BT + 4)
                nc.vector.tensor_copy(t0[:, 0:1, 0:1], t0[:, 0:1, 0:1]).then_inc(o_ready, 1)
                assert link.n == STEPS, link.n


def finish_stage(nc, K, o, x2, gamma0, beta0, gamma1, r3_out, y3_out):
    with stage(nc, "fin") as s:
        ob = s.sb("ob", [P, TILES, DIM])
        xb = s.sb("xb", [P, BT, DIM])
        yb = s.sb("yb", [P, BT, DIM])
        sq = s.sb("sq", [P, 2, DIM])
        gain = s.sb("gain", [P, DIM])
        shift = s.sb("shift", [P, C])
        g0 = s.sb("g0", [P, 2 * C])
        b0 = s.sb("b0", [P, C])
        norm = RowNorm(nc, s, K)
        loaded, x_loaded, sums, centred, squared, squares, used, col_sd, step, r_ready, written = (
            s.sem(n) for n in ("loaded", "x_loaded", "sums", "centred", "squared", "squares", "used", "col_sd", "step",
                               "r_ready", "written"))
        block = s.block()

        @block.sync
        def _(sp):
            sp.dma_start(ob[:, :, :], tiles_of(o)).then_inc(loaded, 16)
            sp.dma_start(g0[:, 0:C], row_bc(gamma0)).then_inc(loaded, 16)
            sp.dma_start(g0[:, C:], row_bc(gamma1)).then_inc(loaded, 16)
            sp.dma_start(b0[:, :], row_bc(beta0)).then_inc(loaded, 16)

            def turn(i, first=False):
                if not first:
                    sp.wait_ge(written, 32 * i)
                load_block(sp, (x2,), (xb,), i, x_loaded)
                sp.wait_ge(r_ready, i + 1)
                sp.dma_start(tiles_of(r3_out)[:, bass.ds(i * BT, BT), :], xb[:, :, :]).then_inc(written, 16)
                sp.dma_start(tiles_of(y3_out)[:, bass.ds(i * BT, BT), :], yb[:, :, :]).then_inc(written, 16)

            turn(0, first=True)
            with sp.Fori(1, BLOCKS) as i:
                turn(i)
            sp.wait_ge(written, 32 * BLOCKS)

        @block.tensor
        def _(pe):
            pe.wait_ge(loaded, 64)
            nc.tensor.matmul(K.ps[0][:, 0:C], K.ones[:, :], ob[:, 0, 0:C], start=True, stop=False)
            with pe.Fori(1, TILES - 1) as t:
                nc.tensor.matmul(K.ps[0][:, 0:C], K.ones[:, :], ob[:, t, 0:C], start=False, stop=False)
            nc.tensor.matmul(K.ps[0][:, 0:C], K.ones[0:TAIL, :], ob[0:TAIL, TILES - 1, 0:C], start=False,
                             stop=True).then_inc(sums, 1)
            pe.sem_inc(used, 2)
            for t in range(2):
                pe.wait_ge(squared, t + 1)
                nc.tensor.matmul(K.ps[1][:, 0:DIM], K.ones[:, :], sq[:, t, :], start=(t == 0), stop=False).then_inc(used, 1)
            with pe.Fori(1, (TILES - 1) // 2) as i:
                for k in range(2):
                    pe.wait_ge(squared, 2 * i + k + 1)
                    nc.tensor.matmul(K.ps[1][:, 0:DIM], K.ones[:, :], sq[:, k, :], start=False, stop=False).then_inc(used, 1)
            pe.wait_ge(squared, TILES)
            nc.tensor.matmul(K.ps[1][:, 0:DIM], K.ones[0:TAIL, :], sq[0:TAIL, 0, :], start=False,
                             stop=True).then_inc(squares, 1)

        @block.scalar
        def _(act):
            act.wait_ge(centred, 1)
            with act.Fori(0, (TILES - 1) // 2) as i:
                for k in range(2):
                    act.wait_ge(used, 2 * i + k + 1)
                    nc.scalar.activation(sq[:, k, :], ob[:, 2 * i + k, :], ACT.Square).then_inc(squared, 1)
            act.wait_ge(used, TILES)
            nc.scalar.activation(sq[:, 0, :], ob[:, TILES - 1, :], ACT.Square).then_inc(squared, 1)
            act.wait_ge(step, 4)
            nc.scalar.activation(gain[:, 0:C], gain[:, 0:C], ACT.Sqrt, bias=K.eps[:, :], scale=1.0 / NODES)
            nc.scalar.activation(gain[:, C:2 * C], gain[:, C:2 * C], ACT.Sqrt, bias=K.eps[:, :],
                                 scale=1.0 / (3 * NODES)).then_inc(col_sd, 1)
            with act.Fori(0, BLOCKS) as i:
                norm.on_scalar(act, i)

        @block.vector
        def _(dve):
            link = Chain(dve, step)
            TT = nc.vector.tensor_tensor
            dve.wait_ge(sums, 1)
            link(nc.vector.tensor_scalar(shift[:, :], K.ps[0][:, 0:C], 1.0 / NODES, None, ALU.mult))
            TT(ob[:, :, 0:C], ob[:, :, 0:C], bc(shift[:, :].unsqueeze(1), [P, TILES, C]), ALU.subtract).then_inc(centred, 1)
            dve.wait_ge(squares, 1)
            link(nc.vector.tensor_copy(gain[:, :], K.ps[1][:, 0:DIM]))
            link(TT(gain[:, C:2 * C], gain[:, C:2 * C], gain[:, 2 * C:3 * C], ALU.add))
            link(TT(gain[:, C:2 * C], gain[:, C:2 * C], gain[:, 3 * C:], ALU.add))
            dve.wait_ge(col_sd, 1)
            link(nc.vector.reciprocal(gain[:, 0:2 * C], gain[:, 0:2 * C]))
            link(TT(gain[:, 0:2 * C], gain[:, 0:2 * C], g0[:, :], ALU.mult))
            dve.wait_ge(centred, 1)
            for x in range(4):
                ins = TT(ob[:, :, x * C:(x + 1) * C], ob[:, :, x * C:(x + 1) * C],
                         bc(gain[:, min(x, 1) * C:(min(x, 1) + 1) * C].unsqueeze(1), [P, TILES, C]), ALU.mult)
            link(ins)
            link(TT(ob[:, :, 0:C], ob[:, :, 0:C], bc(b0[:, :].unsqueeze(1), [P, TILES, C]), ALU.add))
            base = link.n

            def turn(i, first=False):
                here = Chain(dve, step, i * 2 + base)
                dve.wait_ge(x_loaded, 16 * i + 16)
                TT(xb[:, :, 0:C], xb[:, :, 0:C], ob[:, bass.ds(i * BT, BT), 0:C], ALU.add)
                for x in range(3):
                    into = xb[:, :, C:].rearrange("p j (d x) -> p j d x", x=3)[:, :, :, x]
                    ins = TT(into, into, ob[:, bass.ds(i * BT, BT), (x + 1) * C:(x + 2) * C], ALU.add)
                here(ins)
                here(nc.vector.tensor_copy(yb[:, :, :], xb[:, :, :]))
                norm.on_vector(dve, i, lambda j: yb[:, j, :])
                dve.wait_ge(norm.done, i + 1)
                TT(xb[:, :, :], xb[:, :, :], yb[:, :, :], ALU.add).then_inc(r_ready, 1)

            with dve.Fori(0, BLOCKS) as i:
                turn(i)


def ffn_stage(nc, K, y3, wr, br, w1, b1, w2, b2, z_out, score):
    M = HID // P
    WIDE = TOK // 2
    NB = 4
    with stage(nc, "ffn") as s:
        w1s = s.sb("w1", [P, 2, HID])
        w2s = s.sb("w2", [P, M, DIM])
        b1s = s.sb("b1", [P, M])
        b2s, wrs = s.sb("b2", [P, DIM]), s.sb("wr", [P, DIM])
        brs = s.sb("br", [P, 1])
        yb = s.sb("yb", [P, BT, DIM])
        scr = s.sb("scr", [P, BT, DIM])
        yT = s.sb("yT", [P, 2, TOK])
        hT = s.sb("hT", [P, M, TOK])
        z = s.sb("z", [P, BT, DIM])
        (w_loaded, loaded, turned, yT_ready, hidden, hT_ready, output, used, weighed, scored, step, written) = (
            s.sem(n) for n in ("w_loaded", "loaded", "turned", "yT_ready", "hidden", "hT_ready", "output", "used",
                               "weighed", "scored", "step", "written"))
        block = s.block()

        @block.sync
        def _(sp):
            sp.dma_start(w1s[:, :, :], w1.rearrange("(k p) n -> p k n", p=P)).then_inc(w_loaded, 16)
            sp.dma_start(w2s[:, :, :], w2.rearrange("(m p) n -> p m n", p=P)).then_inc(w_loaded, 16)
            with nc.allow_non_contiguous_dma("the first bias, once"):
                sp.dma_start(b1s[:, :], b1.rearrange("(m p) -> p m", p=P)).then_inc(w_loaded, 16)
            sp.dma_start(b2s[:, :], row_bc(b2)).then_inc(w_loaded, 16)
            sp.dma_start(wrs[:, :], row_bc(wr.rearrange("d o -> (d o)"))).then_inc(w_loaded, 16)
            sp.dma_start(brs[:, :], row_bc(br)).then_inc(w_loaded, 16)
            with sp.Fori(0, BLOCKS) as i:
                sp.wait_ge(scored, i + 1)
                sp.wait_ge(turned, i * NB + 1)
                load_block(sp, (y3,), (yb,), i, loaded)

        @block.gpsimd
        def _(pool):
            with pool.Fori(0, BLOCKS) as i:
                pool.wait_ge(weighed, i + 1)
                hold(pool)
                pool.dma_start(tiles_of(z_out)[:, bass.ds(i * BT, BT), :], z[:, :, :]).then_inc(written, 16)
            pool.wait_ge(written, 16 * BLOCKS)

        @block.tensor
        def _(pe):
            pe.wait_ge(w_loaded, 96)
            pe.sem_inc(turned, 1)
            with pe.Fori(0, BLOCKS) as i:
                pe.wait_ge(loaded, 16 * i + 16)
                for n in range(NB):
                    pe.wait_ge(yT_ready, i * NB + n + 1)
                    pe.wait_ge(hT_ready, i * 2 * M + 4)
                    for m in range(4 * n, min(4 * n + 4, 2 * BT)):
                        k, j = divmod(m, BT)
                        ins = nc.tensor.transpose(K.ps[n][:, (m % 4) * P:(m % 4 + 1) * P],
                                                  yb[:, j, k * P:(k + 1) * P], K.ident[:, :])
                    ins.then_inc(turned, 1)
                pe.wait_ge(yT_ready, (i + 1) * NB + 4)
                for m in range(M):
                    for q in range(2):
                        n = 2 * m + q
                        pe.wait_ge(hT_ready, i * 2 * M + n + 1)
                        for k in range(2):
                            ins = nc.tensor.matmul(K.ps[n % 4][:, 0:WIDE], w1s[:, k, m * P:(m + 1) * P],
                                                   yT[:, k, q * WIDE:(q + 1) * WIDE], start=(k == 0), stop=(k == 1))
                        ins.then_inc(hidden, 1)
                pe.wait_ge(hT_ready, (i + 1) * 2 * M + 4)
                for j in range(BT):
                    pe.wait_ge(used, i * BT + j + 1)
                    for m in range(M):
                        ins = nc.tensor.matmul(K.ps[4 + j % 4][:, 0:DIM], hT[:, m, j * P:(j + 1) * P], w2s[:, m, :],
                                               start=(m == 0), stop=(m == M - 1))
                    ins.then_inc(output, 1)

        @block.scalar
        def _(act):
            act.sem_inc(yT_ready, 4)
            act.sem_inc(hT_ready, 4)
            with act.Fori(0, BLOCKS) as i:
                act.wait_ge(used, i * BT + 4)
                hold(act)
                for n in range(NB):
                    act.wait_ge(turned, i * NB + n + 2)
                    width = min(4, 2 * BT - 4 * n)
                    nc.scalar.activation(yT[:, :, :].rearrange("p k t -> p (k t)")[:, 4 * n * P:(4 * n + width) * P],
                                         K.ps[n][:, 0:width * P], ACT.Copy).then_inc(yT_ready, 1)
                for m in range(M):
                    for q in range(2):
                        n = 2 * m + q
                        act.wait_ge(hidden, i * 2 * M + n + 1)
                        nc.scalar.activation(hT[:, m, q * WIDE:(q + 1) * WIDE], K.ps[n % 4][:, 0:WIDE],
                                             ACT.Gelu_apprx_tanh, bias=b1s[:, m:m + 1]).then_inc(hT_ready, 1)

        @block.vector
        def _(dve):
            dve.wait_ge(w_loaded, 96)
            dve.sem_inc(used, 4)
            dve.sem_inc(scored, 1)
            TT = nc.vector.tensor_tensor

            def turn(i, first=False):
                link = Chain(dve, step, i * 2)
                dve.wait_ge(loaded, 16 * i + 16)
                link(TT(scr[:, :, :], yb[:, :, :], bc(wrs[:, :].unsqueeze(1), [P, BT, DIM]), ALU.mult))
                at = score[:, bass.ds(i * BT, BT)]
                link(nc.vector.tensor_reduce(at, scr[:, :, :], AXX, ALU.add))
                nc.vector.tensor_scalar(at, at, brs[:, :], None, ALU.add).then_inc(scored, 1)
                dve.wait_ge(scored, i + 2)
                if not first:
                    dve.wait_ge(written, 16 * i)
                for j in range(BT):
                    dve.wait_ge(output, i * BT + j + 1)
                    TT(z[:, j, :], K.ps[4 + j % 4][:, 0:DIM], b2s[:, :], ALU.add).then_inc(used, 1)
                dve.wait_ge(used, (i + 1) * BT + 4)
                TT(z[:, :, :], z[:, :, :], bc(at.unsqueeze(2), [P, BT, DIM]), ALU.mult).then_inc(weighed, 1)

            turn(0, first=True)
            with dve.Fori(1, BLOCKS) as i:
                turn(i)


def select_stage(nc, K, score, z, r3, out):
    KEPT = max(1, int(0.5 * NODES)) - 1
    SIGN = -2 ** 31
    with stage(nc, "sel") as s:
        zb = s.sb("zb", [P, TILES, DIM])
        rb = s.sb("rb", [P, TILES, DIM])
        w = s.sb("w", [P, TILES])
        hit = s.sb("hit", [P, TILES])
        above = s.sb("above", [P, TILES])
        prior = s.sb("prior", [P, TILES])
        order = s.sb("order", [P, 1], I32)
        trial, neg, word = (s.sb(n, [P, 1], I32) for n in ("trial", "neg", "word"))
        bits = s.sb("bits", [P, 32], I32)
        keep = s.sb("keep", [P, 1])
        keep_i = s.sb("keep_i", [P, 1], I32)
        cnt = s.sb("cnt", [P, 1])
        loaded, masked, bits_ready, counted, summed, step, turned_on, ready, written = (
            s.sem(n) for n in ("loaded", "masked", "bits_ready", "counted", "summed", "step", "turned_on", "ready",
                               "written"))
        block = s.block()

        @block.sync
        def _(sp):
            sp.dma_start(zb[:, :, :], tiles_of(z)).then_inc(loaded, 16)
            sp.dma_start(rb[:, :, :], tiles_of(r3)).then_inc(loaded, 16)
            sp.wait_ge(ready, 1)
            full = (TILES - 1) * P
            sp.dma_start(tiles_of(out[0:full, :]), rb[:, 0:TILES - 1, :]).then_inc(written, 16)
            sp.dma_start(out[full:NODES, :], rb[0:TAIL, TILES - 1, :]).then_inc(written, 16)
            sp.wait_ge(written, 32)

        @block.gpsimd
        def _(pool):
            nc.gpsimd.affine_select(out=w[:, :], in_=score[:, :], compare_op=ALU.is_ge, fill=-3.4028234663852886e38,
                                    base=NODES - 1, pattern=[[-P, TILES]], channel_multiplier=-1).then_inc(masked, 1)

        @block.tensor
        def _(pe):
            with pe.Fori(0, 33) as n:
                pe.wait_ge(counted, n + 1)
                nc.tensor.matmul(K.ps[0][:, 0:1], K.ones[:, :], cnt[:, :], start=True, stop=True).then_inc(summed, 1)
            pe.wait_ge(counted, 34)
            nc.tensor.matmul(K.ps[1][:, 0:TILES], K.before[:, :], hit[:, :], start=True, stop=True)
            nc.tensor.matmul(K.ps[2][:, 0:TILES], K.ones[:, :], hit[:, :], start=True, stop=True).then_inc(summed, 1)

        @block.vector
        def _(dve):
            link = Chain(dve, step)
            TS, TT = nc.vector.tensor_scalar, nc.vector.tensor_tensor
            link(nc.vector.memset(order[:, :], 0))
            for n in range(32):
                link(nc.vector.memset(bits[:, n:n + 1], SIGN if n == 0 else 1 << (31 - n)))
            dve.wait_ge(masked, 1)

            def to_float(into, code):
                yield TS(neg[:, :], code[:, :], 31, None, ALU.arith_shift_right)
                yield TS(word[:, :], neg[:, :], -1, SIGN, ALU.bitwise_xor, ALU.bitwise_or)
                yield TT(into[:, :], code[:, :], word[:, :], ALU.bitwise_xor)

            base = link.n
            STEPS = 7
            with dve.Fori(0, 32) as n:
                here = Chain(dve, step, base + n * STEPS)
                here(TT(trial[:, :], order[:, :], bits[:, bass.ds(n, 1)], ALU.bitwise_or))
                for ins in to_float(keep_i, trial):
                    here(ins)
                TS(hit[:, :], w[:, :], keep_i[:, :].bitcast(F32), None, ALU.is_ge, ALU.add,
                   accum_out=cnt[:, :]).then_inc(counted, 1)
                dve.wait_ge(summed, n + 1)
                here(TS(keep[:, :], K.ps[0][:, 0:1], float(KEPT), -1.0, ALU.is_ge, ALU.mult))
                here(nc.vector.tensor_copy(neg[:, :], keep[:, :]))
                TT(neg[:, :], neg[:, :], bits[:, bass.ds(n, 1)], ALU.bitwise_and).then_inc(turned_on, 1)
                dve.wait_ge(turned_on, n + 1)
                here(TT(order[:, :], order[:, :], neg[:, :], ALU.bitwise_or))
            link = Chain(dve, step, base + 32 * STEPS)
            for ins in to_float(trial, order):
                link(ins)
            lowest = trial[:, :].bitcast(F32)
            TS(above[:, :], w[:, :], lowest, None, ALU.is_gt, ALU.add, accum_out=cnt[:, :]).then_inc(counted, 1)
            dve.wait_ge(summed, 33)
            link(TS(cnt[:, :], K.ps[0][:, 0:1], -1.0, float(KEPT), ALU.mult, ALU.add))
            TS(hit[:, :], w[:, :], lowest, None, ALU.is_equal).then_inc(counted, 1)
            dve.wait_ge(summed, 34)
            link(nc.vector.memset(prior[:, 0:1], 0.0))
            link(nc.vector.tensor_copy(w[:, :], K.ps[2][:, 0:TILES]))
            link(nc.vector.tensor_tensor_scan(prior[:, 1:TILES], w[:, 0:TILES - 1], w[:, 0:TILES - 1], 0.0, ALU.add, ALU.max))
            link(TT(prior[:, :], prior[:, :], K.ps[1][:, 0:TILES], ALU.add))
            link(TS(prior[:, :], prior[:, :], cnt[:, :], None, ALU.is_lt))
            link(TT(prior[:, :], prior[:, :], hit[:, :], ALU.mult))
            link(TT(above[:, :], above[:, :], prior[:, :], ALU.add))
            dve.wait_ge(loaded, 32)
            link(TT(zb[:, :, :], zb[:, :, :], bc(above[:, :].unsqueeze(2), [P, TILES, DIM]), ALU.mult))
            TT(rb[:, :, :], rb[:, :, :], zb[:, :, :], ALU.add).then_inc(ready, 1)


class Consts:

    def __init__(self, nc, ctx):
        def sb(name, shape, dt=F32):
            return ctx.enter_context(nc.sbuf_tensor(name, shape, dt))
        self.ones, self.ident, self.before, self.upto = (sb(n, [P, P]) for n in ("ones", "ident", "before", "upto"))
        self.count = sb("count", [P, CHUNKS])
        self.eps = sb("eps", [P, 1])
        self.bucket = {side: sb(f"bucket_{side}", [1, CHUNKS], I32) for side in ("dst", "src")}
        self.base = sb("base", [P, CHUNKS])
        self.off = sb("off", [1, CHUNKS], I32)
        self.unsorted = sb("unsorted", [1, 1], I32)
        self.psum = ctx.enter_context(nc.psum_tensor("psum", [P, 8, 512], F32))
        self.ps = [self.psum[:, n, :] for n in range(8)]


def program(nc, A, out):
    def nodes(name):
        return nc.dram_tensor(name, [ROWS, DIM], F32).ap()

    rows_dst = nc.dram_tensor("rows_dst", [CHUNKS * P, META], F32).ap()
    rows_src = nc.dram_tensor("rows_src", [CHUNKS * P, META2], F32).ap()
    x0, h, feat_in, feat_out, a_in, a_out = (nodes(n) for n in ("x0", "h", "feat_in", "feat_out", "a_in", "a_out"))
    x1, y1, x2, y2, up, skip, msg, o = (nodes(n) for n in ("x1", "y1", "x2", "y2", "up", "skip", "msg", "o"))
    r3, y3, z = (nodes(n) for n in ("r3", "y3", "z"))
    with ExitStack() as ctx:
        K = Consts(nc, ctx)
        front_stage(nc, K, A, x0, h, (feat_in, feat_out), rows_dst, rows_src)
        unsorted_stages(nc, K, A, rows_dst)
        gather_stage(nc, K, "dst", rows_dst, META, feat_in, a_in)
        gather_stage(nc, K, "src", rows_src, META2, feat_out, a_out)
        update_stage(nc, K, x0, h, a_in, a_out, A["L0_gnn_W_x2i"], A["L0_gnn_b_x2i"], A["L0_gnn_W_h2h"], x1, y1)
        moe_stage(nc, K, y1, x1, A["router_T"], A["L0_ffn_w1"], A["L0_ffn_b1"], A["L0_ffn_w2"], A["L0_ffn_b2"], x2, y2)
        project_stage(nc, K, "proj1", y2, (A["W_up"], A["W_sc"]), None, (up, skip))
        message_stage(nc, K, rows_dst, up, A["M1_blocks"], A["M2_blocks"], A["M3_blocks"], A["M4_twice"], msg)
        mix_stage(nc, K, msg, skip, A["W_lin"], A["W_wb"], A["poly0"], A["poly1"], o)
        finish_stage(nc, K, o, x2, A["L1_gnn_gamma0"], A["L1_gnn_beta0"], A["L1_gnn_gamma1"], r3, y3)
        score = ctx.enter_context(nc.sbuf_tensor("score", [P, TILES], F32))
        ffn_stage(nc, K, y3, A["L1_ffn_wr"], A["L1_ffn_br"], A["L1_ffn_w1"], A["L1_ffn_b1"], A["L1_ffn_w2"],
                  A["L1_ffn_b2"], z, score)
        select_stage(nc, K, score, z, r3, out)


def kernel(**inputs):
    import numpy as np
    import concourse.bacc as bacc
    from concourse.bass_utils import run_bass_kernel_spmd

    nc = bacc.Bacc("TRN2", target_bir_lowering=False, num_devices=1)
    laid = {name: np.asarray(a) for name, a in inputs.items() if name in USED}
    rows = np.zeros((EDGES, META), np.float32)
    rows[:, 2] = np.asarray(inputs["edge_weight"])
    rows[:, 3:7] = np.asarray(inputs["edge_attr_4"])
    rows[:, 8:24] = np.asarray(inputs["edge_attr_16"])
    laid["edge_rows"] = rows
    for name, w0, w1 in (("up", "L1_gnn_W_up0", "L1_gnn_W_up1"), ("sc", "L1_gnn_Wsc0", "L1_gnn_Wsc1")):
        w = np.zeros((DIM, DIM), np.float32)
        w[:C, :C] = np.asarray(inputs[w0])
        for a in range(3):
            w[C + a::3, C + C * a:2 * C + C * a] = np.asarray(inputs[w1])
        laid["W_" + name] = w
    m1 = np.zeros((P, HALF // 2, P), np.float32)
    for c in range(HALF):
        m1[MLP_IN * c:MLP_IN * (c + 1), c // 2, C * (c % 2):C * (c % 2 + 1)] = np.asarray(inputs["L1_gnn_M1"])
    laid["M1_blocks"] = m1
    for name in ("M2", "M3"):
        w = np.zeros((P, P), np.float32)
        w[:C, :C] = w[C:, C:] = np.asarray(inputs["L1_gnn_" + name])
        laid[name + "_blocks"] = w
    laid["M4_twice"] = np.concatenate([np.asarray(inputs["L1_gnn_M4"])] * 2)
    for name, w0, w1 in (("lin", "L1_gnn_W_lin0", "L1_gnn_W_lin1"), ("wb", "L1_gnn_WB0", "L1_gnn_WB1")):
        w = np.zeros((P, 2, P), np.float32)
        w[:C, 0, :C] = np.asarray(inputs[w0])
        w[C:, 0, C:] = w[:C, 1, :C] = w[C:, 1, C:] = np.asarray(inputs[w1])
        laid["W_" + name] = w
    laid["poly0"] = np.ascontiguousarray(np.asarray(inputs["L1_gnn_Wc0"]).T)
    laid["poly1"] = np.ascontiguousarray(np.asarray(inputs["L1_gnn_Wc1"]).T)
    laid["router_T"] = np.ascontiguousarray(np.asarray(inputs["L0_ffn_router_w"]).T)
    arrays, A = {}, {}
    for name, a in laid.items():
        arrays[f"in_{name}"] = np.ascontiguousarray(a)
        A[name] = nc.dram_tensor(f"in_{name}", a.shape, mybir.dt.from_np(a.dtype), kind="ExternalInput").ap()
    out = nc.dram_tensor("out_0", (NODES, DIM), F32, kind="ExternalOutput").ap()
    program(nc, A, out)
    return run_bass_kernel_spmd(nc, [arrays], core_ids=[0]).results[0]["out_0"]


USED = ["x", "src", "dst", "edge_weight_n2", "L0_gnn_gamma", "L0_gnn_beta", "L0_gnn_W_in", "L0_gnn_b_in", "L0_gnn_W_out",
        "L0_gnn_b_out", "L0_gnn_W_x2i", "L0_gnn_b_x2i", "L0_gnn_W_h2h", "L0_ffn_w1", "L0_ffn_b1", "L0_ffn_w2",
        "L0_ffn_b2", "L1_gnn_gamma0", "L1_gnn_beta0", "L1_gnn_gamma1", "L1_ffn_wr", "L1_ffn_br", "L1_ffn_w1",
        "L1_ffn_b1", "L1_ffn_w2", "L1_ffn_b2"]
```

```python
import concourse.bass as bass
from concourse import mybir
from contextlib import ExitStack, contextmanager

F32 = mybir.dt.float32
I32 = mybir.dt.int32
ALU = mybir.AluOpType
ACT = mybir.ActivationFunctionType
AXX = mybir.AxisListType.X

NODES, DIM, EDGES = 6250, 256, 200000
P = 128
TILES = -(-NODES // P)
ROWS = TILES * P
TAIL = NODES - (TILES - 1) * P
BT = 7
BLOCKS = TILES // BT
TOK = BT * P
EP = 125
EC = EDGES // EP
HALF = 8
TURN = 2 * HALF
PARTS = 4
LAP = PARTS * HALF
PAIR = 2 * P
PAIRS = HALF // 2
CHUNKS = -(-2 * ((EDGES - TILES) // PAIR + TILES) // LAP) * LAP
LAPS = CHUNKS // LAP
META = 32
META2 = 4
C = 64
EPS = 1e-5
HID = 4 * DIM
MLP_IN = 16
EXPERTS = 8


class Chain:

    def __init__(self, eng, sem, start=0):
        self.eng, self.sem, self.start, self.n = eng, sem, start, 0

    def __call__(self, ins):
        ins.then_inc(self.sem, 1)
        self.n += 1
        self.eng.wait_ge(self.sem, self.start + self.n)
        return ins


def hold(eng):
    eng.nop(nofuse=True)


class Stage:

    def __init__(self, nc, ctx, tag):
        self.nc, self.ctx, self.tag = nc, ctx, tag

    def sb(self, name, shape, dt=F32):
        return self.ctx.enter_context(self.nc.sbuf_tensor(f"{self.tag}_{name}", shape, dt))

    def sem(self, name):
        return self.nc.alloc_semaphore(f"{self.tag}_{name}")

    def sems(self, name, n):
        return [self.sem(f"{name}{i}") for i in range(n)]

    def block(self):
        return self.ctx.enter_context(self.nc.Block())


@contextmanager
def stage(nc, tag):
    with nc.cleanup_on_exit():
        with ExitStack() as ctx:
            yield Stage(nc, ctx, tag)


def bc(ap, shape):
    return ap.to_broadcast(shape)


def tiles_of(dram):
    return dram.rearrange("(t p) d -> p t d", p=P)


class RowNorm:

    def __init__(self, nc, s, K):
        self.nc, self.K = nc, K
        self.stats = s.sb("ln_stats", [P, BT, 6])
        self.mv = s.sb("ln_mv", [P, BT, 2])
        self.sd = s.sb("ln_sd", [P, BT, 1])
        self.rstd = s.sb("ln_rstd", [P, BT, 1])
        self.stats_done = s.sem("ln_stats_done")
        self.mv_done = s.sem("ln_mv_done")
        self.sd_done = s.sem("ln_sd_done")
        self.rstd_done = s.sem("ln_rstd_done")
        self.done = s.sem("ln_done")

    def on_vector(self, dve, i, tile):
        nc = self.nc
        for j in range(BT):
            ins = nc.vector.bn_stats(self.stats[:, j, :], tile(j))
        ins.then_inc(self.stats_done, 1)
        dve.wait_ge(self.stats_done, i + 1)
        hold(dve)
        for j in range(BT):
            ins = nc.vector.bn_aggr(self.mv[:, j, :], self.stats[:, j, :])
        ins.then_inc(self.mv_done, 1)
        dve.wait_ge(self.sd_done, i + 1)
        nc.vector.reciprocal(self.rstd[:, :, :], self.sd[:, :, :]).then_inc(self.rstd_done, 1)
        dve.wait_ge(self.rstd_done, i + 1)
        hold(dve)
        for j in range(BT):
            ins = nc.vector.tensor_scalar(tile(j), tile(j), self.mv[:, j, 0:1], self.rstd[:, j, :],
                                          ALU.subtract, ALU.mult)
        ins.then_inc(self.done, 1)

    def on_scalar(self, act, i):
        act.wait_ge(self.mv_done, i + 1)
        self.nc.scalar.activation(self.sd[:, :, :], self.mv[:, :, 1:2], ACT.Sqrt,
                                  bias=self.K.eps[:, :]).then_inc(self.sd_done, 1)




class Sorter:

    def __init__(self, nc, s, K, side, work):
        self.nc, self.K, self.side, self.work = nc, K, side, work
        self.counts = s.sb(f"{side}_counts", [EP, TILES])
        self.first = s.sb(f"{side}_first", [EP, TILES])
        self.total_i = s.sb(f"{side}_total_i", [TILES, 1], I32)
        self.padded = s.sb(f"{side}_padded", [TILES, 1])
        self.slack = s.sb(f"{side}_slack", [TILES, 1])
        self.slack_wide = s.sb(f"{side}_slack_wide", [TILES, P])
        self.padded_wide = s.sb(f"{side}_padded_wide", [TILES, EP])
        self.end_chunk = s.sb(f"{side}_end_chunk", [TILES, 1])
        self.step, self.counted, self.totalled, self.padded_ready, self.placed, self.ended_ready, self.tables = (
            s.sem(f"{side}_{n}") for n in ("step", "counted", "totalled", "padded_ready", "placed", "ended_ready",
                                           "tables"))
        self.link = None

    def count_on_vector(self, dve, index, local_out=None):
        nc, K, W, side = self.nc, self.K, self.work, self.side
        link = self.link = Chain(dve, self.step)
        link(nc.vector.tensor_scalar(W.key_i[:, :], index[:, :], 7, None, ALU.arith_shift_right))
        link(nc.vector.tensor_copy(W.key[:, :], W.key_i[:, :]))
        if local_out is not None:
            link(nc.vector.tensor_scalar(W.key_i[:, :], index[:, :], P - 1, None, ALU.bitwise_and))
            link(nc.vector.tensor_copy(local_out, W.key_i[:, :]))
        with dve.Fori(0, TILES) as b:
            dve.wait_ge(self.counted, b + 1)
            nc.vector.tensor_scalar(W.mask[:, :], W.key[:, :], K.count[0:EP, bass.ds(b, 1)], None, ALU.is_equal,
                                    ALU.add, accum_out=self.counts[:, bass.ds(b, 1)]).then_inc(self.counted, 1)
        dve.wait_ge(self.totalled, 1)
        link(nc.vector.tensor_scalar(self.total_i[:, :], K.ps[0][0:TILES, 0:1], float(PAIR - 1), None, ALU.add))
        link(nc.vector.tensor_scalar(self.total_i[:, :], self.total_i[:, :], -PAIR, None, ALU.bitwise_and))
        link(nc.vector.tensor_copy(self.padded[:, :], self.total_i[:, :]))
        link(nc.vector.tensor_tensor(self.slack[:, :], self.padded[:, :], K.ps[0][0:TILES, 0:1], ALU.subtract))
        nc.vector.tensor_scalar(self.slack_wide[:, :], K.ones[0:TILES, :], self.slack[:, :], None, ALU.mult)
        nc.vector.tensor_scalar(self.padded_wide[:, :], K.ones[0:TILES, 0:EP], self.padded[:, :], None,
                                ALU.mult).then_inc(self.padded_ready, 1)
        dve.wait_ge(self.placed, 2)
        link(nc.vector.tensor_copy(self.first[:, :], K.ps[1][0:EP, 0:TILES]))
        link(nc.vector.tensor_scalar(self.end_chunk[:, :], K.ps[2][0:TILES, 0:1], 1.0 / P, None, ALU.mult))
        nc.vector.tensor_scalar(W.ended[:, :], K.count[0:TILES, :], self.end_chunk[:, :], None,
                                ALU.is_ge).then_inc(self.ended_ready, 1)
        PART = CHUNKS // 4
        for n in range(4):
            here = slice(n * PART, (n + 1) * PART)
            dve.wait_ge(self.tables, n + 1)
            bucket = nc.vector.tensor_scalar(K.bucket[side][:, here], K.ps[3][0:1, 0:PART], float(TILES - 1), None, ALU.min)
            if side == "dst":
                link(nc.vector.tensor_scalar(K.base[:, here], K.ps[3][:, 0:PART], float(TILES - 1), float(P),
                                             ALU.min, ALU.mult))
                link(nc.vector.scalar_tensor_tensor(W.off[:, here], K.count[0:1, here], float(P), K.ps[4][0:1, 0:PART],
                                                    ALU.mult, ALU.subtract))
                ins = nc.vector.tensor_scalar(K.off[:, here], W.off[:, here], float(EDGES), None, ALU.min)
            else:
                ins = bucket
            link(ins)

    def count_on_tensor(self, pe):
        nc, K, W = self.nc, self.K, self.work
        pe.sem_inc(self.counted, 1)
        pe.wait_ge(self.counted, TILES + 1)
        nc.tensor.matmul(K.ps[0][0:TILES, 0:1], self.counts[:, :], K.ones[0:EP, 0:1], start=True,
                         stop=True).then_inc(self.totalled, 1)
        pe.wait_ge(self.padded_ready, 1)
        nc.tensor.matmul(K.ps[1][0:EP, 0:TILES], K.before[0:EP, 0:EP], self.counts[:, :], start=True, stop=False)
        nc.tensor.matmul(K.ps[1][0:EP, 0:TILES], self.padded_wide[:, :], K.before[0:TILES, 0:TILES], start=False,
                         stop=True).then_inc(self.placed, 1)
        nc.tensor.matmul(K.ps[2][0:TILES, 0:1], K.upto[0:TILES, 0:TILES], self.padded[:, :], start=True,
                         stop=True).then_inc(self.placed, 1)
        pe.wait_ge(self.ended_ready, 1)
        PART = CHUNKS // 4
        per = 3 if self.side == "dst" else 1
        for n in range(4):
            if n:
                pe.wait_ge(self.step, self.steps_before_tables() + n * per)
            here = slice(n * PART, (n + 1) * PART)
            nc.tensor.matmul(K.ps[3][:, 0:PART], K.ones[0:TILES, :], W.ended[:, here], start=True, stop=True)
            nc.tensor.matmul(K.ps[4][:, 0:PART], self.slack_wide[:, :], W.ended[:, here], start=True,
                             stop=True).then_inc(self.tables, 1)

    def steps_before_tables(self):
        return 8 if self.side == "dst" else 10

    def rank_on_vector(self, dve, place_out):
        nc, K, W = self.nc, self.K, self.work
        link = self.link
        link(nc.vector.memset(W.rank[:, :], 0.0))
        base = link.n
        with dve.Fori(0, TILES) as b:
            turn = Chain(dve, self.step, base + b * 4)
            turn(nc.vector.tensor_scalar(W.mask[:, :], W.key[:, :], K.count[0:EP, bass.ds(b, 1)], None, ALU.is_equal))
            turn(nc.vector.tensor_tensor_scan(W.running[:, :], W.mask[:, :], W.mask[:, :], self.first[:, bass.ds(b, 1)],
                                              ALU.add, ALU.max))
            turn(nc.vector.tensor_tensor(W.running[:, :], W.running[:, :], W.mask[:, :], ALU.mult))
            turn(nc.vector.tensor_tensor(W.rank[:, :], W.rank[:, :], W.running[:, :], ALU.add))
        link = self.link = Chain(dve, self.step, base + 4 * TILES)
        link(nc.vector.tensor_scalar(place_out, W.rank[:, :], -1.0, None, ALU.add))

    def interleave_on_vector(self, place):
        nc, W, link = self.nc, self.work, self.link
        r7 = W.mask[:, :].bitcast(I32)
        link(nc.vector.tensor_scalar(W.key_i[:, :], place, P - 1, 3, ALU.bitwise_and, ALU.logical_shift_left))
        link(nc.vector.tensor_scalar(r7, place, 7, HALF - 1, ALU.arith_shift_right, ALU.bitwise_and))
        link(nc.vector.tensor_tensor(W.key_i[:, :], W.key_i[:, :], r7, ALU.bitwise_or))
        link(nc.vector.tensor_scalar(place, place, -P * HALF, None, ALU.bitwise_and))
        link(nc.vector.tensor_tensor(place, place, W.key_i[:, :], ALU.bitwise_or))


class SortWork:

    def __init__(self, s):
        self.key_i = s.sb("key_i", [EP, EC], I32)
        self.key, self.mask = (s.sb(n, [EP, EC]) for n in ("key", "mask"))
        running, rank = (s.sb(n, [EP, CHUNKS]) for n in ("running", "rank"))
        self.running, self.rank = running[:, 0:EC], rank[:, 0:EC]
        self.ended, self.off = rank[0:TILES, :], running[0:1, :]


class Project:
    NT = 4

    def __init__(self, nc, s, K, h, weights, bias, outs):
        self.nc, self.K, self.h, self.weights, self.bias, self.outs = nc, K, h, weights, bias, outs
        self.w = s.sb("pr_w", [P, 2, 2 * DIM])
        self.b = s.sb("pr_b", [P, 2 * DIM]) if bias is not None else None
        self.hb = s.sb("pr_hb", [P, BT, DIM])
        self.hT = s.sb("pr_hT", [P, 2 * BT, P])
        self.f = s.sb("pr_f", [P, BT, 2 * DIM])
        (self.w_loaded, self.h_loaded, self.transposed, self.hT_ready, self.product, self.f_ready, self.f_written) = (
            s.sem(n) for n in ("w_loaded", "h_loaded", "transposed", "hT_ready", "product", "f_ready", "f_written"))
        self.n_w = 2 + (2 if bias is not None else 0)

    def on_tensor(self, pe):
        nc, K, NT = self.nc, self.K, self.NT
        pe.wait_ge(self.w_loaded, 16 * self.n_w)
        with pe.Fori(0, BLOCKS) as i:
            pe.wait_ge(self.h_loaded, 16 * i + 16)
            for n in range(NT):
                pe.wait_ge(self.hT_ready, i * NT + 1)
                for m in range(4 * n, min(4 * n + 4, 2 * BT)):
                    ins = nc.tensor.transpose(K.ps[n][:, (m % 4) * P:(m % 4 + 1) * P],
                                              self.hb[:, m // 2, (m % 2) * P:(m % 2 + 1) * P], K.ident[:, :])
                ins.then_inc(self.transposed, 1)
            pe.wait_ge(self.hT_ready, i * NT + NT + 1)
            for j in range(BT):
                pe.wait_ge(self.f_ready, i * BT + j + 1)
                for k in range(2):
                    ins = nc.tensor.matmul(K.ps[4 + j % 4][:, :], self.hT[:, 2 * j + k, :], self.w[:, k, :],
                                           start=(k == 0), stop=(k == 1))
                ins.then_inc(self.product, 1)

    def on_scalar(self, act, h_written=None):
        nc, K, NT = self.nc, self.K, self.NT
        for n in range(2):
            act.dma_start(self.w[:, :, n * DIM:(n + 1) * DIM],
                          self.weights[n].rearrange("(k p) n -> p k n", p=P)).then_inc(self.w_loaded, 16)
        if self.bias is not None:
            for n, row in enumerate(self.bias):
                act.dma_start(self.b[:, n * DIM:(n + 1) * DIM], row_bc(row)).then_inc(self.w_loaded, 16)
        if h_written is not None:
            act.wait_ge(h_written, 16)

        def load(i):
            act.dma_start(self.hb[:, :, :], tiles_of(self.h)[:, bass.ds(i * BT, BT), :]).then_inc(self.h_loaded, 16)

        act.sem_inc(self.hT_ready, 1)
        load(0)

        def turn(i, last=False):
            act.wait_ge(self.f_ready, i * BT + 4)
            hold(act)
            for n in range(NT):
                act.wait_ge(self.transposed, i * NT + n + 1)
                width = min(4, 2 * BT - 4 * n)
                nc.scalar.activation(self.hT[:, 4 * n:4 * n + width, :],
                                     K.ps[n][:, 0:width * P].rearrange("p (m q) -> p m q", q=P),
                                     ACT.Copy).then_inc(self.hT_ready, 1)
            if not last:
                load(i + 1)
            act.wait_ge(self.f_ready, (i + 1) * BT + 4)
            for n in range(2):
                act.dma_start(tiles_of(self.outs[n])[:, bass.ds(i * BT, BT), :],
                              self.f[:, :, n * DIM:(n + 1) * DIM]).then_inc(self.f_written, 16)

        with act.Fori(0, BLOCKS - 1) as i:
            turn(i)
        turn(BLOCKS - 1, last=True)
        act.wait_ge(self.f_written, 32 * BLOCKS)

    def on_vector(self, dve):
        nc, K = self.nc, self.K
        dve.wait_ge(self.w_loaded, 16 * self.n_w)
        dve.sem_inc(self.f_ready, 4)

        def copy_out(i, first=False):
            if not first:
                dve.wait_ge(self.f_written, 32 * i)
                hold(dve)
            for j in range(BT):
                dve.wait_ge(self.product, i * BT + j + 1)
                if self.bias is None:
                    ins = nc.vector.tensor_copy(self.f[:, j, :], K.ps[4 + j % 4][:, :])
                else:
                    ins = nc.vector.tensor_tensor(self.f[:, j, :], K.ps[4 + j % 4][:, :], self.b[:, :], ALU.add)
                ins.then_inc(self.f_ready, 1)

        copy_out(0, first=True)
        with dve.Fori(1, BLOCKS) as i:
            copy_out(i)


def project_stage(nc, K, tag, h, weights, bias, outs):
    with stage(nc, tag) as s:
        project = Project(nc, s, K, h, weights, bias, outs)
        block = s.block()

        @block.tensor
        def _(pe):
            project.on_tensor(pe)

        @block.scalar
        def _(act):
            project.on_scalar(act)

        @block.vector
        def _(dve):
            project.on_vector(dve)


COPY_COLS = 32


def front_stage(nc, K, A, x0, h, feats, rows_dst, rows_src):
    with stage(nc, "front") as s:
        W = SortWork(s)
        src_i = s.sb("src_i", [EP, EC], I32)
        dst_i = s.sb("dst_i", [EP, EC], I32)
        record = s.sb("record", [EP, EC, META2])
        slot = s.sb("slot", [EP, 2, HALF, META2])
        broken = s.sb("broken", [EP, 1])
        zero = s.sb("zero", [P, CHUNKS * META2 // 16])
        y = s.sb("y", [P, TILES, DIM])
        sq = s.sb("sq", [P, 2, DIM])
        mean, gain, gam, bet = (s.sb(n, [P, DIM]) for n in ("mean", "gain", "gam", "bet"))
        rows = s.sb("rows", [EP, 2, COPY_COLS, META])
        to_src = Sorter(nc, s, K, "src", W)
        to_dst = Sorter(nc, s, K, "dst", W)
        norm = RowNorm(nc, s, K)
        project = Project(nc, s, K, h, (A["L0_gnn_W_in"], A["L0_gnn_W_out"]), (A["L0_gnn_b_in"], A["L0_gnn_b_out"]), feats)
        (consts, edges_loaded, next_loaded, zeroed, zeros_written, recorded, x_cleared, x_loaded, sums, centred, squared,
         squares, used, h_ready, h_written, col_sd, step, checked, broken_ready, flag_done, x0_written, rows_filled) = (
            s.sem(n) for n in ("consts", "edges_loaded", "next_loaded", "zeroed", "zeros_written", "recorded", "x_cleared",
                               "x_loaded", "sums", "centred", "squared", "squares", "used", "h_ready", "h_written",
                               "col_sd", "step", "checked", "broken_ready", "flag_done", "x0_written", "rows_filled"))
        slot_loaded, sent = s.sems("slot_loaded", 2), s.sems("sent", 2)
        rows_loaded, rows_written = s.sems("rows_loaded", 2), s.sems("rows_written", 2)
        block = s.block()
        TURNS_E = EC // TURN
        SENT = 16 * HALF
        COPIES = EC // (2 * COPY_COLS)
        following = W.running[:, :].bitcast(I32)

        @block.sync
        def _(sp):
            sp.dma_start(src_i[:, :], A["src"].rearrange("(p c) -> p c", p=EP)).then_inc(edges_loaded, 16)
            sp.dma_start(W.rank, A["edge_weight_n2"].rearrange("(p c) -> p c", p=EP)).then_inc(edges_loaded, 16)
            sp.dma_start(dst_i[:, :], A["dst"].rearrange("(p c) -> p c", p=EP)).then_inc(edges_loaded, 16)
            cut = (EP - 1) * EC
            sp.dma_start(following[0:EP - 1, :], A["dst"][1:cut + 1].rearrange("(p c) -> p c", p=EP - 1)).then_inc(next_loaded, 16)
            sp.dma_start(following[EP - 1:EP, 0:EC - 1], A["dst"][cut + 1:EDGES].rearrange("(p c) -> p c", p=1)).then_inc(next_loaded, 16)
            sp.dma_start(following[EP - 1:EP, EC - 1:EC], A["dst"][EDGES - 1:EDGES].rearrange("(p c) -> p c", p=1)).then_inc(next_loaded, 16)
            sp.dma_start(x0[0:NODES, :], A["x"][:, :]).then_inc(x0_written, 16)
            sp.wait_ge(zeroed, 1)
            src_view = rows_src.rearrange("(p r) w -> p (r w)", p=P)
            wide = CHUNKS * META2 // 16
            for n in range(16):
                sp.dma_start(src_view[:, n * wide:(n + 1) * wide], zero[:, :]).then_inc(zeros_written, 16)
            sp.dma_start(rows_dst[EDGES:EDGES + P, :], zero[:, 0:META]).then_inc(zeros_written, 16)
            sp.dma_start(x0[NODES:ROWS, :], zero[0:ROWS - NODES, 0:DIM]).then_inc(x0_written, 16)

            def load(i, first=False):
                for k in range(2):
                    if not first:
                        sp.wait_ge(sent[k], i * SENT)
                    sp.dma_start(slot[:, k, :, :], record[:, bass.ds(i * TURN + HALF * k, HALF), :]).then_inc(slot_loaded[k], 16)

            sp.wait_ge(recorded, 1)
            load(0, first=True)
            with sp.Fori(1, TURNS_E) as i:
                load(i)
            sp.wait_ge(x0_written, 32)

        @block.gpsimd
        def _(pool):
            link = Chain(pool, consts)
            nc.gpsimd.memset(K.ones[:, :], 1.0)
            nc.gpsimd.memset(K.ident[:, :], 0.0)
            nc.gpsimd.iota(K.count[:, :], pattern=[[1, CHUNKS]], base=0, channel_multiplier=0,
                           allow_small_or_imprecise_dtypes=True)
            link(nc.gpsimd.memset(K.before[:, :], 1.0))
            nc.gpsimd.affine_select(out=K.ident[:, :], in_=K.ident[:, :], compare_op=ALU.not_equal, fill=1.0,
                                    base=0, pattern=[[-1, P]], channel_multiplier=1)
            link(nc.gpsimd.affine_select(out=K.upto[:, :], in_=K.before[:, :], compare_op=ALU.is_ge, fill=0.0,
                                         base=0, pattern=[[1, P]], channel_multiplier=-1))
            link(nc.gpsimd.affine_select(out=K.before[:, :], in_=K.before[:, :], compare_op=ALU.is_gt, fill=0.0,
                                         base=0, pattern=[[1, P]], channel_multiplier=-1))
            pool.wait_ge(zeros_written, 16 * 17)
            with pool.Fori(0, TURNS_E) as i:
                for k in range(2):
                    pool.wait_ge(slot_loaded[k], 16 * i + 16)
                    hold(pool)
                    for c in range(HALF):
                        nc.gpsimd.indirect_dma_start(
                            out=rows_src[:, :],
                            out_offset=bass.IndirectOffsetOnAxis(ap=slot[:, k, c, 3:4].bitcast(I32), axis=0),
                            in_=slot[:, k, c, :], in_offset=None).then_inc(sent[k], 16)
            for k in range(2):
                pool.wait_ge(sent[k], TURNS_E * SENT)

        @block.vector
        def _(dve):
            nc.vector.memset(zero[:, :], 0.0).then_inc(zeroed, 1)
            nc.vector.memset(K.eps[:, :], EPS)
            nc.vector.memset(y[:, TILES - 1, :], 0.0).then_inc(x_cleared, 1)
            TT = nc.vector.tensor_tensor
            link = Chain(dve, step)
            dve.wait_ge(edges_loaded, 48)
            dve.wait_ge(next_loaded, 48)
            link(nc.vector.tensor_copy(record[:, :, 2], W.rank))
            link(TT(W.mask[:, :], dst_i[:, :], following, ALU.is_gt))
            nc.vector.tensor_reduce(broken[:, :], W.mask[:, :], AXX, ALU.add).then_inc(broken_ready, 1)
            dve.wait_ge(broken_ready, 1)
            dve.wait_ge(consts, 3)
            to_src.count_on_vector(dve, src_i, record[:, :, 1])
            assert to_src.link.n == 10 + 4, to_src.link.n
            place = record[:, :, 3].bitcast(I32)
            to_src.rank_on_vector(dve, place)
            to_src.interleave_on_vector(place)
            nc.vector.tensor_copy(record[:, :, 0].bitcast(I32), dst_i[:, :]).then_inc(recorded, 1)
            dve.wait_ge(recorded, 1)
            to_dst.count_on_vector(dve, dst_i)
            assert to_dst.link.n == 8 + 12, to_dst.link.n
            dve.wait_ge(flag_done, 1)
            link(nc.vector.tensor_copy(K.unsorted[:, :], K.ps[5][0:1, 0:1]))

            dve.wait_ge(x_loaded, 64)
            with dve.Fori(0, BLOCKS) as i:
                norm.on_vector(dve, i, lambda j: y[:, i * BT + j, :])
            dve.wait_ge(sums, 1)
            link(nc.vector.tensor_scalar(mean[:, :], K.ps[0][:, 0:DIM], 1.0 / NODES, None, ALU.mult))
            TT(y[:, :, :], y[:, :, :], bc(mean[:, :].unsqueeze(1), [P, TILES, DIM]), ALU.subtract).then_inc(centred, 1)
            dve.wait_ge(col_sd, 1)
            link(nc.vector.reciprocal(gain[:, :], gain[:, :]))
            link(TT(gain[:, :], gain[:, :], gam[:, :], ALU.mult))
            link(TT(y[:, :, :], y[:, :, :], bc(gain[:, :].unsqueeze(1), [P, TILES, DIM]), ALU.mult))
            TT(y[:, :, :], y[:, :, :], bc(bet[:, :].unsqueeze(1), [P, TILES, DIM]), ALU.add).then_inc(h_ready, 1)
            project.on_vector(dve)

            with dve.Fori(0, COPIES) as i:
                for k in range(2):
                    here = bass.ds((2 * i + k) * COPY_COLS, COPY_COLS)
                    dve.wait_ge(rows_loaded[k], 16 * i + 16)
                    nc.vector.tensor_copy(rows[:, k, :, 0].bitcast(I32), src_i[:, here])
                    nc.vector.tensor_copy(rows[:, k, :, 1], dst_i[:, here]).then_inc(rows_filled, 1)

        @block.scalar
        def _(act):
            full = (TILES - 1) * P
            act.wait_ge(x_cleared, 1)
            act.dma_start(y[:, 0:TILES - 1, :], tiles_of(A["x"][0:full, :])).then_inc(x_loaded, 16)
            act.dma_start(y[0:TAIL, TILES - 1, :], A["x"][full:NODES, :]).then_inc(x_loaded, 16)
            act.dma_start(gam[:, :], row_bc(A["L0_gnn_gamma"])).then_inc(x_loaded, 16)
            act.dma_start(bet[:, :], row_bc(A["L0_gnn_beta"])).then_inc(x_loaded, 16)
            with act.Fori(0, BLOCKS) as i:
                norm.on_scalar(act, i)
            act.wait_ge(centred, 1)
            with act.Fori(0, (TILES - 1) // 2) as i:
                for k in range(2):
                    act.wait_ge(used, 2 * i + k + 1)
                    nc.scalar.activation(sq[:, k, :], y[:, 2 * i + k, :], ACT.Square).then_inc(squared, 1)
            act.wait_ge(used, TILES)
            nc.scalar.activation(sq[:, 0, :], y[:, TILES - 1, :], ACT.Square).then_inc(squared, 1)
            act.wait_ge(squares, 1)
            nc.scalar.activation(gain[:, :], K.ps[1][:, 0:DIM], ACT.Sqrt, bias=K.eps[:, :],
                                 scale=1.0 / NODES).then_inc(col_sd, 1)
            act.wait_ge(h_ready, 1)
            act.dma_start(tiles_of(h), y[:, :, :]).then_inc(h_written, 16)
            project.on_scalar(act, h_written)

            edge_view = A["edge_rows"].rearrange("(p c) w -> p c w", p=EP)
            table_view = rows_dst[0:EDGES, :].rearrange("(p c) w -> p c w", p=EP)

            def load(i):
                for k in range(2):
                    if not isinstance(i, int):
                        act.wait_ge(rows_written[k], 16 * i)
                    act.dma_start(rows[:, k, :, :],
                                  edge_view[:, bass.ds((2 * i + k) * COPY_COLS, COPY_COLS), :]).then_inc(rows_loaded[k], 16)

            def store(i):
                for k in range(2):
                    act.wait_ge(rows_filled, 2 * i + k + 1)
                    act.dma_start(table_view[:, bass.ds((2 * i + k) * COPY_COLS, COPY_COLS), :],
                                  rows[:, k, :, :]).then_inc(rows_written[k], 16)

            load(0)
            store(0)
            with act.Fori(1, COPIES) as i:
                load(i)
                store(i)
            for k in range(2):
                act.wait_ge(rows_written[k], 16 * COPIES)

        @block.tensor
        def _(pe):
            to_src.count_on_tensor(pe)
            to_dst.count_on_tensor(pe)
            nc.tensor.matmul(K.ps[5][:, 0:1], K.ones[0:EP, :], broken[:, :], start=True, stop=True).then_inc(flag_done, 1)
            pe.wait_ge(norm.done, BLOCKS)
            nc.tensor.matmul(K.ps[0][:, 0:DIM], K.ones[:, :], y[:, 0, :], start=True, stop=False)
            with pe.Fori(1, TILES - 1) as t:
                nc.tensor.matmul(K.ps[0][:, 0:DIM], K.ones[:, :], y[:, t, :], start=False, stop=False)
            nc.tensor.matmul(K.ps[0][:, 0:DIM], K.ones[0:TAIL, :], y[0:TAIL, TILES - 1, :], start=False,
                             stop=True).then_inc(sums, 1)
            pe.sem_inc(used, 2)
            for t in range(2):
                pe.wait_ge(squared, t + 1)
                nc.tensor.matmul(K.ps[1][:, 0:DIM], K.ones[:, :], sq[:, t, :], start=(t == 0), stop=False).then_inc(used, 1)
            with pe.Fori(1, (TILES - 1) // 2) as i:
                for k in range(2):
                    pe.wait_ge(squared, 2 * i + k + 1)
                    nc.tensor.matmul(K.ps[1][:, 0:DIM], K.ones[:, :], sq[:, k, :], start=False, stop=False).then_inc(used, 1)
            pe.wait_ge(squared, TILES)
            nc.tensor.matmul(K.ps[1][:, 0:DIM], K.ones[0:TAIL, :], sq[0:TAIL, 0, :], start=False,
                             stop=True).then_inc(squares, 1)
            project.on_tensor(pe)


def unsorted_stages(nc, K, A, rows_dst):
    with stage(nc, "order") as s:
        W = SortWork(s)
        dst_i = s.sb("dst_i", [EP, EC], I32)
        place = s.sb("place_all", [EP, EC], I32)
        src_i = s.sb("src_i", [EP, EC], I32)
        zero = s.sb("zero", [P, CHUNKS * META // 16])
        row = s.sb("row", [EP, 2, HALF, META])
        at = s.sb("at", [EP, 2, HALF], I32)
        sorter = Sorter(nc, s, K, "dst", W)
        edges_loaded, zeroed, zeros_written, filled, ranked = (
            s.sem(n) for n in ("edges_loaded", "zeroed", "zeros_written", "filled", "ranked"))
        loaded, sent = s.sems("loaded", 2), s.sems("sent", 2)
        TURNS_E = EC // TURN
        SENT = 16 * HALF
        any_broken = nc.values_load(K.unsorted[0:1, 0:1], min_val=0, max_val=EDGES)
        with nc.If(any_broken > 0):
            nc.all_engine_barrier()
            blocks = ExitStack()
            block = blocks.enter_context(nc.Block())

            @block.sync
            def _(sp):
                sp.dma_start(dst_i[:, :], A["dst"].rearrange("(p c) -> p c", p=EP)).then_inc(edges_loaded, 16)
                sp.dma_start(src_i[:, :], A["src"].rearrange("(p c) -> p c", p=EP)).then_inc(edges_loaded, 16)
                sp.wait_ge(zeroed, 1)
                view = rows_dst.rearrange("(p r) w -> p (r w)", p=P)
                wide = CHUNKS * META // 16
                for n in range(16):
                    sp.dma_start(view[:, n * wide:(n + 1) * wide], zero[:, :]).then_inc(zeros_written, 16)
                edge_view = A["edge_rows"].rearrange("(p c) w -> p c w", p=EP)

                def load(i, first=False):
                    for k in range(2):
                        if not first:
                            sp.wait_ge(sent[k], i * SENT)
                        sp.dma_start(row[:, k, :, :], edge_view[:, bass.ds(i * TURN + HALF * k, HALF), :]).then_inc(loaded[k], 16)

                load(0, first=True)
                with sp.Fori(1, TURNS_E) as i:
                    load(i)

            @block.vector
            def _(dve):
                nc.vector.memset(zero[:, :], 0.0).then_inc(zeroed, 1)
                dve.wait_ge(edges_loaded, 32)
                sorter.count_on_vector(dve, dst_i)
                sorter.rank_on_vector(dve, place[:, :])
                sorter.link(nc.vector.tensor_scalar(K.off[:, :], K.count[0:1, :], float(P), None, ALU.mult))

                def fill(i, first=False):
                    for k in range(2):
                        if not first:
                            dve.wait_ge(sent[k], i * SENT)
                        dve.wait_ge(loaded[k], 16 * i + 16)
                        here = bass.ds(i * TURN + HALF * k, HALF)
                        nc.vector.tensor_copy(row[:, k, :, 0].bitcast(I32), src_i[:, here])
                        nc.vector.tensor_copy(row[:, k, :, 1], dst_i[:, here])
                        nc.vector.tensor_copy(at[:, k, :], place[:, here]).then_inc(filled, 1)

                fill(0, first=True)
                with dve.Fori(1, TURNS_E) as i:
                    fill(i)

            @block.tensor
            def _(pe):
                sorter.count_on_tensor(pe)

            @block.gpsimd
            def _(pool):
                pool.wait_ge(zeros_written, 16 * 16)
                with pool.Fori(0, TURNS_E) as i:
                    for k in range(2):
                        pool.wait_ge(filled, 2 * i + k + 1)
                        hold(pool)
                        for c in range(HALF):
                            nc.gpsimd.indirect_dma_start(
                                out=rows_dst[:, :], out_offset=bass.IndirectOffsetOnAxis(ap=at[:, k, c:c + 1], axis=0),
                                in_=row[:, k, c, :], in_offset=None).then_inc(sent[k], 16)
                for k in range(2):
                    pool.wait_ge(sent[k], TURNS_E * SENT)
            blocks.close()


def load_rows(nc, eng, K, rows_dst, row, h, i, loaded):
    for c in range(HALF):
        at = eng.value_load(K.off[0:1, bass.ds(i * LAP + HALF * h + c, 1)], min_val=0, max_val=(CHUNKS - 1) * P)
        eng.dma_start(row[:, h, c, :], rows_dst[bass.ds(at, P), :]).then_inc(loaded, 16)


def gather_on_pool(nc, pool, table, row, got, used, ahead, loaded, load, gathered):
    with pool.Fori(0, LAPS) as i:
        for h in range(PARTS):
            pool.wait_ge(used[h], PAIRS * i + ahead)
            hold(pool)
            pool.wait_ge(loaded[h], load * i + load)
            hold(pool)
            for c in range(HALF):
                nc.gpsimd.indirect_dma_start(
                    out=got[:, HALF * h + c, :], out_offset=None, in_=table[:, :],
                    in_offset=bass.IndirectOffsetOnAxis(ap=row[:, h, c, 0:1].bitcast(I32), axis=0)
                ).then_inc(gathered[h], 16)


def gather_stage(nc, K, side, rows, words, table, out):
    dst = side == "dst"
    with stage(nc, f"gather_{side}") as s:
        acc = s.sb("acc", [P, TILES, DIM])
        row = s.sb("row", [P, PARTS, HALF, words])
        local = s.sb("local", [P, PARTS, HALF])
        got = s.sb("got", [P, LAP, DIM])
        pick = s.sb("pick", [P, LAP, P])
        loaded = s.sems("loaded", PARTS)
        gathered = s.sems("gathered", PARTS)
        used = s.sems("used", PARTS)
        localised, picked, added, cleared, written = (
            s.sem(n) for n in ("localised", "picked", "added", "cleared", "written"))
        block = s.block()
        LOAD = 16 * (HALF if dst else 1)


        def load(eng, i, h):
            eng.wait_ge(used[h], PAIRS * i + 1)
            if dst:
                load_rows(nc, eng, K, rows, row, h, i, loaded[h])
            else:
                view = rows.rearrange("(g p c) w -> g p c w", p=P, c=HALF)
                eng.dma_start(row[:, h, :, :], view[i * PARTS + h, :, :, :]).then_inc(loaded[h], 16)

        @block.sync
        def _(sp):
            with sp.Fori(0, LAPS) as i:
                for h in range(0, PARTS, 2):
                    load(sp, i, h)
            sp.wait_ge(added, CHUNKS // 2 + 8)
            sp.dma_start(tiles_of(out), acc[:, :, :]).then_inc(written, 16)
            sp.wait_ge(written, 16)

        @block.scalar
        def _(act):
            with act.Fori(0, LAPS) as i:
                for h in range(1, PARTS, 2):
                    load(act, i, h)

        @block.gpsimd
        def _(pool):
            gather_on_pool(nc, pool, table, row, got, used, 1, loaded, LOAD, gathered)

        @block.vector
        def _(dve):
            nc.vector.memset(acc[:, :, :], 0.0).then_inc(cleared, 1)
            dve.wait_ge(cleared, 1)
            dve.sem_inc(added, 8)
            for h in range(PARTS):
                dve.sem_inc(used[h], 1)

            def match(i, h):
                dve.wait_ge(used[h], PAIRS * i + 1)
                dve.wait_ge(loaded[h], LOAD * i + LOAD)
                if dst:
                    nc.vector.tensor_tensor(local[:, h, :], row[:, h, :, 1], K.base[:, bass.ds(i * LAP + HALF * h, HALF)],
                                            ALU.subtract).then_inc(localised, 1)
                    dve.wait_ge(localised, PARTS * i + h + 1)
                for c in range(HALF):
                    node = local[:, h, c:c + 1] if dst else row[:, h, c, 1:2]
                    ins = nc.vector.tensor_scalar(pick[:, HALF * h + c, :], K.count[:, 0:P], node,
                                                  row[:, h, c, 2:3], ALU.is_equal, ALU.mult)
                ins.then_inc(picked, 1)

            def turn(i, last=False):
                for h in range(PARTS):
                    if h + 1 < PARTS:
                        match(i, h + 1)
                    elif not last:
                        match(i + 1, 0)
                    for p in range(PAIRS):
                        b = nc.vector.value_load(K.bucket[side][0:1, bass.ds(i * LAP + HALF * h + 2 * p, 1)],
                                                 min_val=0, max_val=TILES - 1)
                        dve.wait_ge(used[h], PAIRS * i + p + 2)
                        dve.wait_ge(added, (i * PARTS + h) * PAIRS + p + 8)
                        nc.vector.tensor_tensor(acc[:, b, :], acc[:, b, :], K.ps[h % 2 * PAIRS + p][:, 0:DIM],
                                                ALU.add).then_inc(added, 1)

            match(0, 0)
            with dve.Fori(0, LAPS - 1) as i:
                turn(i)
            turn(LAPS - 1, last=True)

        @block.tensor
        def _(pe):
            with pe.Fori(0, LAPS) as i:
                for h in range(PARTS):
                    pe.wait_ge(gathered[h], 16 * HALF * i + 16 * HALF)
                    pe.wait_ge(picked, i * PARTS + h + 1)
                    for p in range(PAIRS):
                        pe.wait_ge(added, (i * PARTS + h) * PAIRS + p + 1)
                        for c in range(2):
                            n = HALF * h + 2 * p + c
                            ins = nc.tensor.matmul(K.ps[h % 2 * PAIRS + p][:, 0:DIM], pick[:, n, :], got[:, n, :],
                                                   start=(c == 0), stop=(c == 1))
                        ins.then_inc(used[h], 1)


def load_block(sp, views, tiles, i, loaded):
    for view, tile in zip(views, tiles):
        sp.dma_start(tile[:, :, :], tiles_of(view)[:, bass.ds(i * BT, BT), :]).then_inc(loaded, 16)


def row_bc(vec):
    return vec.rearrange("(a d) -> a d", a=1).broadcast_to([P, vec.shape[0]])


def update_stage(nc, K, x, h, a_in, a_out, w_x2i, b_x2i, w_h2h, x1_out, y1_out):
    with stage(nc, "upd") as s:
        KT = 6
        w = s.sb("w", [P, KT, 2 * DIM])
        b = s.sb("b", [P, 2 * DIM])
        srcs = [s.sb(n, [P, BT, DIM]) for n in ("a_in", "a_out", "h")]
        xb = s.sb("x", [P, BT, DIM])
        aT = s.sb("aT", [P, KT * BT, P])
        gate = s.sb("gate", [P, BT, 2 * DIM])
        y = s.sb("y", [P, BT, DIM])
        norm = RowNorm(nc, s, K)
        w_loaded, loaded, x_loaded, transposed, aT_ready, product, biased, gates, step, written = (
            s.sem(n) for n in ("w_loaded", "loaded", "x_loaded", "transposed", "aT_ready", "product", "biased", "gates",
                               "step", "written"))
        block = s.block()
        n_banks = -(-KT * BT // 4)

        @block.sync
        def _(sp):
            sp.dma_start(w[:, 0:4, :], w_x2i.rearrange("(k p) n -> p k n", p=P)).then_inc(w_loaded, 16)
            sp.dma_start(w[:, 4:6, :], w_h2h.rearrange("(k p) n -> p k n", p=P)).then_inc(w_loaded, 16)
            sp.dma_start(b[:, :], row_bc(b_x2i)).then_inc(w_loaded, 16)

            def turn(i, last=False):
                if not last:
                    sp.wait_ge(transposed, (i + 1) * n_banks)
                    load_block(sp, (a_in, a_out), srcs[0:2], i + 1, loaded)
                    sp.wait_ge(step, i * 5 + 1)
                    load_block(sp, (h,), srcs[2:3], i + 1, loaded)
                sp.wait_ge(norm.done, i + 1)
                sp.dma_start(tiles_of(x1_out)[:, bass.ds(i * BT, BT), :], xb[:, :, :]).then_inc(written, 16)
                sp.dma_start(tiles_of(y1_out)[:, bass.ds(i * BT, BT), :], y[:, :, :]).then_inc(written, 16)
                if not last:
                    sp.wait_ge(written, 32 * i + 32)
                    load_block(sp, (x,), (xb,), i + 1, x_loaded)

            load_block(sp, (a_in, a_out, h), srcs, 0, loaded)
            load_block(sp, (x,), (xb,), 0, x_loaded)
            with sp.Fori(0, BLOCKS - 1) as i:
                turn(i)
            turn(BLOCKS - 1, last=True)
            sp.wait_ge(written, 32 * BLOCKS)

        @block.tensor
        def _(pe):
            pe.wait_ge(w_loaded, 48)
            with pe.Fori(0, BLOCKS) as i:
                pe.wait_ge(loaded, 48 * i + 48)
                for n in range(n_banks):
                    pe.wait_ge(aT_ready, i * n_banks + n + 1)
                    for m in range(4 * n, min(4 * n + 4, KT * BT)):
                        j, k = divmod(m, KT)
                        ins = nc.tensor.transpose(K.ps[n % 4][:, (m % 4) * P:(m % 4 + 1) * P],
                                                  srcs[k // 2][:, j, (k % 2) * P:(k % 2 + 1) * P], K.ident[:, :])
                    ins.then_inc(transposed, 1)
                pe.wait_ge(aT_ready, (i + 1) * n_banks + 4)
                for j in range(BT):
                    pe.wait_ge(biased, i * BT + j + 1)
                    for k in range(KT):
                        ins = nc.tensor.matmul(K.ps[4 + j % 2][:, :], aT[:, KT * j + k, :], w[:, k, :],
                                               start=(k == 0), stop=(k == KT - 1))
                    ins.then_inc(product, 1)

        @block.scalar
        def _(act):
            act.sem_inc(aT_ready, 4)
            with act.Fori(0, BLOCKS) as i:
                act.wait_ge(biased, i * BT + 2)
                hold(act)
                for n in range(n_banks):
                    act.wait_ge(transposed, i * n_banks + n + 1)
                    width = min(4, KT * BT - 4 * n)
                    nc.scalar.activation(aT[:, 4 * n:4 * n + width, :],
                                         K.ps[n % 4][:, 0:width * P].rearrange("p (m q) -> p m q", q=P),
                                         ACT.Copy).then_inc(aT_ready, 1)
                act.wait_ge(biased, (i + 1) * BT + 2)
                nc.scalar.activation(gate[:, :, 0:DIM], gate[:, :, 0:DIM], ACT.Sigmoid).then_inc(gates, 1)
                nc.scalar.activation(gate[:, :, DIM:], gate[:, :, DIM:], ACT.Tanh).then_inc(gates, 1)
                norm.on_scalar(act, i)

        @block.vector
        def _(dve):
            dve.wait_ge(w_loaded, 48)
            dve.sem_inc(biased, 2)

            def turn(i, first=False):
                for j in range(BT):
                    dve.wait_ge(product, i * BT + j + 1)
                    nc.vector.tensor_tensor(gate[:, j, :], K.ps[4 + j % 2][:, :], b[:, :], ALU.add).then_inc(biased, 1)
                link = Chain(dve, step, i * 5)
                if not first:
                    dve.wait_ge(written, 32 * i)
                dve.wait_ge(loaded, 48 * i + 48)
                dve.wait_ge(x_loaded, 16 * i + 16)
                dve.wait_ge(gates, 2 * i + 2)
                link(nc.vector.tensor_tensor(y[:, :, :], srcs[2][:, :, :], gate[:, :, DIM:], ALU.subtract))
                link(nc.vector.tensor_tensor(y[:, :, :], y[:, :, :], gate[:, :, 0:DIM], ALU.mult))
                link(nc.vector.tensor_tensor(y[:, :, :], y[:, :, :], gate[:, :, DIM:], ALU.add))
                link(nc.vector.tensor_tensor(xb[:, :, :], xb[:, :, :], y[:, :, :], ALU.add))
                link(nc.vector.tensor_copy(y[:, :, :], xb[:, :, :]))
                norm.on_vector(dve, i, lambda j: y[:, j, :])

            turn(0, first=True)
            with dve.Fori(1, BLOCKS) as i:
                turn(i)


def moe_stage(nc, K, y1, x1, router_T, w1, b1, w2, b2, x2_out, y2_out):
    E8 = EXPERTS
    NB = 4
    WIDE = TOK // 2
    with stage(nc, "moe") as s:
        w1s = s.sb("w1", [P, E8, 2, DIM])
        w2s = s.sb("w2", [P, E8, 2, DIM])
        b1s = s.sb("b1", [P, E8, 2])
        b2s = s.sb("b2", [E8, DIM])
        rT = s.sb("rT", [P, 2, E8])
        yb = s.sb("yb", [P, BT, DIM])
        xb = s.sb("xb", [P, BT, DIM])
        yT = s.sb("yT", [P, 2, TOK])
        hT = s.sb("hT", [P, 2, 2, TOK])
        acc = s.sb("acc", [P, BT, DIM])
        lg, pr, left, pick, comb = (s.sb(n, [P, BT, E8]) for n in ("lg", "pr", "left", "pick", "comb"))
        rev = s.sb("rev", [P, BT, E8])
        m1, m2, tot, idx = (s.sb(n, [P, BT, 1]) for n in ("m1", "m2", "tot", "idx"))
        combT = s.sb("combT", [E8, BT, P])
        norm = RowNorm(nc, s, K)
        (w_loaded, loaded, x_loaded, transposed, yT_ready, logits, shifted, expd, step, comb_ready, combT_done, combT_ready,
         hidden, hT_ready, expert, added, written) = (
            s.sem(n) for n in ("w_loaded", "loaded", "x_loaded", "transposed", "yT_ready", "logits", "shifted", "expd", "step",
                               "comb_ready", "combT_done", "combT_ready", "hidden", "hT_ready", "expert", "added",
                               "written"))
        block = s.block()
        HPE = 4
        ADDS = BT * E8 + BT

        @block.sync
        def _(sp):
            sp.dma_start(w1s[:, :, :, :], w1.rearrange("e (k p) n -> p e k n", p=P)).then_inc(w_loaded, 16)
            sp.dma_start(w2s[:, :, :, :], w2.rearrange("e (k p) n -> p e k n", p=P)).then_inc(w_loaded, 16)
            with nc.allow_non_contiguous_dma("the first biases, once"):
                sp.dma_start(b1s[:, :, :], b1.rearrange("e (k p) -> p e k", p=P)).then_inc(w_loaded, 16)
            sp.dma_start(b2s[:, :], b2[:, :]).then_inc(w_loaded, 16)
            sp.dma_start(rT[:, :, :], router_T.rearrange("(k p) e -> p k e", p=P)).then_inc(w_loaded, 16)

            def turn(i, last=False):
                if not last:
                    sp.wait_ge(added, i * ADDS + BT + 3)
                    load_block(sp, (y1,), (yb,), i + 1, loaded)
                sp.wait_ge(norm.done, i + 1)
                sp.dma_start(tiles_of(x2_out)[:, bass.ds(i * BT, BT), :], xb[:, :, :]).then_inc(written, 16)
                sp.dma_start(tiles_of(y2_out)[:, bass.ds(i * BT, BT), :], acc[:, :, :]).then_inc(written, 16)
                if not last:
                    sp.wait_ge(written, 32 * i + 32)
                    load_block(sp, (x1,), (xb,), i + 1, x_loaded)

            load_block(sp, (y1,), (yb,), 0, loaded)
            load_block(sp, (x1,), (xb,), 0, x_loaded)
            with sp.Fori(0, BLOCKS - 1) as i:
                turn(i)
            turn(BLOCKS - 1, last=True)
            sp.wait_ge(written, 32 * BLOCKS)

        @block.tensor
        def _(pe):
            pe.wait_ge(w_loaded, 80)
            with pe.Fori(0, BLOCKS) as i:
                pe.wait_ge(loaded, 16 * i + 16)
                for n in range(NB):
                    pe.wait_ge(yT_ready, i * NB + n + 1)
                    for m in range(4 * n, min(4 * n + 4, 2 * BT)):
                        k, j = divmod(m, BT)
                        ins = nc.tensor.transpose(K.ps[n][:, (m % 4) * P:(m % 4 + 1) * P],
                                                  yb[:, j, k * P:(k + 1) * P], K.ident[:, :])
                    ins.then_inc(transposed, 1)
                pe.wait_ge(yT_ready, (i + 1) * NB + 4)
                pe.wait_ge(shifted, i + 1)
                for j in range(BT):
                    for k in range(2):
                        ins = nc.tensor.matmul(K.ps[4][:, j * E8:(j + 1) * E8], yT[:, k, j * P:(j + 1) * P],
                                               rT[:, k, :], start=(k == 0), stop=(k == 1))
                ins.then_inc(logits, 1)

                def hidden_of(e):
                    for m in range(2):
                        for q in range(2):
                            n = (2 * m + q)
                            pe.wait_ge(hT_ready, (i * E8 + e) * HPE + n + 1)
                            for k in range(2):
                                ins = nc.tensor.matmul(K.ps[n][:, 0:WIDE], w1s[:, e, k, m * P:(m + 1) * P],
                                                       yT[:, k, q * WIDE:(q + 1) * WIDE], start=(k == 0), stop=(k == 1))
                            ins.then_inc(hidden, 1)

                def output_of(e):
                    pe.wait_ge(hT_ready, (i * E8 + e + 1) * HPE + 4)
                    for j in range(BT):
                        n = e * BT + j
                        pe.wait_ge(added, i * ADDS + n + 1)
                        for k in range(2):
                            ins = nc.tensor.matmul(K.ps[5 + n % 3][:, 0:DIM], hT[:, e % 2, k, j * P:(j + 1) * P],
                                                   w2s[:, e, k, :], start=(k == 0), stop=(k == 1))
                        ins.then_inc(expert, 1)

                hidden_of(0)
                for e in range(E8):
                    if e + 1 < E8:
                        hidden_of(e + 1)
                    output_of(e)
                pe.wait_ge(comb_ready, i + 1)
                for j in range(BT):
                    ins = nc.tensor.transpose(K.ps[j // 4][0:E8, (j % 4) * P:(j % 4 + 1) * P],
                                              comb[:, j, :], K.ident[:, :])
                ins.then_inc(combT_done, 1)
                pe.wait_ge(combT_ready, i + 1)
                for j in range(BT):
                    n = E8 * BT + j
                    pe.wait_ge(added, i * ADDS + n + 1)
                    nc.tensor.matmul(K.ps[5 + n % 3][:, 0:DIM], combT[:, j, :], b2s[:, :], start=True,
                                     stop=True).then_inc(expert, 1)

        @block.scalar
        def _(act):
            act.sem_inc(yT_ready, 4)
            act.sem_inc(hT_ready, 4)
            with act.Fori(0, BLOCKS) as i:
                act.wait_ge(added, i * ADDS + 3)
                hold(act)
                for n in range(NB):
                    act.wait_ge(transposed, i * NB + n + 1)
                    width = min(4, 2 * BT - 4 * n)
                    nc.scalar.activation(yT[:, :, :].rearrange("p k t -> p (k t)")[:, 4 * n * P:(4 * n + width) * P],
                                         K.ps[n][:, 0:width * P], ACT.Copy).then_inc(yT_ready, 1)
                act.wait_ge(shifted, i + 2)
                nc.scalar.activation(pr[:, :, :], lg[:, :, :], ACT.Exp).then_inc(expd, 1)
                for e in range(E8):
                    if e >= 2:
                        act.wait_ge(expert, i * ADDS + (e - 1) * BT)
                        hold(act)
                    for m in range(2):
                        for q in range(2):
                            n = 2 * m + q
                            act.wait_ge(hidden, (i * E8 + e) * HPE + n + 1)
                            nc.scalar.activation(hT[:, e % 2, m, q * WIDE:(q + 1) * WIDE], K.ps[n][:, 0:WIDE], ACT.Gelu,
                                                 bias=b1s[:, e, m:m + 1]).then_inc(hT_ready, 1)
                act.wait_ge(combT_done, i + 1)
                nc.scalar.activation(combT[:, 0:4, :], K.ps[0][0:E8, :].rearrange("p (j t) -> p j t", t=P), ACT.Copy)
                nc.scalar.activation(combT[:, 4:BT, :], K.ps[1][0:E8, 0:(BT - 4) * P].rearrange("p (j t) -> p j t", t=P),
                                     ACT.Copy).then_inc(combT_ready, 1)
                norm.on_scalar(act, i)

        @block.vector
        def _(dve):
            dve.wait_ge(w_loaded, 80)
            dve.sem_inc(shifted, 1)
            dve.sem_inc(added, 3)
            nc.vector.tensor_scalar(rev[:, :, :], bc(K.count[:, 0:E8].unsqueeze(1), [P, BT, E8]), -1.0, float(E8),
                                    ALU.mult, ALU.add).then_inc(step, 1)
            dve.wait_ge(step, 1)

            def turn(i, first=False):
                link = Chain(dve, step, i * STEPS + 1)
                wide = lambda t: bc(t[:, :, :], [P, BT, E8])
                TT, TR = nc.vector.tensor_tensor, nc.vector.tensor_reduce
                dve.wait_ge(logits, i + 1)
                link(nc.vector.tensor_copy(lg[:, :, :], K.ps[4][:, 0:BT * E8].rearrange("p (j e) -> p j e", e=E8)))
                link(TR(m1[:, :, :], lg[:, :, :], AXX, ALU.max))
                TT(lg[:, :, :], lg[:, :, :], wide(m1), ALU.subtract).then_inc(shifted, 1)
                dve.wait_ge(expd, i + 1)
                link(TR(tot[:, :, :], pr[:, :, :], AXX, ALU.add))
                link(nc.vector.reciprocal(tot[:, :, :], tot[:, :, :]))
                link(TT(pr[:, :, :], pr[:, :, :], wide(tot), ALU.mult))

                def choose(source, best, mask_out):
                    link(TR(best[:, :, :], source[:, :, :], AXX, ALU.max))
                    link(TT(mask_out[:, :, :], source[:, :, :], wide(best), ALU.is_equal))
                    link(TT(mask_out[:, :, :], mask_out[:, :, :], rev[:, :, :], ALU.mult))
                    link(TR(idx[:, :, :], mask_out[:, :, :], AXX, ALU.max))
                    link(TT(mask_out[:, :, :], rev[:, :, :], wide(idx), ALU.is_equal))

                choose(pr, m1, comb)
                link(nc.vector.scalar_tensor_tensor(left[:, :, :], comb[:, :, :], -2.0, pr[:, :, :], ALU.mult, ALU.add))
                choose(left, m2, pick)
                link(TT(comb[:, :, :], comb[:, :, :], pick[:, :, :], ALU.add))
                link(TT(comb[:, :, :], comb[:, :, :], pr[:, :, :], ALU.mult))
                link(TT(tot[:, :, :], m1[:, :, :], m2[:, :, :], ALU.add))
                link(nc.vector.tensor_scalar(tot[:, :, :], tot[:, :, :], 1e-12, None, ALU.max))
                link(nc.vector.reciprocal(tot[:, :, :], tot[:, :, :]))
                TT(comb[:, :, :], comb[:, :, :], wide(tot), ALU.mult).then_inc(comb_ready, 1)
                dve.wait_ge(comb_ready, i + 1)
                if not first:
                    dve.wait_ge(written, 32 * i)
                dve.wait_ge(loaded, 16 * i + 16)
                dve.wait_ge(x_loaded, 16 * i + 16)
                for e in range(E8):
                    for j in range(BT):
                        n = e * BT + j
                        dve.wait_ge(expert, i * ADDS + n + 1)
                        if e:
                            dve.wait_ge(added, i * ADDS + n - BT + 4)
                        base = yb[:, j, :] if e == 0 else acc[:, j, :]
                        nc.vector.scalar_tensor_tensor(acc[:, j, :], K.ps[5 + n % 3][:, 0:DIM], comb[:, j, e:e + 1], base,
                                                       ALU.mult, ALU.add).then_inc(added, 1)
                for j in range(BT):
                    n = E8 * BT + j
                    dve.wait_ge(expert, i * ADDS + n + 1)
                    dve.wait_ge(added, i * ADDS + n - BT + 4)
                    TT(acc[:, j, :], acc[:, j, :], K.ps[5 + n % 3][:, 0:DIM], ALU.add).then_inc(added, 1)
                dve.wait_ge(added, (i + 1) * ADDS + 3)
                link(TT(xb[:, :, :], xb[:, :, :], acc[:, :, :], ALU.add))
                link(nc.vector.tensor_copy(acc[:, :, :], xb[:, :, :]))
                steps.append(link.n)
                norm.on_vector(dve, i, lambda j: acc[:, j, :])

            steps = []
            STEPS = 23
            turn(0, first=True)
            assert steps[0] == STEPS, steps
            with dve.Fori(1, BLOCKS) as i:
                turn(i)
def message_stage(nc, K, rows, table, m1, m2, m3, m4, out):
    with stage(nc, "msg") as s:
        acc = s.sb("acc", [P, TILES, DIM])
        row = s.sb("row", [P, PARTS, HALF, META])
        local = s.sb("local", [P, PARTS, HALF])
        got = s.sb("got", [P, LAP, DIM])
        m1s = s.sb("m1", [P, PAIRS, P])
        m2s, m3s = s.sb("m2", [P, P]), s.sb("m3", [P, P])
        m4s = s.sb("m4", [P, DIM])
        attr = s.sb("attr", [P, P])
        attrT = s.sb("attrT", [P, P])
        hid = s.sb("hid", [P, 2, 512])
        hid3 = s.sb("hid3", [P, 2, 512])
        same = s.sb("same", [P, PAIRS, 2, P])
        wsh = s.sb("wsh", [P, 2, 2, 2, C])
        xsh = s.sb("xsh", [P, 2, 2, 3, C])
        first = s.sb("first", [P, 2, 2, 4, C])
        second = s.sb("second", [P, 2, 2, 4, C])
        u = s.sb("u", [P, 2, 2, C])
        dot = s.sb("dot", [P, 2, 2, C])
        loaded = s.sems("loaded", PARTS)
        gathered = s.sems("gathered", PARTS)
        used = s.sems("used", PARTS)
        (w_loaded, scaled, attr_ready, attr_turned, attrT_ready, layer, act_done, weights, w_scaled, x_scaled, matched,
         step, joined, added, cleared, written, localised) = (
            s.sem(n) for n in ("w_loaded", "scaled", "attr_ready", "attr_turned", "attrT_ready", "layer", "act_done",
                               "weights", "w_scaled", "x_scaled", "matched", "step", "joined", "added", "cleared",
                               "written", "localised"))
        block = s.block()
        mlp_bank = (K.ps[0], K.ps[7])
        weight_part = [K.psum[:, 1 + 2 * n:3 + 2 * n, 0:DIM] for n in range(2)]
        sum_part = [K.ps[5 + n][:, 0:DIM] for n in range(2)]
        LOAD = 16 * HALF

        @block.sync
        def _(sp):
            sp.dma_start(m1s[:, :, :], m1[:, :, :]).then_inc(w_loaded, 16)
            for tile, array in ((m2s, m2), (m3s, m3), (m4s, m4)):
                sp.dma_start(tile[:, :], array[:, :]).then_inc(w_loaded, 16)
            with sp.Fori(0, LAPS) as i:
                for h in range(PARTS):
                    sp.wait_ge(used[h], PAIRS * i + 2)
                    load_rows(nc, sp, K, rows, row, h, i, loaded[h])
            sp.wait_ge(added, CHUNKS // 2 + 2)
            sp.dma_start(tiles_of(out), acc[:, :, :]).then_inc(written, 16)
            sp.wait_ge(written, 16)

        @block.gpsimd
        def _(pool):
            gather_on_pool(nc, pool, table, row, got, used, 2, loaded, LOAD, gathered)

        def part_ahead(i, h, n, last):
            if h + n < PARTS:
                return i, h + n
            return None if last else (i + 1, h + n - PARTS)

        def pair_ahead(i, h, p, n, last):
            part = part_ahead(i, h, (p + n) // PAIRS, last)
            return part and (*part, (p + n) % PAIRS)

        def number(i, h, p):
            return (i * PARTS + h) * PAIRS + p

        def turns(eng, turn):
            with eng.Fori(0, LAPS - 1) as i:
                turn(i)
            turn(LAPS - 1, last=True)

        @block.vector
        def _(dve):
            nc.vector.memset(acc[:, :, :], 0.0).then_inc(cleared, 1)
            dve.wait_ge(w_loaded, 64)
            nc.vector.tensor_scalar(m4s[:, 3 * C:], m4s[:, 3 * C:], float(3.0 ** -0.5), None, ALU.mult).then_inc(scaled, 1)
            dve.wait_ge(cleared, 1)
            for sem in (joined, added, *used):
                dve.sem_inc(sem, 2)
            TT = nc.vector.tensor_tensor
            STEPS = 6

            def prepare(i, h):
                if not (isinstance(i, int) and i == 0 and h == 0):
                    dve.wait_ge(attr_turned, PARTS * i + h)
                dve.wait_ge(loaded[h], LOAD * i + LOAD)
                nc.vector.tensor_copy(attr[:, :].rearrange("p (c f) -> p c f", f=MLP_IN),
                                      row[:, h, :, 8:8 + MLP_IN]).then_inc(attr_ready, 1)
                TT(local[:, h, :], row[:, h, :, 1], K.base[:, bass.ds(i * LAP + HALF * h, HALF)],
                   ALU.subtract).then_inc(localised, 1)

            def match(i, h, p):
                dve.wait_ge(localised, PARTS * i + h + 1)
                TT(same[:, p, :, :], bc(K.count[:, 0:P].unsqueeze(1), [P, 2, P]),
                   bc(local[:, h, 2 * p:2 * p + 2].unsqueeze(2), [P, 2, P]), ALU.is_equal).then_inc(matched, 1)

            def join(i, h, p):
                g, slot, c = number(i, h, p), p % 2, 2 * p
                w, x = weight_part[slot], got[:, HALF * h + c:HALF * h + c + 2, :]
                m, m2 = first[:, slot, :, :, :], second[:, slot, :, :, :]
                base = g * STEPS
                dve.wait_ge(x_scaled, g + 1)
                TT(dot[:, slot, :, :], xsh[:, slot, :, 0, :], xsh[:, slot, :, 1, :], ALU.add).then_inc(step, 1)
                dve.wait_ge(w_scaled, g + 1)
                TT(u[:, slot, :, :], w[:, :, C:2 * C], x[:, :, 0:C], ALU.mult).then_inc(step, 1)
                TT(m[:, :, 1:4, :], bc(wsh[:, slot, :, 1, :].unsqueeze(2), [P, 2, 3, C]),
                   x[:, :, C:].rearrange("p c (a d) -> p c a d", d=C), ALU.mult).then_inc(step, 1)
                dve.wait_ge(step, base + 1)
                TT(dot[:, slot, :, :], dot[:, slot, :, :], xsh[:, slot, :, 2, :], ALU.add).then_inc(step, 1)
                dve.wait_ge(step, base + 2)
                TT(m2[:, :, 1:4, :], bc(u[:, slot, :, :].unsqueeze(2), [P, 2, 3, C]),
                   bc(row[:, h, c:c + 2, 4:7].unsqueeze(3), [P, 2, 3, C]), ALU.mult).then_inc(step, 1)
                TT(m[:, :, 0, :], wsh[:, slot, :, 0, :], x[:, :, 0:C], ALU.mult).then_inc(step, 1)
                dve.wait_ge(step, base + 4)
                TT(m2[:, :, 0, :], w[:, :, 3 * C:], dot[:, slot, :, :], ALU.mult).then_inc(joined, 1)

            def tile_of(i, h, p):
                return nc.vector.value_load(K.bucket["dst"][0:1, bass.ds(i * LAP + HALF * h + 2 * p, 1)], min_val=0,
                                            max_val=TILES - 1)

            def add(i, h, p, b):
                dve.wait_ge(used[h], PAIRS * i + p + 3)
                dve.wait_ge(added, number(i, h, p) + 2)
                TT(acc[:, b, :], acc[:, b, :], sum_part[p % 2], ALU.add).then_inc(added, 1)

            def turn(i, last=False):
                for h in range(PARTS):
                    for p in range(PAIRS):
                        if after := pair_ahead(i, h, p, 1, last):
                            match(*after)
                        join(i, h, p)
                        if p:
                            add(i, h, p - 1, before)
                        before = tile_of(i, h, p)
                        if p == 3 and (part := part_ahead(i, h, 3, last)):
                            prepare(*part)
                    add(i, h, PAIRS - 1, before)

            for h in range(3):
                prepare(0, h)
            match(0, 0, 0)
            turns(dve, turn)

        @block.scalar
        def _(act):
            def mlp(i, h, part):
                half = i * PARTS + h
                if part == 0:
                    act.wait_ge(attr_turned, half + 1)
                    nc.scalar.activation(attrT[:, :], mlp_bank[h % 2][:, 0:P], ACT.Copy).then_inc(attrT_ready, 1)
                else:
                    act.wait_ge(layer, half * 3 + part)
                    into = hid[:, part - 1, :] if part < 3 else hid3[:, h % 2, :]
                    nc.scalar.activation(into, mlp_bank[h % 2][:, :], ACT.Silu).then_inc(act_done, 1)

            def scale_weights(i, h, p):
                act.wait_ge(weights, number(i, h, p) + 1)
                for n in range(2):
                    w = weight_part[p % 2][:, n, :].rearrange("p (k d) -> p k d", d=C)
                    ins = nc.scalar.activation(wsh[:, p % 2, n, :, :], w[:, 0:3:2, :], ACT.Copy,
                                               scale=row[:, h, 2 * p + n, 3:4])
                ins.then_inc(w_scaled, 1)

            def scale_vectors(i, h, p):
                if p == 0:
                    act.wait_ge(gathered[h], 16 * HALF * i + 16 * HALF)
                act.wait_ge(joined, number(i, h, p) + 1)
                for n in range(2):
                    c = 2 * p + n
                    for a in range(3):
                        ins = nc.scalar.activation(xsh[:, p % 2, n, a, :], got[:, HALF * h + c, C * (a + 1):C * (a + 2)],
                                                   ACT.Copy, scale=row[:, h, c, 4 + a:5 + a])
                ins.then_inc(x_scaled, 1)

            def turn(i, last=False):
                for h in range(PARTS):
                    for p in range(PAIRS):
                        if after := pair_ahead(i, h, p, 1, last):
                            scale_vectors(*after)
                            scale_weights(*after)
                        if part := part_ahead(i, h, 2 if p else 1, last):
                            mlp(*part, (p + 3) % 4)

            for part in range(4):
                mlp(0, 0, part)
            scale_vectors(0, 0, 0)
            scale_weights(0, 0, 0)
            for part in range(3):
                mlp(0, 1, part)
            turns(act, turn)

        @block.tensor
        def _(pe):
            pe.wait_ge(w_loaded, 64)
            pe.wait_ge(scaled, 1)

            def mlp(i, h, part):
                half = i * PARTS + h
                if part == 0:
                    pe.wait_ge(attr_ready, half + 1)
                    nc.tensor.transpose(mlp_bank[h % 2][:, 0:P], attr[:, :], K.ident[:, :]).then_inc(attr_turned, 1)
                elif part == 1:
                    pe.wait_ge(attrT_ready, half + 1)
                    for j in range(PAIRS):
                        ins = nc.tensor.matmul(mlp_bank[h % 2][:, j * P:(j + 1) * P], m1s[:, j, :], attrT[:, :],
                                               start=True, stop=True)
                    ins.then_inc(layer, 1)
                else:
                    pe.wait_ge(act_done, half * 3 + part - 1)
                    nc.tensor.matmul(mlp_bank[h % 2][:, :], (m2s, m3s)[part - 2][:, :], hid[:, part - 2, :], start=True,
                                     stop=True).then_inc(layer, 1)

            def weigh(i, h, p):
                if p == 0:
                    pe.wait_ge(act_done, (i * PARTS + h) * 3 + 3)
                pe.wait_ge(joined, number(i, h, p) + 1)
                for n in range(2):
                    ins = nc.tensor.matmul(weight_part[p % 2][:, n, :], hid3[C * n:C * n + C, h % 2, p * P:(p + 1) * P],
                                           m4s[C * n:C * n + C, :], start=True, stop=True)
                ins.then_inc(weights, 1)

            def turn(i, last=False):
                for h in range(PARTS):
                    for p in range(PAIRS):
                        g = number(i, h, p)
                        pe.wait_ge(matched, g + 1)
                        pe.wait_ge(joined, g + 3)
                        pe.wait_ge(added, g + 1)
                        for n in range(2):
                            for k, terms in enumerate((first, second)):
                                ins = nc.tensor.matmul(sum_part[p % 2], same[:, p, n, :],
                                                       terms[:, p % 2, n, :, :].rearrange("p k d -> p (k d)"),
                                                       start=(n == 0 and k == 0), stop=(n == 1 and k == 1))
                        ins.then_inc(used[h], 1)
                        if after := pair_ahead(i, h, p, 2, last):
                            weigh(*after)
                        if part := part_ahead(i, h, 2, last):
                            mlp(*part, p)

            for part in range(4):
                mlp(0, 0, part)
            weigh(0, 0, 0)
            weigh(0, 0, 1)
            for part in range(4):
                mlp(0, 1, part)
            turns(pe, turn)


def mix_stage(nc, K, msg, sc, w_lin, w_b, poly0, poly1, o_out):
    with stage(nc, "mix") as s:
        wl, wb = s.sb("wl", [P, 2, P]), s.sb("wb", [P, 2, P])
        c0, c1 = s.sb("c0", [P, 5, C]), s.sb("c1", [P, 4, C])
        mb, scb = s.sb("mb", [P, BT, DIM]), s.sb("scb", [P, BT, DIM])
        T = s.sb("T", [P, 2 * BT, P])
        a = s.sb("a", [P, BT, DIM])
        bb = s.sb("bb", [P, BT, DIM])
        a2, vv, t0, t1 = (s.sb(n, [P, BT, C]) for n in ("a2", "vv", "t0", "t1"))
        w_loaded, loaded, sc_loaded, turned, T_ready, product, copied, step, written, b_ready = (
            s.sem(n) for n in ("w_loaded", "loaded", "sc_loaded", "turned", "T_ready", "product", "copied", "step",
                               "written", "b_ready"))
        block = s.block()
        NB = 4

        @block.sync
        def _(sp):
            sp.dma_start(wl[:, :, :], w_lin[:, :, :]).then_inc(w_loaded, 16)
            sp.dma_start(wb[:, :, :], w_b[:, :, :]).then_inc(w_loaded, 16)
            for tile, array, n in ((c0, poly0, 5), (c1, poly1, 4)):
                sp.dma_start(tile[:, :, :], array.rearrange("(a n) d -> a n d", a=1).broadcast_to([P, n, C])).then_inc(w_loaded, 16)

            def turn(i, last=False):
                if not last:
                    sp.wait_ge(turned, 2 * i * NB + NB)
                    load_block(sp, (msg,), (mb,), i + 1, loaded)
                sp.wait_ge(copied, (2 * i + 2) * BT + 4)
                sp.dma_start(tiles_of(o_out)[:, bass.ds(i * BT, BT), :], scb[:, :, :]).then_inc(written, 16)
                if not last:
                    sp.wait_ge(written, 16 * i + 16)
                    load_block(sp, (sc,), (scb,), i + 1, sc_loaded)

            load_block(sp, (msg,), (mb,), 0, loaded)
            load_block(sp, (sc,), (scb,), 0, sc_loaded)
            with sp.Fori(0, BLOCKS - 1) as i:
                turn(i)
            turn(BLOCKS - 1, last=True)
            sp.wait_ge(written, 16 * BLOCKS)

        @block.tensor
        def _(pe):
            pe.wait_ge(w_loaded, 64)
            with pe.Fori(0, BLOCKS) as i:
                for r, (src, w) in enumerate(((mb, wl), (bb, wb))):
                    if r == 0:
                        pe.wait_ge(loaded, 16 * i + 16)
                    else:
                        pe.wait_ge(b_ready, i + 1)
                    for n in range(NB):
                        pe.wait_ge(T_ready, (2 * i + r) * NB + n + 1)
                        for m in range(4 * n, min(4 * n + 4, 2 * BT)):
                            ins = nc.tensor.transpose(K.ps[n][:, (m % 4) * P:(m % 4 + 1) * P],
                                                      src[:, m // 2, (m % 2) * P:(m % 2 + 1) * P], K.ident[:, :])
                        ins.then_inc(turned, 1)
                    pe.wait_ge(T_ready, (2 * i + r + 1) * NB + 4)
                    for j in range(BT):
                        pe.wait_ge(copied, (2 * i + r) * BT + j + 1)
                        for k in range(2):
                            ins = nc.tensor.matmul(K.ps[4 + j % 4][:, k * P:(k + 1) * P], T[:, 2 * j + k, :], w[:, k, :],
                                                   start=True, stop=True)
                        ins.then_inc(product, 1)

        @block.scalar
        def _(act):
            act.sem_inc(T_ready, 4)
            with act.Fori(0, BLOCKS) as i:
                for r in range(2):
                    act.wait_ge(copied, (2 * i + r) * BT + 4)
                    hold(act)
                    for n in range(NB):
                        act.wait_ge(turned, (2 * i + r) * NB + n + 1)
                        width = min(4, 2 * BT - 4 * n)
                        nc.scalar.activation(T[:, 4 * n:4 * n + width, :],
                                             K.ps[n][:, 0:width * P].rearrange("p (m q) -> p m q", q=P),
                                             ACT.Copy).then_inc(T_ready, 1)

        @block.vector
        def _(dve):
            dve.wait_ge(w_loaded, 64)
            dve.sem_inc(copied, 4)
            STEPS = 21
            with dve.Fori(0, BLOCKS) as i:
                link = Chain(dve, step, i * STEPS)
                TT = nc.vector.tensor_tensor
                wide = lambda t: bc(t.unsqueeze(1), [P, BT, C])
                for j in range(BT):
                    dve.wait_ge(product, 2 * i * BT + j + 1)
                    nc.vector.tensor_copy(a[:, j, :], K.ps[4 + j % 4][:, 0:DIM]).then_inc(copied, 1)
                dve.wait_ge(copied, 2 * i * BT + BT + 4)
                A0 = a[:, :, 0:C]
                A1 = a[:, :, C:].rearrange("p j (x d) -> p j x d", d=C)
                B0, tt = bb[:, :, 0:C], t1[:, :, :]
                link(TT(bb[:, :, C:], a[:, :, C:], a[:, :, C:], ALU.mult))
                link(TT(vv[:, :, :], bb[:, :, C:2 * C], bb[:, :, 2 * C:3 * C], ALU.add))
                link(TT(vv[:, :, :], vv[:, :, :], bb[:, :, 3 * C:], ALU.add))
                link(TT(a2[:, :, :], A0, A0, ALU.mult))
                link(TT(t0[:, :, :], A0, wide(c1[:, 1, :]), ALU.mult))
                link(TT(t0[:, :, :], t0[:, :, :], wide(c1[:, 0, :]), ALU.add))
                link(TT(tt, a2[:, :, :], wide(c1[:, 2, :]), ALU.mult))
                link(TT(t0[:, :, :], t0[:, :, :], tt, ALU.add))
                link(TT(tt, vv[:, :, :], wide(c1[:, 3, :]), ALU.mult))
                link(TT(t0[:, :, :], t0[:, :, :], tt, ALU.add))
                for x in range(3):
                    ins = TT(bb[:, :, C + C * x:2 * C + C * x], a[:, :, C + C * x:2 * C + C * x], t0[:, :, :], ALU.mult)
                link(ins)
                link(TT(B0, A0, wide(c0[:, 0, :]), ALU.mult))
                link(TT(tt, a2[:, :, :], wide(c0[:, 1, :]), ALU.mult))
                link(TT(B0, B0, tt, ALU.add))
                link(TT(tt, vv[:, :, :], wide(c0[:, 2, :]), ALU.mult))
                link(TT(B0, B0, tt, ALU.add))
                link(TT(a2[:, :, :], a2[:, :, :], A0, ALU.mult))
                link(TT(tt, a2[:, :, :], wide(c0[:, 3, :]), ALU.mult))
                link(TT(B0, B0, tt, ALU.add))
                link(TT(vv[:, :, :], vv[:, :, :], A0, ALU.mult))
                link(TT(tt, vv[:, :, :], wide(c0[:, 4, :]), ALU.mult))
                TT(B0, B0, tt, ALU.add).then_inc(b_ready, 1)
                dve.wait_ge(sc_loaded, 16 * i + 16)
                for j in range(BT):
                    dve.wait_ge(product, (2 * i + 1) * BT + j + 1)
                    TT(scb[:, j, :], scb[:, j, :], K.ps[4 + j % 4][:, 0:DIM], ALU.add).then_inc(copied, 1)
                assert link.n == STEPS, link.n


def finish_stage(nc, K, o, x2, gamma0, beta0, gamma1, r3_out, y3_out):
    with stage(nc, "fin") as s:
        ob = s.sb("ob", [P, TILES, DIM])
        xb = s.sb("xb", [P, BT, DIM])
        yb = s.sb("yb", [P, BT, DIM])
        sq = s.sb("sq", [P, 2, DIM])
        gain = s.sb("gain", [P, DIM])
        shift = s.sb("shift", [P, C])
        g0 = s.sb("g0", [P, 2 * C])
        b0 = s.sb("b0", [P, C])
        norm = RowNorm(nc, s, K)
        loaded, x_loaded, sums, centred, squared, squares, used, col_sd, step, r_ready, written = (
            s.sem(n) for n in ("loaded", "x_loaded", "sums", "centred", "squared", "squares", "used", "col_sd", "step",
                               "r_ready", "written"))
        block = s.block()

        @block.sync
        def _(sp):
            sp.dma_start(ob[:, :, :], tiles_of(o)).then_inc(loaded, 16)
            sp.dma_start(g0[:, 0:C], row_bc(gamma0)).then_inc(loaded, 16)
            sp.dma_start(g0[:, C:], row_bc(gamma1)).then_inc(loaded, 16)
            sp.dma_start(b0[:, :], row_bc(beta0)).then_inc(loaded, 16)

            def turn(i, first=False):
                if not first:
                    sp.wait_ge(written, 32 * i)
                load_block(sp, (x2,), (xb,), i, x_loaded)
                sp.wait_ge(r_ready, i + 1)
                sp.dma_start(tiles_of(r3_out)[:, bass.ds(i * BT, BT), :], xb[:, :, :]).then_inc(written, 16)
                sp.dma_start(tiles_of(y3_out)[:, bass.ds(i * BT, BT), :], yb[:, :, :]).then_inc(written, 16)

            turn(0, first=True)
            with sp.Fori(1, BLOCKS) as i:
                turn(i)
            sp.wait_ge(written, 32 * BLOCKS)

        @block.tensor
        def _(pe):
            pe.wait_ge(loaded, 64)
            nc.tensor.matmul(K.ps[0][:, 0:C], K.ones[:, :], ob[:, 0, 0:C], start=True, stop=False)
            with pe.Fori(1, TILES - 1) as t:
                nc.tensor.matmul(K.ps[0][:, 0:C], K.ones[:, :], ob[:, t, 0:C], start=False, stop=False)
            nc.tensor.matmul(K.ps[0][:, 0:C], K.ones[0:TAIL, :], ob[0:TAIL, TILES - 1, 0:C], start=False,
                             stop=True).then_inc(sums, 1)
            pe.sem_inc(used, 2)
            for t in range(2):
                pe.wait_ge(squared, t + 1)
                nc.tensor.matmul(K.ps[1][:, 0:DIM], K.ones[:, :], sq[:, t, :], start=(t == 0), stop=False).then_inc(used, 1)
            with pe.Fori(1, (TILES - 1) // 2) as i:
                for k in range(2):
                    pe.wait_ge(squared, 2 * i + k + 1)
                    nc.tensor.matmul(K.ps[1][:, 0:DIM], K.ones[:, :], sq[:, k, :], start=False, stop=False).then_inc(used, 1)
            pe.wait_ge(squared, TILES)
            nc.tensor.matmul(K.ps[1][:, 0:DIM], K.ones[0:TAIL, :], sq[0:TAIL, 0, :], start=False,
                             stop=True).then_inc(squares, 1)

        @block.scalar
        def _(act):
            act.wait_ge(centred, 1)
            with act.Fori(0, (TILES - 1) // 2) as i:
                for k in range(2):
                    act.wait_ge(used, 2 * i + k + 1)
                    nc.scalar.activation(sq[:, k, :], ob[:, 2 * i + k, :], ACT.Square).then_inc(squared, 1)
            act.wait_ge(used, TILES)
            nc.scalar.activation(sq[:, 0, :], ob[:, TILES - 1, :], ACT.Square).then_inc(squared, 1)
            act.wait_ge(step, 4)
            nc.scalar.activation(gain[:, 0:C], gain[:, 0:C], ACT.Sqrt, bias=K.eps[:, :], scale=1.0 / NODES)
            nc.scalar.activation(gain[:, C:2 * C], gain[:, C:2 * C], ACT.Sqrt, bias=K.eps[:, :],
                                 scale=1.0 / (3 * NODES)).then_inc(col_sd, 1)
            with act.Fori(0, BLOCKS) as i:
                norm.on_scalar(act, i)

        @block.vector
        def _(dve):
            link = Chain(dve, step)
            TT = nc.vector.tensor_tensor
            dve.wait_ge(sums, 1)
            link(nc.vector.tensor_scalar(shift[:, :], K.ps[0][:, 0:C], 1.0 / NODES, None, ALU.mult))
            TT(ob[:, :, 0:C], ob[:, :, 0:C], bc(shift[:, :].unsqueeze(1), [P, TILES, C]), ALU.subtract).then_inc(centred, 1)
            dve.wait_ge(squares, 1)
            link(nc.vector.tensor_copy(gain[:, :], K.ps[1][:, 0:DIM]))
            link(TT(gain[:, C:2 * C], gain[:, C:2 * C], gain[:, 2 * C:3 * C], ALU.add))
            link(TT(gain[:, C:2 * C], gain[:, C:2 * C], gain[:, 3 * C:], ALU.add))
            dve.wait_ge(col_sd, 1)
            link(nc.vector.reciprocal(gain[:, 0:2 * C], gain[:, 0:2 * C]))
            link(TT(gain[:, 0:2 * C], gain[:, 0:2 * C], g0[:, :], ALU.mult))
            dve.wait_ge(centred, 1)
            for x in range(4):
                ins = TT(ob[:, :, x * C:(x + 1) * C], ob[:, :, x * C:(x + 1) * C],
                         bc(gain[:, min(x, 1) * C:(min(x, 1) + 1) * C].unsqueeze(1), [P, TILES, C]), ALU.mult)
            link(ins)
            link(TT(ob[:, :, 0:C], ob[:, :, 0:C], bc(b0[:, :].unsqueeze(1), [P, TILES, C]), ALU.add))
            base = link.n

            def turn(i, first=False):
                here = Chain(dve, step, i * 2 + base)
                dve.wait_ge(x_loaded, 16 * i + 16)
                TT(xb[:, :, 0:C], xb[:, :, 0:C], ob[:, bass.ds(i * BT, BT), 0:C], ALU.add)
                for x in range(3):
                    into = xb[:, :, C:].rearrange("p j (d x) -> p j d x", x=3)[:, :, :, x]
                    ins = TT(into, into, ob[:, bass.ds(i * BT, BT), (x + 1) * C:(x + 2) * C], ALU.add)
                here(ins)
                here(nc.vector.tensor_copy(yb[:, :, :], xb[:, :, :]))
                norm.on_vector(dve, i, lambda j: yb[:, j, :])
                dve.wait_ge(norm.done, i + 1)
                TT(xb[:, :, :], xb[:, :, :], yb[:, :, :], ALU.add).then_inc(r_ready, 1)

            with dve.Fori(0, BLOCKS) as i:
                turn(i)


def ffn_stage(nc, K, y3, wr, br, w1, b1, w2, b2, z_out, score):
    M = HID // P
    WIDE = TOK // 2
    NB = 4
    with stage(nc, "ffn") as s:
        w1s = s.sb("w1", [P, 2, HID])
        w2s = s.sb("w2", [P, M, DIM])
        b1s = s.sb("b1", [P, M])
        b2s, wrs = s.sb("b2", [P, DIM]), s.sb("wr", [P, DIM])
        brs = s.sb("br", [P, 1])
        yb = s.sb("yb", [P, BT, DIM])
        scr = s.sb("scr", [P, BT, DIM])
        yT = s.sb("yT", [P, 2, TOK])
        hT = s.sb("hT", [P, M, TOK])
        z = s.sb("z", [P, BT, DIM])
        (w_loaded, loaded, turned, yT_ready, hidden, hT_ready, output, used, weighed, scored, step, written) = (
            s.sem(n) for n in ("w_loaded", "loaded", "turned", "yT_ready", "hidden", "hT_ready", "output", "used",
                               "weighed", "scored", "step", "written"))
        block = s.block()

        @block.sync
        def _(sp):
            sp.dma_start(w1s[:, :, :], w1.rearrange("(k p) n -> p k n", p=P)).then_inc(w_loaded, 16)
            sp.dma_start(w2s[:, :, :], w2.rearrange("(m p) n -> p m n", p=P)).then_inc(w_loaded, 16)
            with nc.allow_non_contiguous_dma("the first bias, once"):
                sp.dma_start(b1s[:, :], b1.rearrange("(m p) -> p m", p=P)).then_inc(w_loaded, 16)
            sp.dma_start(b2s[:, :], row_bc(b2)).then_inc(w_loaded, 16)
            sp.dma_start(wrs[:, :], row_bc(wr.rearrange("d o -> (d o)"))).then_inc(w_loaded, 16)
            sp.dma_start(brs[:, :], row_bc(br)).then_inc(w_loaded, 16)
            with sp.Fori(0, BLOCKS) as i:
                sp.wait_ge(scored, i + 1)
                sp.wait_ge(turned, i * NB + 1)
                load_block(sp, (y3,), (yb,), i, loaded)

        @block.gpsimd
        def _(pool):
            with pool.Fori(0, BLOCKS) as i:
                pool.wait_ge(weighed, i + 1)
                hold(pool)
                pool.dma_start(tiles_of(z_out)[:, bass.ds(i * BT, BT), :], z[:, :, :]).then_inc(written, 16)
            pool.wait_ge(written, 16 * BLOCKS)

        @block.tensor
        def _(pe):
            pe.wait_ge(w_loaded, 96)
            pe.sem_inc(turned, 1)
            with pe.Fori(0, BLOCKS) as i:
                pe.wait_ge(loaded, 16 * i + 16)
                for n in range(NB):
                    pe.wait_ge(yT_ready, i * NB + n + 1)
                    pe.wait_ge(hT_ready, i * 2 * M + 4)
                    for m in range(4 * n, min(4 * n + 4, 2 * BT)):
                        k, j = divmod(m, BT)
                        ins = nc.tensor.transpose(K.ps[n][:, (m % 4) * P:(m % 4 + 1) * P],
                                                  yb[:, j, k * P:(k + 1) * P], K.ident[:, :])
                    ins.then_inc(turned, 1)
                pe.wait_ge(yT_ready, (i + 1) * NB + 4)
                for m in range(M):
                    for q in range(2):
                        n = 2 * m + q
                        pe.wait_ge(hT_ready, i * 2 * M + n + 1)
                        for k in range(2):
                            ins = nc.tensor.matmul(K.ps[n % 4][:, 0:WIDE], w1s[:, k, m * P:(m + 1) * P],
                                                   yT[:, k, q * WIDE:(q + 1) * WIDE], start=(k == 0), stop=(k == 1))
                        ins.then_inc(hidden, 1)
                pe.wait_ge(hT_ready, (i + 1) * 2 * M + 4)
                for j in range(BT):
                    pe.wait_ge(used, i * BT + j + 1)
                    for m in range(M):
                        ins = nc.tensor.matmul(K.ps[4 + j % 4][:, 0:DIM], hT[:, m, j * P:(j + 1) * P], w2s[:, m, :],
                                               start=(m == 0), stop=(m == M - 1))
                    ins.then_inc(output, 1)

        @block.scalar
        def _(act):
            act.sem_inc(yT_ready, 4)
            act.sem_inc(hT_ready, 4)
            with act.Fori(0, BLOCKS) as i:
                act.wait_ge(used, i * BT + 4)
                hold(act)
                for n in range(NB):
                    act.wait_ge(turned, i * NB + n + 2)
                    width = min(4, 2 * BT - 4 * n)
                    nc.scalar.activation(yT[:, :, :].rearrange("p k t -> p (k t)")[:, 4 * n * P:(4 * n + width) * P],
                                         K.ps[n][:, 0:width * P], ACT.Copy).then_inc(yT_ready, 1)
                for m in range(M):
                    for q in range(2):
                        n = 2 * m + q
                        act.wait_ge(hidden, i * 2 * M + n + 1)
                        nc.scalar.activation(hT[:, m, q * WIDE:(q + 1) * WIDE], K.ps[n % 4][:, 0:WIDE],
                                             ACT.Gelu_apprx_tanh, bias=b1s[:, m:m + 1]).then_inc(hT_ready, 1)

        @block.vector
        def _(dve):
            dve.wait_ge(w_loaded, 96)
            dve.sem_inc(used, 4)
            dve.sem_inc(scored, 1)
            TT = nc.vector.tensor_tensor

            def turn(i, first=False):
                link = Chain(dve, step, i * 2)
                dve.wait_ge(loaded, 16 * i + 16)
                link(TT(scr[:, :, :], yb[:, :, :], bc(wrs[:, :].unsqueeze(1), [P, BT, DIM]), ALU.mult))
                at = score[:, bass.ds(i * BT, BT)]
                link(nc.vector.tensor_reduce(at, scr[:, :, :], AXX, ALU.add))
                nc.vector.tensor_scalar(at, at, brs[:, :], None, ALU.add).then_inc(scored, 1)
                dve.wait_ge(scored, i + 2)
                if not first:
                    dve.wait_ge(written, 16 * i)
                for j in range(BT):
                    dve.wait_ge(output, i * BT + j + 1)
                    TT(z[:, j, :], K.ps[4 + j % 4][:, 0:DIM], b2s[:, :], ALU.add).then_inc(used, 1)
                dve.wait_ge(used, (i + 1) * BT + 4)
                TT(z[:, :, :], z[:, :, :], bc(at.unsqueeze(2), [P, BT, DIM]), ALU.mult).then_inc(weighed, 1)

            turn(0, first=True)
            with dve.Fori(1, BLOCKS) as i:
                turn(i)


def select_stage(nc, K, score, z, r3, out):
    KEPT = max(1, int(0.5 * NODES)) - 1
    SIGN = -2 ** 31
    with stage(nc, "sel") as s:
        zb = s.sb("zb", [P, TILES, DIM])
        rb = s.sb("rb", [P, TILES, DIM])
        w = s.sb("w", [P, TILES])
        hit = s.sb("hit", [P, TILES])
        above = s.sb("above", [P, TILES])
        prior = s.sb("prior", [P, TILES])
        order = s.sb("order", [P, 1], I32)
        trial, neg, word = (s.sb(n, [P, 1], I32) for n in ("trial", "neg", "word"))
        bits = s.sb("bits", [P, 32], I32)
        keep = s.sb("keep", [P, 1])
        keep_i = s.sb("keep_i", [P, 1], I32)
        cnt = s.sb("cnt", [P, 1])
        loaded, masked, bits_ready, counted, summed, step, turned_on, ready, written = (
            s.sem(n) for n in ("loaded", "masked", "bits_ready", "counted", "summed", "step", "turned_on", "ready",
                               "written"))
        block = s.block()

        @block.sync
        def _(sp):
            sp.dma_start(zb[:, :, :], tiles_of(z)).then_inc(loaded, 16)
            sp.dma_start(rb[:, :, :], tiles_of(r3)).then_inc(loaded, 16)
            sp.wait_ge(ready, 1)
            full = (TILES - 1) * P
            sp.dma_start(tiles_of(out[0:full, :]), rb[:, 0:TILES - 1, :]).then_inc(written, 16)
            sp.dma_start(out[full:NODES, :], rb[0:TAIL, TILES - 1, :]).then_inc(written, 16)
            sp.wait_ge(written, 32)

        @block.gpsimd
        def _(pool):
            nc.gpsimd.affine_select(out=w[:, :], in_=score[:, :], compare_op=ALU.is_ge, fill=-3.4028234663852886e38,
                                    base=NODES - 1, pattern=[[-P, TILES]], channel_multiplier=-1).then_inc(masked, 1)

        @block.tensor
        def _(pe):
            with pe.Fori(0, 33) as n:
                pe.wait_ge(counted, n + 1)
                nc.tensor.matmul(K.ps[0][:, 0:1], K.ones[:, :], cnt[:, :], start=True, stop=True).then_inc(summed, 1)
            pe.wait_ge(counted, 34)
            nc.tensor.matmul(K.ps[1][:, 0:TILES], K.before[:, :], hit[:, :], start=True, stop=True)
            nc.tensor.matmul(K.ps[2][:, 0:TILES], K.ones[:, :], hit[:, :], start=True, stop=True).then_inc(summed, 1)

        @block.vector
        def _(dve):
            link = Chain(dve, step)
            TS, TT = nc.vector.tensor_scalar, nc.vector.tensor_tensor
            link(nc.vector.memset(order[:, :], 0))
            for n in range(32):
                link(nc.vector.memset(bits[:, n:n + 1], SIGN if n == 0 else 1 << (31 - n)))
            dve.wait_ge(masked, 1)

            def to_float(into, code):
                yield TS(neg[:, :], code[:, :], 31, None, ALU.arith_shift_right)
                yield TS(word[:, :], neg[:, :], -1, SIGN, ALU.bitwise_xor, ALU.bitwise_or)
                yield TT(into[:, :], code[:, :], word[:, :], ALU.bitwise_xor)

            base = link.n
            STEPS = 7
            with dve.Fori(0, 32) as n:
                here = Chain(dve, step, base + n * STEPS)
                here(TT(trial[:, :], order[:, :], bits[:, bass.ds(n, 1)], ALU.bitwise_or))
                for ins in to_float(keep_i, trial):
                    here(ins)
                TS(hit[:, :], w[:, :], keep_i[:, :].bitcast(F32), None, ALU.is_ge, ALU.add,
                   accum_out=cnt[:, :]).then_inc(counted, 1)
                dve.wait_ge(summed, n + 1)
                here(TS(keep[:, :], K.ps[0][:, 0:1], float(KEPT), -1.0, ALU.is_ge, ALU.mult))
                here(nc.vector.tensor_copy(neg[:, :], keep[:, :]))
                TT(neg[:, :], neg[:, :], bits[:, bass.ds(n, 1)], ALU.bitwise_and).then_inc(turned_on, 1)
                dve.wait_ge(turned_on, n + 1)
                here(TT(order[:, :], order[:, :], neg[:, :], ALU.bitwise_or))
            link = Chain(dve, step, base + 32 * STEPS)
            for ins in to_float(trial, order):
                link(ins)
            lowest = trial[:, :].bitcast(F32)
            TS(above[:, :], w[:, :], lowest, None, ALU.is_gt, ALU.add, accum_out=cnt[:, :]).then_inc(counted, 1)
            dve.wait_ge(summed, 33)
            link(TS(cnt[:, :], K.ps[0][:, 0:1], -1.0, float(KEPT), ALU.mult, ALU.add))
            TS(hit[:, :], w[:, :], lowest, None, ALU.is_equal).then_inc(counted, 1)
            dve.wait_ge(summed, 34)
            link(nc.vector.memset(prior[:, 0:1], 0.0))
            link(nc.vector.tensor_copy(w[:, :], K.ps[2][:, 0:TILES]))
            link(nc.vector.tensor_tensor_scan(prior[:, 1:TILES], w[:, 0:TILES - 1], w[:, 0:TILES - 1], 0.0, ALU.add, ALU.max))
            link(TT(prior[:, :], prior[:, :], K.ps[1][:, 0:TILES], ALU.add))
            link(TS(prior[:, :], prior[:, :], cnt[:, :], None, ALU.is_lt))
            link(TT(prior[:, :], prior[:, :], hit[:, :], ALU.mult))
            link(TT(above[:, :], above[:, :], prior[:, :], ALU.add))
            dve.wait_ge(loaded, 32)
            link(TT(zb[:, :, :], zb[:, :, :], bc(above[:, :].unsqueeze(2), [P, TILES, DIM]), ALU.mult))
            TT(rb[:, :, :], rb[:, :, :], zb[:, :, :], ALU.add).then_inc(ready, 1)


class Consts:

    def __init__(self, nc, ctx):
        def sb(name, shape, dt=F32):
            return ctx.enter_context(nc.sbuf_tensor(name, shape, dt))
        self.ones, self.ident, self.before, self.upto = (sb(n, [P, P]) for n in ("ones", "ident", "before", "upto"))
        self.count = sb("count", [P, CHUNKS])
        self.eps = sb("eps", [P, 1])
        self.bucket = {side: sb(f"bucket_{side}", [1, CHUNKS], I32) for side in ("dst", "src")}
        self.base = sb("base", [P, CHUNKS])
        self.off = sb("off", [1, CHUNKS], I32)
        self.unsorted = sb("unsorted", [1, 1], I32)
        self.psum = ctx.enter_context(nc.psum_tensor("psum", [P, 8, 512], F32))
        self.ps = [self.psum[:, n, :] for n in range(8)]


def program(nc, A, out):
    def nodes(name):
        return nc.dram_tensor(name, [ROWS, DIM], F32).ap()

    rows_dst = nc.dram_tensor("rows_dst", [CHUNKS * P, META], F32).ap()
    rows_src = nc.dram_tensor("rows_src", [CHUNKS * P, META2], F32).ap()
    x0, h, feat_in, feat_out, a_in, a_out = (nodes(n) for n in ("x0", "h", "feat_in", "feat_out", "a_in", "a_out"))
    x1, y1, x2, y2, up, skip, msg, o = (nodes(n) for n in ("x1", "y1", "x2", "y2", "up", "skip", "msg", "o"))
    r3, y3, z = (nodes(n) for n in ("r3", "y3", "z"))
    with ExitStack() as ctx:
        K = Consts(nc, ctx)
        front_stage(nc, K, A, x0, h, (feat_in, feat_out), rows_dst, rows_src)
        unsorted_stages(nc, K, A, rows_dst)
        gather_stage(nc, K, "dst", rows_dst, META, feat_in, a_in)
        gather_stage(nc, K, "src", rows_src, META2, feat_out, a_out)
        update_stage(nc, K, x0, h, a_in, a_out, A["L0_gnn_W_x2i"], A["L0_gnn_b_x2i"], A["L0_gnn_W_h2h"], x1, y1)
        moe_stage(nc, K, y1, x1, A["router_T"], A["L0_ffn_w1"], A["L0_ffn_b1"], A["L0_ffn_w2"], A["L0_ffn_b2"], x2, y2)
        project_stage(nc, K, "proj1", y2, (A["W_up"], A["W_sc"]), None, (up, skip))
        message_stage(nc, K, rows_dst, up, A["M1_blocks"], A["M2_blocks"], A["M3_blocks"], A["M4_twice"], msg)
        mix_stage(nc, K, msg, skip, A["W_lin"], A["W_wb"], A["poly0"], A["poly1"], o)
        finish_stage(nc, K, o, x2, A["L1_gnn_gamma0"], A["L1_gnn_beta0"], A["L1_gnn_gamma1"], r3, y3)
        score = ctx.enter_context(nc.sbuf_tensor("score", [P, TILES], F32))
        ffn_stage(nc, K, y3, A["L1_ffn_wr"], A["L1_ffn_br"], A["L1_ffn_w1"], A["L1_ffn_b1"], A["L1_ffn_w2"],
                  A["L1_ffn_b2"], z, score)
        select_stage(nc, K, score, z, r3, out)


def kernel(**inputs):
    import numpy as np
    import concourse.bacc as bacc
    from concourse.bass_utils import run_bass_kernel_spmd

    nc = bacc.Bacc("TRN2", target_bir_lowering=False, num_devices=1)
    laid = {name: np.asarray(a) for name, a in inputs.items() if name in USED}
    rows = np.zeros((EDGES, META), np.float32)
    rows[:, 2] = np.asarray(inputs["edge_weight"])
    rows[:, 3:7] = np.asarray(inputs["edge_attr_4"])
    rows[:, 8:24] = np.asarray(inputs["edge_attr_16"])
    laid["edge_rows"] = rows
    for name, w0, w1 in (("up", "L1_gnn_W_up0", "L1_gnn_W_up1"), ("sc", "L1_gnn_Wsc0", "L1_gnn_Wsc1")):
        w = np.zeros((DIM, DIM), np.float32)
        w[:C, :C] = np.asarray(inputs[w0])
        for a in range(3):
            w[C + a::3, C + C * a:2 * C + C * a] = np.asarray(inputs[w1])
        laid["W_" + name] = w
    m1 = np.zeros((P, HALF // 2, P), np.float32)
    for c in range(HALF):
        m1[MLP_IN * c:MLP_IN * (c + 1), c // 2, C * (c % 2):C * (c % 2 + 1)] = np.asarray(inputs["L1_gnn_M1"])
    laid["M1_blocks"] = m1
    for name in ("M2", "M3"):
        w = np.zeros((P, P), np.float32)
        w[:C, :C] = w[C:, C:] = np.asarray(inputs["L1_gnn_" + name])
        laid[name + "_blocks"] = w
    laid["M4_twice"] = np.concatenate([np.asarray(inputs["L1_gnn_M4"])] * 2)
    for name, w0, w1 in (("lin", "L1_gnn_W_lin0", "L1_gnn_W_lin1"), ("wb", "L1_gnn_WB0", "L1_gnn_WB1")):
        w = np.zeros((P, 2, P), np.float32)
        w[:C, 0, :C] = np.asarray(inputs[w0])
        w[C:, 0, C:] = w[:C, 1, :C] = w[C:, 1, C:] = np.asarray(inputs[w1])
        laid["W_" + name] = w
    laid["poly0"] = np.ascontiguousarray(np.asarray(inputs["L1_gnn_Wc0"]).T)
    laid["poly1"] = np.ascontiguousarray(np.asarray(inputs["L1_gnn_Wc1"]).T)
    laid["router_T"] = np.ascontiguousarray(np.asarray(inputs["L0_ffn_router_w"]).T)
    arrays, A = {}, {}
    for name, a in laid.items():
        arrays[f"in_{name}"] = np.ascontiguousarray(a)
        A[name] = nc.dram_tensor(f"in_{name}", a.shape, mybir.dt.from_np(a.dtype), kind="ExternalInput").ap()
    out = nc.dram_tensor("out_0", (NODES, DIM), F32, kind="ExternalOutput").ap()
    program(nc, A, out)
    return run_bass_kernel_spmd(nc, [arrays], core_ids=[0]).results[0]["out_0"]


USED = ["x", "src", "dst", "edge_weight_n2", "L0_gnn_gamma", "L0_gnn_beta", "L0_gnn_W_in", "L0_gnn_b_in", "L0_gnn_W_out",
        "L0_gnn_b_out", "L0_gnn_W_x2i", "L0_gnn_b_x2i", "L0_gnn_W_h2h", "L0_ffn_w1", "L0_ffn_b1", "L0_ffn_w2",
        "L0_ffn_b2", "L1_gnn_gamma0", "L1_gnn_beta0", "L1_gnn_gamma1", "L1_ffn_wr", "L1_ffn_br", "L1_ffn_w1",
        "L1_ffn_b1", "L1_ffn_w2", "L1_ffn_b2"]
```
